# Optimizing a Trainium2 kernel written in Bass

```python
import numpy as np
import jax
import jax.numpy as jnp

def _softmax(x, axis=-1):
    return jax.nn.softmax(x, axis=axis)

def _gelu(x):
    return jax.nn.gelu(x, approximate=True)

def _silu(x):
    return jax.nn.silu(x)

def _sigmoid(x):
    return jax.nn.sigmoid(x)

def _layernorm(x, axis=-1, eps=1e-05):
    m = jnp.mean(x, axis=axis, keepdims=True)
    v = jnp.var(x, axis=axis, keepdims=True)
    return (x - m) / jnp.sqrt(v + eps)

def _scatter_add(tgt, idx, src, axis=0):
    return tgt.at[idx].add(src)

def _segment_sum(src, seg, n):
    return jax.ops.segment_sum(src, seg, n)
kernel_name = 'mk_recurrent_d2_jaxref_r8_782e93'

def setup_inputs(seed: int=0):
    np.random.seed(seed)
    _w = jnp.asarray

    def _L0_attn_setup():
        import jax, jax.numpy as jnp
        import numpy as np
        NUM_HEAD = 16
        SCALE = 8.0
        LN_EPS = 1e-05
        key = jax.random.key(seed)
        ks = jax.random.split(key, 9)
        B, S, D = (4, 256, 128)
        s = 1.0 / np.sqrt(D)
        return {'x': jax.random.normal(ks[0], (B, S, D), dtype=jnp.float32), 'Wq': jax.random.normal(ks[1], (D, D), dtype=jnp.float32) * s, 'bq': jax.random.normal(ks[2], (D,), dtype=jnp.float32) * 0.01, 'Wk': jax.random.normal(ks[3], (D, D), dtype=jnp.float32) * s, 'bk': jax.random.normal(ks[4], (D,), dtype=jnp.float32) * 0.01, 'Wv': jax.random.normal(ks[5], (D, D), dtype=jnp.float32) * s, 'bv': jax.random.normal(ks[6], (D,), dtype=jnp.float32) * 0.01, 'Wf': jax.random.normal(ks[7], (D, D), dtype=jnp.float32) * s, 'bf': jax.random.normal(ks[8], (D,), dtype=jnp.float32) * 0.01}
    _L0_attn_in = _L0_attn_setup()

    def _L0_ffn_setup():
        import jax, jax.numpy as jnp
        import numpy as np
        TOP_K = 8
        key = jax.random.key(seed)
        ks = jax.random.split(key, 6)
        B, S, D, F, E = (2, 128, 128, 64, 64)
        x = jax.random.normal(ks[0], (B, S, D), dtype=jnp.float32)
        centroids = jax.random.normal(ks[1], (E, D), dtype=jnp.float32) * 0.05
        expert_biases = jnp.zeros((E,), dtype=jnp.float32)
        Ws_up = jax.random.normal(ks[2], (D, F), dtype=jnp.float32) / np.sqrt(D)
        Ws_down = jax.random.normal(ks[3], (F, D), dtype=jnp.float32) / np.sqrt(F)
        W_up = jax.random.normal(ks[4], (E, D, F), dtype=jnp.float32) / np.sqrt(D)
        W_down = jax.random.normal(ks[5], (E, F, D), dtype=jnp.float32) / np.sqrt(F)
        return {'x': x, 'centroids': centroids, 'expert_biases': expert_biases, 'Ws_up': Ws_up, 'Ws_down': Ws_down, 'W_up': W_up, 'W_down': W_down}
    _L0_ffn_in = _L0_ffn_setup()

    def _L1_attn_setup():
        import jax, jax.numpy as jnp
        import numpy as np
        LN_EPS = 1e-05

        def _layer_norm(c, ln_w, ln_b):
            mu = jnp.mean(c, axis=-1, keepdims=True)
            var = jnp.mean(jnp.square(c - mu), axis=-1, keepdims=True)
            return (c - mu) * jax.lax.rsqrt(var + LN_EPS) * ln_w + ln_b
        key = jax.random.key(seed)
        k_x, k_w, k_b, k_g, k_beta = jax.random.split(key, 5)
        B, S, D, H = (8, 256, 128, 128)
        x = jax.random.normal(k_x, (B, S, D), dtype=jnp.float32)
        W = jax.random.normal(k_w, (4 * H, D), dtype=jnp.float32) * (1.0 / np.sqrt(D))
        b = jax.random.normal(k_b, (4 * H,), dtype=jnp.float32) * 0.01
        ln_w = jnp.ones((H,), dtype=jnp.float32) + 0.01 * jax.random.normal(k_g, (H,), dtype=jnp.float32)
        ln_b = 0.01 * jax.random.normal(k_beta, (H,), dtype=jnp.float32)
        return {'x': x, 'W': W, 'b': b, 'ln_w': ln_w, 'ln_b': ln_b}
    _L1_attn_in = _L1_attn_setup()

    def _L1_ffn_setup():
        import jax, jax.numpy as jnp
        import numpy as np
        NUM_EXPERTS = 8
        TOP_K = 2
        CAP_RATIO = 1.25
        INIT_STD = 0.02
        key = jax.random.key(seed)
        k1, k2, k3, k4 = jax.random.split(key, 4)
        B, T, H, F = (4, 256, 128, 512)
        x = jax.random.normal(k1, (B, T, H), jnp.float32)
        router_w = jax.random.normal(k2, (NUM_EXPERTS, H), jnp.float32) * INIT_STD
        w1 = jax.random.normal(k3, (NUM_EXPERTS, H, F), jnp.float32) * INIT_STD
        w2 = jax.random.normal(k4, (NUM_EXPERTS, F, H), jnp.float32) * INIT_STD
        return {'x': x, 'router_w': router_w, 'w1': w1, 'w2': w2}
    _L1_ffn_in = _L1_ffn_setup()
    _d = {'L0_attn_x': _L0_attn_in['x'], 'L0_attn_Wq': _L0_attn_in['Wq'], 'L0_attn_bq': _L0_attn_in['bq'], 'L0_attn_Wk': _L0_attn_in['Wk'], 'L0_attn_bk': _L0_attn_in['bk'], 'L0_attn_Wv': _L0_attn_in['Wv'], 'L0_attn_bv': _L0_attn_in['bv'], 'L0_attn_Wf': _L0_attn_in['Wf'], 'L0_attn_bf': _L0_attn_in['bf'], 'L0_ffn_centroids': _L0_ffn_in['centroids'], 'L0_ffn_expert_biases': _L0_ffn_in['expert_biases'], 'L0_ffn_Ws_up': _L0_ffn_in['Ws_up'], 'L0_ffn_Ws_down': _L0_ffn_in['Ws_down'], 'L0_ffn_W_up': _L0_ffn_in['W_up'], 'L0_ffn_W_down': _L0_ffn_in['W_down'], 'L1_attn_W': _L1_attn_in['W'], 'L1_attn_b': _L1_attn_in['b'], 'L1_attn_ln_w': _L1_attn_in['ln_w'], 'L1_attn_ln_b': _L1_attn_in['ln_b'], 'L1_ffn_router_w': _L1_ffn_in['router_w'], 'L1_ffn_w1': _L1_ffn_in['w1'], 'L1_ffn_w2': _L1_ffn_in['w2']}
    _x0 = _d['L0_attn_x']
    _d['L0_attn_x'] = jax.random.normal(jax.random.fold_in(jax.random.key(seed), 1), (8, 512, 128), dtype=_x0.dtype)
    del _x0
    return _d

def reference(L0_attn_x, L0_attn_Wq, L0_attn_bq, L0_attn_Wk, L0_attn_bk, L0_attn_Wv, L0_attn_bv, L0_attn_Wf, L0_attn_bf, L0_ffn_centroids, L0_ffn_expert_biases, L0_ffn_Ws_up, L0_ffn_Ws_down, L0_ffn_W_up, L0_ffn_W_down, L1_attn_W, L1_attn_b, L1_attn_ln_w, L1_attn_ln_b, L1_ffn_router_w, L1_ffn_w1, L1_ffn_w2):

    def _L0_attn_ref(x, Wq, bq, Wk, bk, Wv, bv, Wf, bf):
        import jax, jax.numpy as jnp
        import numpy as np
        NUM_HEAD = 16
        SCALE = 8.0
        LN_EPS = 1e-05
        B, S, D = x.shape
        d = D // NUM_HEAD
        q = x @ Wq + bq
        k = x @ Wk + bk
        v = x @ Wv + bv
        q = q.reshape(B * NUM_HEAD, -1, d)
        k = k.reshape(B * NUM_HEAD, -1, d)
        v = v.reshape(B * NUM_HEAD, -1, d)
        attn = jax.nn.softmax(jnp.einsum('bqd,bkd->bqk', q, k) * SCALE, axis=-1)
        ctx = jnp.einsum('bqk,bkd->bqd', attn, v).reshape(B, S, D)
        ctx = ctx + x
        mu = jnp.mean(ctx, axis=-1, keepdims=True)
        var = jnp.var(ctx, axis=-1, keepdims=True)
        ctx = (ctx - mu) * jax.lax.rsqrt(var + LN_EPS)
        return ctx @ Wf + bf

    def _L0_ffn_ref(x, centroids, expert_biases, Ws_up, Ws_down, W_up, W_down):
        import jax, jax.numpy as jnp
        import numpy as np
        TOP_K = 8
        B, S, D = x.shape
        E = centroids.shape[0]
        T = B * S
        xf = x.reshape(T, D)
        shared = jax.nn.silu(xf @ Ws_up) @ Ws_down
        aff = xf @ centroids.T
        biased = aff + expert_biases
        _, idx = jax.lax.top_k(biased, TOP_K)
        sel = jnp.take_along_axis(aff, idx, axis=1)
        w = jax.nn.sigmoid(sel)
        w = w / (jnp.sum(w, axis=-1, keepdims=True) + 1e-08)
        cw = jnp.zeros((T, E), dtype=x.dtype).at[jnp.arange(T)[:, None], idx].add(w)
        h = jax.nn.silu(jnp.einsum('td,edf->etf', xf, W_up))
        y = jnp.einsum('etf,efd->etd', h, W_down)
        routed = jnp.einsum('etd,te->td', y, cw)
        return (shared + routed).reshape(B, S, D)

    def _L1_attn_ref(x, W, b, ln_w, ln_b):
        import jax, jax.numpy as jnp
        import numpy as np
        LN_EPS = 1e-05

        def _layer_norm(c, ln_w, ln_b):
            mu = jnp.mean(c, axis=-1, keepdims=True)
            var = jnp.mean(jnp.square(c - mu), axis=-1, keepdims=True)
            return (c - mu) * jax.lax.rsqrt(var + LN_EPS) * ln_w + ln_b
        B, S, D = x.shape
        H = W.shape[0] // 4
        gates = jnp.einsum('bsd,gd->bsg', x, W) + b
        f, i, o, z_raw = jnp.split(gates, 4, axis=-1)
        f = jax.nn.sigmoid(f)
        i = jax.nn.sigmoid(i)
        o = jax.nn.sigmoid(o)
        z = jnp.tanh(z_raw)

        def step(c, fioz_t):
            f_t, i_t, o_t, z_t = fioz_t
            c = f_t * c + i_t * z_t
            h = o_t * jnp.tanh(_layer_norm(c, ln_w, ln_b))
            return (c, h)
        c0 = jnp.zeros((B, H), dtype=x.dtype)
        fs = jnp.swapaxes(f, 0, 1)
        is_ = jnp.swapaxes(i, 0, 1)
        os_ = jnp.swapaxes(o, 0, 1)
        zs = jnp.swapaxes(z, 0, 1)
        _, h_seq = jax.lax.scan(step, c0, (fs, is_, os_, zs))
        return jnp.swapaxes(h_seq, 0, 1)

    def _L1_ffn_ref(x, router_w, w1, w2):
        import jax, jax.numpy as jnp
        import numpy as np
        NUM_EXPERTS = 8
        TOP_K = 2
        CAP_RATIO = 1.25
        INIT_STD = 0.02
        B, T, H = x.shape
        E, K = (NUM_EXPERTS, TOP_K)
        xf = x.reshape(-1, H)
        N = xf.shape[0]
        P = N * K
        capacity = int(CAP_RATio * N * K / E) + 1 if False else int(CAP_RATIO * N * K / E) + 1
        logits = xf @ router_w.T
        probs = jax.nn.softmax(logits, axis=-1)
        k_probs, k_idx = jax.lax.top_k(probs, K)
        k_probs = k_probs / jnp.sum(k_probs, axis=-1, keepdims=True)
        flat_e = k_idx.reshape(-1)
        onehot = jax.nn.one_hot(flat_e, E, dtype=jnp.int32)
        rank = jnp.take_along_axis(jnp.cumsum(onehot, axis=0) - 1, flat_e[:, None], axis=1)[:, 0]
        keep = rank < capacity
        slot = jnp.minimum(rank, capacity - 1)
        token_id = jnp.arange(P) // K
        dispatched = jnp.where(keep[:, None], xf[token_id], 0.0)
        buf = jnp.zeros((E, capacity, H), x.dtype).at[flat_e, slot].add(dispatched)
        h = jax.nn.silu(jnp.einsum('ech,ehf->ecf', buf, w1))
        out_buf = jnp.einsum('ecf,efh->ech', h, w2)
        pair_out = out_buf[flat_e, slot] * keep[:, None].astype(x.dtype)
        combined = jnp.sum(pair_out.reshape(N, K, H) * k_probs[..., None], axis=1)
        return combined.reshape(B, T, H) + x
    x = L0_attn_x
    xn = _layernorm(x, axis=-1)
    s = _L0_attn_ref(xn, L0_attn_Wq, L0_attn_bq, L0_attn_Wk, L0_attn_bk, L0_attn_Wv, L0_attn_bv, L0_attn_Wf, L0_attn_bf)
    g = _silu(_L0_ffn_ref(xn, L0_ffn_centroids, L0_ffn_expert_biases, L0_ffn_Ws_up, L0_ffn_Ws_down, L0_ffn_W_up, L0_ffn_W_down))
    x = x + s * g
    xn = _layernorm(x, axis=-1)
    s = _L1_attn_ref(xn, L1_attn_W, L1_attn_b, L1_attn_ln_w, L1_attn_ln_b)
    g = _silu(_L1_ffn_ref(xn, L1_ffn_router_w, L1_ffn_w1, L1_ffn_w2))
    x = x + s * g
    return x

_drawn_inputs = setup_inputs


def setup_inputs(seed=0):
    import zlib

    import numpy as np

    out = dict(_drawn_inputs(seed))
    spreads = {'L0_ffn_expert_biases': (0.0, 0.1)}
    factors = {'L0_attn_bq': 5.465,
     'L0_attn_bk': 5.38,
     'L0_attn_bv': 8.0,
     'L0_attn_bf': 8.0,
     'L1_attn_b': 8.0,
     'L1_attn_ln_w': 200.0,
     'L1_attn_ln_b': 78.047,
     'L1_ffn_router_w': 8.0,
     'L1_ffn_w1': 7.916,
     'L1_ffn_w2': 7.879}
    for name, (base, spread) in spreads.items():
        noise = np.random.default_rng([zlib.crc32(name.encode()), seed]).standard_normal(out[name].shape)
        drawn = base * np.exp(spread * noise) if base else spread * noise
        out[name] = jnp.asarray(drawn.astype(out[name].dtype))
    for name, factor in factors.items():
        out[name] = (out[name] * factor).astype(out[name].dtype)
    return out
```

```python
import numpy as np

import concourse.bass as bass
from concourse import mybir
from contextlib import ExitStack

ALU = mybir.AluOpType
ACT = mybir.ActivationFunctionType
AX = mybir.AxisListType
F32 = mybir.dt.float32
BF16 = mybir.dt.bfloat16
F16 = mybir.dt.float16

P = 128
D = 128
BATCH, SEQ = 8, 512
NTOK = BATCH * SEQ
TOK = 512
TILES = TOK // P
PASSES = BATCH // 2
CH, DH = 16, 8
GT = 32
NG = P // GT
KT = CH * GT // P
SCALE = 8.0
LN_EPS = 1e-5
E0, K0 = 64, 8
E1, K1 = 8, 2
CAPACITY = int(1.25 * NTOK * K1 / E1) + 1
UNITS = 32
WS = 64.0
TERMS = [(a, b) for a in range(3) for b in range(3)]
ROWS = DH * len(TERMS)
MROW = 96
KROWS = MROW + 2


class Stage:

    def __init__(self, i, p):
        self.i, self.p = i, p

    def at(self, per, k):
        return self.i * (2 * per) + (self.p * per + k)

    def own(self, per, k):
        return self.i * per + k

    def next(self):
        return Stage(self.i, 1) if self.p == 0 else Stage(self.i + 1, 0)

    def tokens(self):
        return bass.ds(self.i * (2 * TOK) + self.p * TOK, TOK)

    def first(self):
        return isinstance(self.i, int) and self.i == 0 and self.p == 0

    def last(self):
        return isinstance(self.i, int) and self.i == PASSES - 1 and self.p == 1


def passes(eng, body):
    body(0)
    with eng.Fori(1, PASSES - 1) as i:
        body(i)
    body(PASSES - 1)


def apart(eng):
    eng.nop(nofuse=True)



def attention_phase(nc, io, scratch, ident, identh, consts_ready):
    with ExitStack() as ctx:
        def sb(name, shape, dt=F32):
            return ctx.enter_context(nc.sbuf_tensor(name, shape, dt))

        def sem(name):
            return ctx.enter_context(nc.semaphore(name))

        wq, wk, wv, wf = (sb(f"a_w{n}", [P, D]) for n in "qkvf")
        bq, bk, bf = (sb(f"a_b{n}", [P, 1]) for n in "qkf")
        bv = sb("a_bv", [P, KT, DH])
        cent = sb("a_cent", [P, E0])
        ebias = sb("a_ebias", [P, E0])
        xin = [sb(f"a_xin{p}", [P, TILES, D]) for p in range(2)]
        xn = [sb(f"a_xn{p}", [P, TILES, D]) for p in range(2)]
        stats = sb("a_stats", [P, TILES, 6])
        meanvar = sb("a_meanvar", [P, TILES, 2])
        rstd = sb("a_rstd", [P, TILES, 1])
        vareps = sb("a_vareps", [P, TILES, 1])
        cvareps = sb("a_cvareps", [P, 1])
        neghalf = sb("a_neghalf", [P, TILES])
        xnT = sb("a_xnT", [P, TOK])
        xh = sb("a_xh", [P, TOK], F16)
        xl = sb("a_xl", [P, TOK], F16)
        full = [sb(f"a_{n}32", [P, TOK]) for n in "qk"]
        rest = [sb(f"a_{n}rest", [P, TOK]) for n in "qk"]
        parts = [sb(f"a_{n}parts", [P, 3, TOK], BF16) for n in "qk"]
        stack = [[sb(f"a_{n}stack{p}", [KROWS, TILES, CH * GT, NG], BF16) for p in range(2)] for n in "qk"]
        mrow = sb("a_mrow", [KROWS, 4, 8, NG, GT], BF16)
        vtmp = sb("a_vtmp", [P, TOK // GT, KT, DH])
        vst = [sb(f"a_vst{p}", [P, TOK // GT, KT, 32]) for p in range(2)]
        probs = sb("a_probs", [P, 2, NG, 512])
        mx = [sb(f"a_mx{p}", [P, 16]) for p in range(2)]
        zeros = sb("a_zeros", [P, TOK])
        ones = sb("a_ones", [P, E0])
        mneg = sb("a_mneg", [P, 2, 32], BF16)
        mT = sb("a_mT", [P, 2, 32], BF16)
        oT = sb("a_oT", [P, CH, 32])
        rden = sb("a_rden", [P, CH, 1])
        ctx_sb = sb("a_ctx", [P, D])
        res = sb("a_res", [P, D])
        xlast = sb("a_xlast", [P, D])
        cstats = sb("a_cstats", [P, 6])
        cmv = sb("a_cmv", [P, 2])
        crstd = sb("a_crstd", [P, 1])
        cn = sb("a_cn", [P, D])
        cT = sb("a_cT", [P, TOK])
        sT = sb("a_sT", [P, TOK])
        aff = sb("a_aff", [P, TILES, E0])
        biased = sb("a_biased", [P, TILES, E0])
        best = sb("a_best", [P, TILES, 8])
        dropped = sb("a_dropped", [P, TILES, E0])
        mask = sb("a_mask", [P, TILES, E0])
        esig = sb("a_esig", [P, TILES, E0])
        esum = sb("a_esum", [P, TILES, E0])
        sig = sb("a_sig", [P, TILES, E0])
        wsel = sb("a_wsel", [P, TILES, E0])
        wsum = sb("a_wsum", [P, TILES, 1])
        wsume = sb("a_wsume", [P, TILES, 1])
        wrec = sb("a_wrec", [P, TILES, 1])
        cw = sb("a_cw", [P, TILES, E0])
        cwhl = sb("a_cwhl", [P, TILES, 2, E0], F16)
        cwT = sb("a_cwT", [P, TOK], F16)

        score = ctx.enter_context(nc.psum_tensor("a_score", [P, 2, 512], F32))
        mxps = ctx.enter_context(nc.psum_tensor("a_mxps", [P, 2, 2, 512], F32))
        ops = ctx.enter_context(nc.psum_tensor("a_ops", [P, 512], F32))
        misc = ctx.enter_context(nc.psum_tensor("a_misc", [P, 512], F32))
        misch = misc[:].bitcast(F16)

        w_in = sem("a_w_in")
        x_in = [sem(f"a_x_in{p}") for p in range(2)]
        ln_eps, c_eps = sem("a_ln_eps"), sem("a_c_eps")
        ln_stats, ln_aggr, ln_rstd = sem("a_ln_stats"), sem("a_ln_aggr"), sem("a_ln_rstd")
        xn_ready = sem("a_xn_ready")
        misc_full, misc_free = sem("a_misc_full"), sem("a_misc_free")
        split = sem("a_split")
        x_out = sem("a_x_out")
        qk_in = [sem(f"a_qk_in{p}") for p in range(2)]
        parts_out = sem("a_parts_out")
        init = sem("a_init")
        v_ready = sem("a_v_ready")
        score_full, exp_done = sem("a_score_full"), sem("a_exp_done")
        mx_full, mx_done = sem("a_mx_full"), sem("a_mx_done")
        mneg_done, mT_done = sem("a_mneg_done"), sem("a_mT_done")
        m_in, m_placed = sem("a_m_in"), sem("a_m_placed")
        pv_done = sem("a_pv_done")
        o_out, den_done = sem("a_o_out"), sem("a_den_done")
        kept = sem("a_kept")
        ctx_done, res_done = sem("a_ctx_done"), sem("a_res_done")
        c_stats, c_aggr, c_rstd, cn_done = (sem(f"a_c_{n}") for n in ("stats", "aggr", "rstd", "norm"))
        s_out = sem("a_s_out")
        biased_done, best_done, drop_done = sem("a_biased"), sem("a_best_done"), sem("a_drop_done")
        esig_done, pool_r, dve_r = sem("a_esig_done"), sem("a_pool_router"), sem("a_dve_router")
        cw_out = sem("a_cw_out")

        W_LOADS = 4 + 3 + NG + 2
        SLOTS_OF_STACK = 2 * len(TERMS)

        MID = ["xnT", "q", "k", "cn3p", "sTp", "V", "logits", "cn0", "cn1", "cwT", "cn2"]
        FIRST = [x for x in MID if x not in ("cn3p", "sTp")]
        START = ["xnT", "q", "k", "V", "logits", "cwT"]
        LAST = ["cn3p", "sTp", "cn0", "cn1", "cn2", "cn3", "sT"]

        def misc_use(s, name):
            if s is None:
                return START.index(name)
            if s.first():
                return len(START) + FIRST.index(name)
            if s.last():
                return len(START) - 2 + len(MID) * (BATCH - 1) + LAST.index(name)
            return s.at(len(MID), len(START) - 2 + MID.index(name))

        SLOTS = {(0, 1): ["xnT"], (0, 2): ["q"], (0, 3): ["k", "cn3p"], (1, 0): ["sTp"], (1, 1): ["V"],
                 (1, 2): ["logits"], (1, 3): ["cn0"], (2, 3): ["cn1"], (3, 1): ["cwT"], (3, 3): ["cn2"]}

        def slot(s, tau, kt):
            names = SLOTS.get((tau, kt), [])
            skip = ("cn3p", "sTp") if s.first() else ()
            if s.last():
                skip = ("xnT", "q", "k", "V", "logits", "cwT")
            return [x for x in names if x not in skip]

        def mx_pairs(s, tau, kt):
            ahead = tau + 1 if kt < 2 else tau + 2
            js = (4, 5) if kt == 0 else (6, 7) if kt == 1 else (0, 1) if kt == 2 else (2, 3)
            if s.last() and ahead > TILES - 1:
                return []
            return [(ahead, j) for j in js]

        def period(f):
            def body(i):
                for p in range(2):
                    for tau in range(TILES):
                        f(Stage(i, p), tau)
            return body

        NONE = Stage(0, 0)

        block = ctx.enter_context(nc.Block())

        @block.sync
        def _(sp):
            x_t = io["x"].rearrange("(n p) d -> p n d", p=P)

            def load_x(s):
                apart(sp)
                sp.dma_start(xin[s.p][:], x_t[:, bass.ds(s.i * (2 * TILES) + s.p * TILES, TILES), :]
                             ).then_inc(x_in[s.p], 16)

            def stack_in(n, side):
                if not (isinstance(n.i, int) and n.i == 0 and n.p == 0):
                    b = Stage(n.i, 0) if n.p else Stage(n.i - 1, 1)
                    sp.wait_ge(qk_in[b.p], b.own(16 * SLOTS_OF_STACK, 16 * SLOTS_OF_STACK))
                    apart(sp)
                sp.wait_ge(split, n.at(12, 5 * side + 5))
                apart(sp)
                there = scratch["parts"][side]
                for a in range(3):
                    sp.dma_start(there[a].rearrange("n r x -> r n x"),
                                 parts[side][:, a, :].rearrange("p (n x) -> p n x", n=TILES)
                                 ).then_inc(parts_out, 16)
                sp.wait_ge(parts_out, n.at(96, 48 * side + 48))
                for r, term in enumerate(TERMS):
                    sp.dma_start(stack[side][n.p][DH * r:DH * r + DH].rearrange("j n c g -> j n (c g)"),
                                 there[term[side]].rearrange("n (j c) x -> j n (c x)", j=DH)
                                 ).then_inc(qk_in[n.p], 16)

            def x_parts_out(n):
                sp.wait_ge(split, n.at(12, 12))
                apart(sp)
                sp.dma_start(scratch["xh0"][:, n.tokens()], xh[:]).then_inc(x_out, 16)
                sp.dma_start(scratch["xl0"][:, n.tokens()], xl[:]).then_inc(x_out, 16)

            def max_rows(s, tau):
                if not (s.first() and tau == 0):
                    sp.wait_ge(m_placed, s.at(4 * TILES, 4 * tau))
                    apart(sp)
                sp.wait_ge(mT_done, s.at(TILES, tau + 1))
                for a in range(2):
                    sp.dma_start(mrow[MROW + a:MROW + a + 1].rearrange("o q r g t -> o (q r g t)"), mT[:, a, :]
                                 ).then_inc(m_in, 16)

            def cw_store(s, n):
                sp.wait_ge(misc_free, misc_use(s, "cwT") + 1)
                apart(sp)
                sp.dma_start(scratch["cw0"][:, n.tokens()], cwT[:]).then_inc(cw_out, 16)

            def s_store(s, name, prev):
                sp.wait_ge(misc_free, misc_use(s, name) + 1)
                apart(sp)
                sp.dma_start(scratch["s0"][:, prev], sT[:]).then_inc(s_out, 16)

            for dst, src in ((wq, "wq"), (wk, "wk"), (wv, "wv"), (wf, "wf"), (bq, "bq"), (bk, "bk"), (bf, "bf"),
                             (cent, "cent")):
                sp.dma_start(dst[:], io[src]).then_inc(w_in, 16)
            sp.dma_start(ebias[:], io["ebias"].broadcast_to([P, E0])).then_inc(w_in, 16)
            for cq in range(NG):
                sp.dma_start(bv[GT * cq:GT * cq + GT, :, :],
                             io["bv"].rearrange("o (k c j) -> o k c j", c=4, j=DH)[:, :, cq, :]
                             .broadcast_to([GT, KT, DH])).then_inc(w_in, 16)
            load_x(Stage(0, 0))
            load_x(Stage(0, 1))
            sp.wait_ge(init, 14)
            stack_in(NONE, 0)
            stack_in(NONE, 1)
            x_parts_out(NONE)
            cw_store(None, NONE)
            max_rows(NONE, 0)

            def step(s, tau):
                n = s.next()
                more = not s.last()
                if tau == 0:
                    if more and not (isinstance(s.i, int) and s.i == PASSES - 1):
                        sp.wait_ge(xn_ready, s.at(TILES, TILES))
                        load_x(Stage(s.i + 1, s.p))
                if tau == 1 and more:
                    if not s.first():
                        sp.wait_ge(score_full, s.at(64, 0))
                    stack_in(n, 0)
                if more or tau < TILES - 1:
                    max_rows(s, tau + 1)
                if tau == 1 and more:
                    stack_in(n, 1)
                    x_parts_out(n)
                if tau == 1 and not s.first():
                    prev = bass.ds(s.i * (2 * TOK) + (s.p - 1) * TOK, TOK)
                    s_store(s, "sTp", prev)
                if tau == 3 and more:
                    cw_store(s, n)

            passes(sp, period(step))
            s_store(Stage(PASSES - 1, 1), "sT", slice(NTOK - TOK, NTOK))
            sp.wait_ge(s_out, 16 * BATCH)
            sp.wait_ge(cw_out, 16 * BATCH)
            sp.wait_ge(x_out, 32 * BATCH)

        @block.gpsimd
        def _(pool):
            def inverse_std(n):
                pool.wait_ge(ln_eps, n.at(1, 1))
                pool.tensor_tensor(rstd[:], vareps[:], neghalf[:, 0:TILES].unsqueeze(2), ALU.pow
                                   ).then_inc(ln_rstd, 1)

            def split3(s, n, side):
                pool.wait_ge(misc_free, misc_use(s, "qk"[side]) + 1)
                if s is not None:
                    pool.wait_ge(parts_out, n.at(96, 0))
                f, r, pt, base = full[side], rest[side], parts[side], 5 * side
                pool.tensor_tensor(pt[:, 0, :], f[:], zeros[:], ALU.add).then_inc(split, 1)
                pool.wait_ge(split, n.at(12, base + 1))
                pool.tensor_tensor(r[:], f[:], pt[:, 0, :], ALU.subtract).then_inc(split, 1)
                pool.wait_ge(split, n.at(12, base + 2))
                pool.tensor_tensor(pt[:, 1, :], r[:], zeros[:], ALU.add).then_inc(split, 1)
                pool.wait_ge(split, n.at(12, base + 3))
                pool.tensor_tensor(f[:], r[:], pt[:, 1, :], ALU.subtract).then_inc(split, 1)
                pool.wait_ge(split, n.at(12, base + 4))
                pool.tensor_tensor(pt[:, 2, :], f[:], zeros[:], ALU.add).then_inc(split, 1)

            def split_x(s, n):
                pool.wait_ge(misc_free, misc_use(s, "xnT") + 1)
                if s is not None:
                    pool.wait_ge(x_out, n.at(32, 0))
                pool.tensor_tensor(xh[:], xnT[:], zeros[:], ALU.add).then_inc(split, 1)
                pool.wait_ge(split, n.at(12, 11))
                pool.tensor_tensor(xl[:], xnT[:], xh[:], ALU.subtract).then_inc(split, 1)

            def values(s, n):
                pool.wait_ge(misc_free, misc_use(s, "V") + 1)
                if s is not None:
                    pool.wait_ge(pv_done, s.at(16, 0))
                pool.tensor_tensor(vst[n.p][:, :, :, 0:DH], vtmp[:],
                                   bv[:].unsqueeze(1).broadcast_to([P, TOK // GT, KT, DH]), ALU.add
                                   ).then_inc(v_ready, 1)

            def router_bias(s, n):
                pool.wait_ge(misc_free, misc_use(s, "logits") + 1)
                pool.tensor_tensor(biased[:], aff[:], ebias[:].unsqueeze(1).broadcast_to([P, TILES, E0]),
                                   ALU.add).then_inc(biased_done, 1)

            def router_sum(n):
                pool.wait_ge(esig_done, n.at(1, 1))
                pool.tensor_tensor(esum[:], esig[:], ones[:].unsqueeze(1).broadcast_to([P, TILES, E0]), ALU.add
                                   ).then_inc(pool_r, 1)
                pool.wait_ge(dve_r, n.at(5, 2))
                pool.tensor_tensor(wsel[:], sig[:], mask[:], ALU.mult).then_inc(pool_r, 1)

            def router_weights(s, n):
                pool.wait_ge(dve_r, n.at(5, 5))
                pool.tensor_tensor(cw[:], wsel[:], wrec[:].broadcast_to([P, TILES, E0]), ALU.mult
                                   ).then_inc(pool_r, 1)
                pool.wait_ge(pool_r, n.at(5, 3))
                pool.tensor_tensor(cwhl[:, :, 0, :], cw[:], zeros[:, 0:TILES * E0].rearrange(
                    "p (t e) -> p t e", t=TILES), ALU.add).then_inc(pool_r, 1)
                pool.wait_ge(pool_r, n.at(5, 4))
                pool.tensor_tensor(cwhl[:, :, 1, :], cw[:], cwhl[:, :, 0, :], ALU.subtract).then_inc(pool_r, 1)

            def context(s, tau):
                pool.wait_ge(den_done, s.at(TILES, tau + 1))
                pool.tensor_tensor(ctx_sb[:].rearrange("p (c j) -> p c j", c=CH), oT[:, :, 0:DH],
                                   rden[:].broadcast_to([P, CH, DH]), ALU.mult).then_inc(ctx_done, 1)
                pool.wait_ge(ctx_done, s.at(TILES, tau + 1))
                if tau == TILES - 1:
                    pool.wait_ge(kept, s.at(1, 1))
                row = xlast[:] if tau == TILES - 1 else xn[s.p][:, tau, :]
                pool.tensor_tensor(res[:], ctx_sb[:], row, ALU.add).then_inc(res_done, 1)

            def context_norm(s, tau):
                pool.wait_ge(c_eps, s.at(TILES, tau + 1))
                pool.tensor_tensor(crstd[:], cvareps[:], neghalf[:, 0:1], ALU.pow).then_inc(c_rstd, 1)

            pool.wait_ge(w_in, 16 * W_LOADS)
            pool.wait_ge(init, 14)
            inverse_std(NONE)
            split3(None, NONE, 0)
            split3(None, NONE, 1)
            split_x(None, NONE)
            values(None, NONE)
            router_bias(None, NONE)
            router_sum(NONE)
            router_weights(None, NONE)

            def back(s):
                return Stage(s.i, 0) if s.p else Stage(s.i - 1, 1)

            def step(s, tau):
                n, more = s.next(), not s.last()
                if tau == 0 and more:
                    inverse_std(n)
                if not (s.first() and tau == 0):
                    before = (s, tau - 1) if tau else (back(s), TILES - 1)
                    context(*before)
                    context_norm(*before)
                if tau == TILES - 1:
                    pool.tensor_tensor(xlast[:], xn[s.p][:, tau, :], zeros[:, 0:D], ALU.add).then_inc(kept, 1)
                if not more:
                    return
                if tau == 0:
                    split3(s, n, 0)
                    split3(s, n, 1)
                    split_x(s, n)
                if tau == 1:
                    values(s, n)
                    router_bias(s, n)
                if tau == 2:
                    router_sum(n)
                    router_weights(s, n)

            passes(pool, period(step))
            context(Stage(PASSES - 1, 1), TILES - 1)
            context_norm(Stage(PASSES - 1, 1), TILES - 1)

        @block.scalar
        def _(act):
            def take(s, name, n):
                act.wait_ge(misc_full, misc_use(s, name) + 1)
                if name == "xnT":
                    if s is not None:
                        act.wait_ge(split, n.at(12, 0))
                    op = act.activation(xnT[:], misc[:], ACT.Copy)
                elif name in ("q", "k"):
                    side = "qk".index(name)
                    op = act.activation(full[side][:].rearrange("p (n t g) -> p n t g", t=GT, g=NG),
                                        misc[:].rearrange("p (n g t) -> p n t g", t=GT, g=NG),
                                        ACT.Identity, bias=(bq, bk)[side][:])
                elif name == "V":
                    if s is not None:
                        act.wait_ge(v_ready, n.at(1, 0))
                    op = act.activation(vtmp[:].rearrange("p g k j -> p (g k j)"), misc[:], ACT.Copy)
                elif name == "logits":
                    if s is not None:
                        act.wait_ge(biased_done, n.at(1, 0))
                        act.wait_ge(esig_done, n.at(1, 0))
                    op = act.activation(aff[:].rearrange("p t e -> p (t e)"), misc[:, :TILES * E0], ACT.Copy)
                elif name == "cwT":
                    if s is not None:
                        act.wait_ge(cw_out, n.at(16, 0))
                    op = act.activation(cwT[:], misch[:, :TOK], ACT.Copy)
                elif name[:2] == "cn":
                    t = int(name[2])
                    op = act.activation(cT[:, t * P:t * P + P], misc[:, :P], ACT.Copy)
                else:
                    if name == "sTp" and not (isinstance(s.i, int) and s.i == 0 and s.p == 1) or name == "sT":
                        done = s.at(16, -16) if name == "sTp" else s.at(16, 0)
                        act.wait_ge(s_out, done)
                    op = act.activation(sT[:], misc[:], ACT.Identity, bias=bf[:])
                op.then_inc(misc_free, 1)
                if name == "logits":
                    act.wait_ge(misc_free, misc_use(s, name) + 1)
                    if s is not None:
                        act.wait_ge(pool_r, n.at(5, 1 - 5))
                    act.activation(esig[:], aff[:], ACT.Exp, scale=-1.0).then_inc(esig_done, 1)

            def place_maxima(s, tau):
                where, at = (s if tau < TILES else s.next()), tau % TILES
                act.wait_ge(m_in, s.at(32 * TILES, 32 * tau + 32))
                for qt in range(4):
                    act.activation(stack[0][where.p][MROW:KROWS, at, qt * P:qt * P + P, :].rearrange(
                        "a (q t) g -> a q t g", q=4), mrow[MROW:KROWS, :, qt, :, :].rearrange("a q g t -> a q t g"),
                        ACT.Copy).then_inc(m_placed, 1)

            act.wait_ge(w_in, 16 * W_LOADS)
            for name in START[:-1]:
                take(None, name, NONE)
            take(None, "cwT", NONE)
            place_maxima(NONE, 0)

            def step(s, tau):
                for kt in range(KT):
                    if kt == 3 and not (s.last() and tau == TILES - 1):
                        place_maxima(s, tau + 1)
                    for g in range(NG):
                        act.wait_ge(score_full, s.at(64, 16 * tau + 4 * kt + g + 1))
                        if g == 0 and not (s.first() and 4 * tau + kt < 2):
                            act.wait_ge(pv_done, s.at(16, 4 * tau + kt - 1))
                        act.activation(probs[:, kt % 2, g, :], score[:, g % 2, :], ACT.Exp, scale=SCALE
                                       ).then_inc(exp_done, 1)
                    for name in slot(s, tau, kt):
                        take(s, name, s.next())

            passes(act, period(step))
            last = Stage(PASSES - 1, 1)
            take(last, "cn3", last)
            take(last, "sT", last)

        @block.tensor
        def _(pe):
            def use(s, name):
                v = misc_use(s, name)
                if not (isinstance(v, int) and v == 0):
                    pe.wait_ge(misc_free, v)

            def fill(s, name, n):
                use(s, name)
                if name == "xnT":
                    pe.wait_ge(xn_ready, n.at(TILES, TILES))
                    for t in range(TILES):
                        op = pe.transpose(misc[:, t * P:t * P + P], xn[n.p][:, t, :], ident[:])
                elif name in ("q", "k"):
                    if name == "q":
                        pe.wait_ge(misc_free, misc_use(s, "xnT") + 1)
                    if s is not None:
                        pe.wait_ge(split, n.at(12, 0))
                    op = pe.matmul(misc[:], (wq if name == "q" else wk)[:], xnT[:], start=True, stop=True)
                elif name == "V":
                    w = wv[:].rearrange("d (k c j) -> d c k j", c=4, j=DH)
                    for g in range(TOK // GT):
                        for cq in range(4):
                            op = pe.matmul(misc[GT * cq:GT * cq + GT, g * GT:g * GT + GT].rearrange(
                                "p (k j) -> p k j", k=KT), xnT[:, g * GT:g * GT + GT], w[:, cq],
                                start=True, stop=True, skip_group_check=True)
                elif name == "logits":
                    for t in range(TILES):
                        op = pe.matmul(misc[:, t * E0:t * E0 + E0], xnT[:, t * P:t * P + P], cent[:],
                                       start=True, stop=True)
                elif name == "cwT":
                    pe.wait_ge(pool_r, n.at(5, 5))
                    for t in range(TILES):
                        op = pe.transpose(misch[:, t * P:t * P + P],
                                          cwhl[:, t, :, :].rearrange("p a e -> p (a e)"), identh[:])
                elif name[:2] == "cn":
                    t = int(name[2])
                    back = -1 if name[-1] == "p" else t
                    pe.wait_ge(cn_done, s.at(TILES, back + 1))
                    op = pe.transpose(misc[:, :P], cn[:], ident[:])
                else:
                    pe.wait_ge(misc_free, misc_use(s, "cn3p" if name == "sTp" else "cn3") + 1)
                    op = pe.matmul(misc[:], wf[:], cT[:], start=True, stop=True)
                op.then_inc(misc_full, 1)

            def maxima(s, ahead, j):
                where = s if ahead < TILES else s.next()
                at = ahead % TILES
                if j == 0 and at == 0:
                    pe.wait_ge(qk_in[where.p], where.own(16 * SLOTS_OF_STACK, 16 * SLOTS_OF_STACK))
                if not (s.first() and 8 * ahead + j < 2):
                    pe.wait_ge(mx_done, s.at(32, 8 * ahead + j - 1))
                qt = j // 2
                for k in range(2):
                    g = 2 * (j % 2) + k
                    op = pe.matmul(mxps[:, j % 2, k, :], stack[0][where.p][0:ROWS, at, qt * P:qt * P + P, g],
                                   stack[1][where.p][0:ROWS, at, :, g], start=True, stop=True)
                op.then_inc(mx_full, 1)

            def scores(s, tau, kt, g):
                if kt == 0 and g == 0:
                    pe.wait_ge(m_placed, s.at(4 * TILES, 4 * tau + 4))
                if not (s.first() and 16 * tau + 4 * kt + g < 2):
                    pe.wait_ge(exp_done, s.at(64, 16 * tau + 4 * kt + g - 1))
                pe.matmul(score[:, g % 2, :], stack[1][s.p][0:KROWS, tau, kt * P:kt * P + P, g],
                          stack[0][s.p][0:KROWS, tau, :, g], start=True, stop=True
                          ).then_inc(score_full, 1)

            def weighted(s, tau, kt, half):
                pe.wait_ge(exp_done, s.at(64, 16 * tau + 4 * kt + 4))
                if kt == 0:
                    if tau == 0:
                        pe.wait_ge(v_ready, s.at(1, 1))
                    if not (s.first() and tau == 0):
                        pe.wait_ge(o_out, s.at(TILES, tau))
                for g in range(NG):
                    op = pe.matmul(ops[GT * g:GT * g + GT, :], vst[half][:, tau * NG + g, kt, :],
                                   probs[:, kt % 2, g, :], start=(kt == 0), stop=(kt == KT - 1),
                                   skip_group_check=True)
                op.then_inc(pv_done, 1)

            pe.wait_ge(consts_ready, 4)
            pe.wait_ge(w_in, 16 * W_LOADS)
            for name in START:
                fill(None, name, NONE)
            pe.wait_ge(init, 14)
            for j in range(8):
                maxima(NONE, 0, j)
            for j in range(4):
                maxima(NONE, 1, j)

            def step(s, tau):
                for kt in range(KT):
                    pairs = mx_pairs(s, tau, kt)
                    scores(s, tau, kt, 0)
                    if pairs:
                        maxima(s, *pairs[0])
                    scores(s, tau, kt, 1)
                    if kt:
                        weighted(s, tau, kt - 1, s.p)
                    elif tau:
                        weighted(s, tau - 1, KT - 1, s.p)
                    elif not s.first():
                        weighted(Stage(s.i, 0) if s.p else Stage(s.i - 1, 1), TILES - 1, KT - 1, 1 - s.p)
                    scores(s, tau, kt, 2)
                    if pairs:
                        maxima(s, *pairs[1])
                    scores(s, tau, kt, 3)
                    for name in slot(s, tau, kt):
                        fill(s, name, s.next())

            passes(pe, period(step))
            last = Stage(PASSES - 1, 1)
            weighted(last, TILES - 1, KT - 1, 1)
            fill(last, "cn3", last)
            fill(last, "sT", last)

        @block.vector
        def _(dve):
            def statistics(n):
                dve.wait_ge(x_in[n.p], n.own(16, 16))
                for t in range(TILES):
                    dve.bn_stats(stats[:, t, :], xin[n.p][:, t, :]).then_inc(ln_stats, 1)
                dve.wait_ge(ln_stats, n.at(TILES, TILES))
                if not (isinstance(n.i, int) and n.i == 0 and n.p == 0):
                    dve.wait_ge(xn_ready, n.at(TILES, 0))
                apart(dve)
                for t in range(TILES):
                    dve.bn_aggr(meanvar[:, t, :], stats[:, t, :]).then_inc(ln_aggr, 1)
                dve.wait_ge(ln_aggr, n.at(TILES, TILES))
                dve.tensor_scalar(vareps[:], meanvar[:, :, 1:2], LN_EPS, None, ALU.add).then_inc(ln_eps, 1)

            def normalise(n):
                dve.wait_ge(ln_rstd, n.at(1, 1))
                for t in range(TILES):
                    dve.tensor_scalar(xn[n.p][:, t, :], xin[n.p][:, t, :], meanvar[:, t, 0:1], rstd[:, t, :],
                                      ALU.subtract, ALU.mult).then_inc(xn_ready, 1)

            def context_norm(s, tau):
                dve.wait_ge(c_rstd, s.at(TILES, tau + 1))
                dve.tensor_scalar(cn[:], res[:], cmv[:, 0:1], crstd[:], ALU.subtract, ALU.mult
                                  ).then_inc(cn_done, 1)

            def maximum(s, ahead, j):
                dve.wait_ge(mx_full, s.at(32, 8 * ahead + j + 1))
                c = (j // 2) * 4 + 2 * (j % 2)
                dve.tensor_reduce(mx[ahead % 2][:, c:c + 2], mxps[:, j % 2, :, :], AX.X, ALU.max
                                  ).then_inc(mx_done, 1)

            def minus_maximum(s, ahead):
                m = mx[ahead % 2]
                dve.wait_ge(mx_done, s.at(32, 8 * ahead + 8))
                dve.tensor_scalar(mneg[:, 0, 0:16], m[:], -1.0, None, ALU.mult).then_inc(mneg_done, 1)
                dve.wait_ge(mneg_done, s.at(2 * TILES, 2 * ahead + 1))
                dve.scalar_tensor_tensor(mneg[:, 1, 0:16], m[:], -1.0, mneg[:, 0, 0:16], ALU.mult, ALU.subtract
                                         ).then_inc(mneg_done, 1)
                dve.wait_ge(mneg_done, s.at(2 * TILES, 2 * ahead + 2))
                if not (s.first() and ahead == 0):
                    dve.wait_ge(m_in, s.at(32 * TILES, 32 * ahead))
                dve.transpose(mT[:].rearrange("p a t -> p (a t)"), mneg[:].rearrange("p a t -> p (a t)")).then_inc(mT_done, 1)

            def context(s, tau):
                dve.wait_ge(pv_done, s.at(16, 4 * tau + 4))
                if not (s.first() and tau == 0):
                    dve.wait_ge(ctx_done, s.at(TILES, tau))
                dve.transpose(oT[:].rearrange("p c j -> p (c j)"), ops[:]).then_inc(o_out, 1)
                dve.wait_ge(o_out, s.at(TILES, tau + 1))
                dve.reciprocal(rden[:], oT[:, :, DH:DH + 1]).then_inc(den_done, 1)

            def context_stats(s, tau):
                dve.wait_ge(res_done, s.at(TILES, tau + 1))
                dve.bn_stats(cstats[:], res[:]).then_inc(c_stats, 1)
                dve.wait_ge(c_stats, s.at(TILES, tau + 1))
                if not (s.first() and tau == 0):
                    dve.wait_ge(cn_done, s.at(TILES, tau))
                apart(dve)
                dve.bn_aggr(cmv[:], cstats[:]).then_inc(c_aggr, 1)
                dve.wait_ge(c_aggr, s.at(TILES, tau + 1))
                dve.tensor_scalar(cvareps[:], cmv[:, 1:2], LN_EPS, None, ALU.add).then_inc(c_eps, 1)

            def choose(n):
                dve.wait_ge(biased_done, n.at(1, 1))
                if not (isinstance(n.i, int) and n.i == 0 and n.p == 0):
                    dve.wait_ge(pool_r, n.at(5, 0))
                apart(dve)
                for t in range(TILES):
                    dve.max(best[:, t, :], biased[:, t, :]).then_inc(best_done, 1)
                dve.wait_ge(best_done, n.at(TILES, TILES))
                apart(dve)
                for t in range(TILES):
                    dve.match_replace(dropped[:, t, :], best[:, t, :], biased[:, t, :], -3.0e38
                                      ).then_inc(drop_done, 1)
                dve.wait_ge(drop_done, n.at(TILES, TILES))
                dve.tensor_tensor(mask[:], dropped[:], biased[:], ALU.not_equal).then_inc(dve_r, 1)

            def sigmoid(n):
                dve.wait_ge(pool_r, n.at(5, 1))
                dve.reciprocal(sig[:], esum[:]).then_inc(dve_r, 1)

            def weights(n):
                dve.wait_ge(pool_r, n.at(5, 2))
                dve.tensor_reduce(wsum[:], wsel[:], AX.X, ALU.add).then_inc(dve_r, 1)
                dve.wait_ge(dve_r, n.at(5, 3))
                dve.tensor_scalar(wsume[:], wsum[:], 1e-8, None, ALU.add).then_inc(dve_r, 1)
                dve.wait_ge(dve_r, n.at(5, 4))
                dve.reciprocal(wrec[:], wsume[:]).then_inc(dve_r, 1)

            for p in range(2):
                for side in range(2):
                    dve.memset(stack[side][p][64:96], 0.0).then_inc(init, 1)
                dve.memset(stack[1][p][MROW:KROWS], 1.0).then_inc(init, 1)
                dve.memset(vst[p][:], 0.0).then_inc(init, 1)
            dve.memset(mneg[:], 0.0).then_inc(init, 1)
            dve.memset(neghalf[:], -0.5).then_inc(init, 1)
            dve.memset(zeros[:], 0.0).then_inc(init, 1)
            dve.memset(ones[:], 1.0).then_inc(init, 1)
            dve.wait_ge(init, 12)
            for p in range(2):
                dve.memset(vst[p][:, :, :, DH:DH + 1], 1.0).then_inc(init, 1)
            statistics(NONE)
            normalise(NONE)
            choose(NONE)
            sigmoid(NONE)
            weights(NONE)
            for j in range(8):
                maximum(NONE, 0, j)
            minus_maximum(NONE, 0)
            for j in range(4):
                maximum(NONE, 1, j)

            def step(s, tau):
                n, more = s.next(), not s.last()
                before = (s, tau - 1) if tau else (Stage(s.i, 0) if s.p else Stage(s.i - 1, 1), TILES - 1)
                for kt in range(KT):
                    if tau == 0 and kt == 0 and more:
                        statistics(n)
                    pairs = mx_pairs(s, tau, kt)
                    if pairs:
                        maximum(s, *pairs[0])
                    if kt == 0 and not (s.first() and tau == 0):
                        context(*before)
                    if tau == 0 and kt == 0 and more:
                        normalise(n)
                    if pairs:
                        maximum(s, *pairs[1])
                    if kt == 2 and not (s.first() and tau == 0):
                        context_norm(*before)
                    if kt == 1 and pairs:
                        minus_maximum(s, tau + 1)
                    if kt == 1 and not (s.first() and tau == 0):
                        context_stats(*before)
                    if more and tau == 2:
                        if kt == 0:
                            choose(n)
                        if kt == 1:
                            sigmoid(n)
                        if kt == 2:
                            weights(n)

            passes(dve, period(step))
            last = Stage(PASSES - 1, 1)
            context(last, TILES - 1)
            context_stats(last, TILES - 1)
            context_norm(last, TILES - 1)



def mixture_phase(nc, io, scratch, ident, identh, layer):
    prep = layer == 0
    with ExitStack() as ctx:
        def sb(name, shape, dt=F32):
            return ctx.enter_context(nc.sbuf_tensor(f"m{layer}_{name}", shape, dt))

        def sem(name):
            return ctx.enter_context(nc.semaphore(f"m{layer}_{name}"))

        UPC = 4 if layer else 1
        SELK = 2 * (E1 if layer else E0)
        NSEL = UNITS // UPC
        NQ = UNITS + 1 if prep else UNITS
        HW = 3 if prep else 4

        wup = sb("wup", [P, NQ, P])
        wuh = sb("wuh", [P, NQ, P], F16)
        wul = sb("wul", [P, NQ, P], F16)
        wdn = sb("wdn", [P, NQ, P])
        sel = sb("sel", [SELK, NSEL, P], F16)
        xh = [sb(f"xh{p}", [P, TOK], F16) for p in range(2)]
        xl = [sb(f"xl{p}", [P, TOK], F16) for p in range(2)]
        cw = [sb(f"cw{p}", [SELK, TOK], F16) for p in range(2)]
        sT = [sb(f"sT{p}", [P, TOK]) for p in range(2)]
        xres = [sb(f"xres{p}", [P, TILES, D]) for p in range(2)]
        silu = sb("silu", [P, 2, TOK])
        hid = sb("hid", [P, HW, TOK])
        gT = sb("gT", [P, TOK])
        prod = sb("prod", [P, TOK])
        xnew = sb("xnew", [P, TILES, D])
        hps = ctx.enter_context(nc.psum_tensor(f"m{layer}_h", [P, 2, 512], F32))
        cps = ctx.enter_context(nc.psum_tensor(f"m{layer}_c", [P, 2, 512], F32))
        yps = ctx.enter_context(nc.psum_tensor(f"m{layer}_y", [P, 512], F32))
        mps = ctx.enter_context(nc.psum_tensor(f"m{layer}_m", [P, 3, 512], F32))

        w_in, up_in, dn_in = sem("w_in"), sem("up_in"), sem("dn_in")
        cst = sem("cst")
        wsplit = sem("wsplit")
        st_in = [sem(f"st_in{p}") for p in range(2)]
        ep_in = [sem(f"ep_in{p}") for p in range(2)]
        up_done, c_done, dn_done = sem("up_done"), sem("c_done"), sem("dn_done")
        silu_done, mul_done = sem("silu_done"), sem("mul_done")
        g_done, prod_done, x_out = sem("g_done"), sem("prod_done"), sem("x_out")
        m_full = sem("m_full")
        act_rel, dve_rel = sem("act_rel"), sem("dve_rel")
        ln_stats, ln_aggr, ln_eps, ln_rstd = (sem("ln_" + n) for n in ("stats", "aggr", "eps", "rstd"))
        xn_ready, split, parts_out = sem("xn_ready"), sem("split"), sem("parts_out")
        gate_lin, iz_done, scan_done = sem("gate_lin"), sem("iz_done"), sem("scan_done")
        c_stats, c_aggr, c_eps, c_rstd = (sem("c_" + n) for n in ("stats", "aggr", "eps", "rstd"))
        h_done, s_done, s_out, lg_out = sem("h_done"), sem("s_done"), sem("s_out"), sem("lg_out")

        if prep:
            wg = sb("wg", [P, 4, D])
            bg = sb("bg", [P, 4])
            bgh = sb("bgh", [P, 4])
            lnw, lnb = sb("lnw", [P, 1]), sb("lnb", [P, 1])
            rw = sb("rw", [P, E1])
            stats, mv = sb("stats", [P, TILES, 6]), sb("mv", [P, TILES, 2])
            vareps, rstd = sb("vareps", [P, TILES, 1]), sb("rstd", [P, TILES, 1])
            cstats, cmv = sb("cstats", [P, TILES, 6]), sb("cmv", [P, TILES, 2])
            cvareps, crstd = sb("cvareps", [P, TILES, 1]), sb("crstd", [P, TILES, 1])
            neghalf = sb("neghalf", [P, TILES, 1])
            zeros = sb("zeros", [P, TOK])
            xn = sb("xn", [P, TILES, D])
            xnT = sb("xnT", [P, TOK])
            oh, ol = sb("oh", [P, TOK], F16), sb("ol", [P, TOK], F16)
            lg = sb("lg", [P, TILES, E1])
            tg = [sb(f"tg{n}", [P, TOK]) for n in "fizo"]
            gl = [sb(f"gl{n}", [P, TOK]) for n in "fio"]
            iz = sb("iz", [P, TOK])
            cell = sb("cell", [P, TOK])
            cn = sb("cn", [P, TILES, D])
            hT = sb("hT", [P, TOK])
            s1 = sb("s1", [P, TOK])

        W_LOADS = 5 if prep else 0

        def turn(s, q):
            return s.p * NQ + q

        def rows(q):
            return P if q < UNITS else D // 2

        USES = ["prodT", "xnT", "logits", "f", "i", "z", "o", "cT", "nT"] if prep else ["prodT"]
        DVE_USES = [x for x in USES if x in ("prodT", "cT")]
        ACT_USES = [x for x in USES if x not in DVE_USES]
        NU, NA, ND = len(USES), len(ACT_USES), len(DVE_USES)
        PE_AT = {"prodT": 4, "xnT": 8, "logits": 9, "f": 10, "i": 11, "z": 12, "o": 13, "cT": 18, "nT": 24}
        ACT_AT = {"g": 1, "xnT": 8, "logits": 9, "f": 10, "i": 11, "z": 12, "o": 13, "nT": 24}
        DVE_AT = {"prod": 2, "xadd": 4, "stats": 5, "norm": 6, "lin": 13, "scan": 15, "cstats": 18, "cnorm": 20}
        out_d = scratch["x1"] if prep else io["out"]
        x_d = io["x"] if prep else scratch["x1"]
        out_t = out_d.rearrange("(n p) d -> p n d", p=P)
        x_t = x_d.rearrange("(n p) d -> p n d", p=P)

        def back(s):
            return Stage(s.i, 0) if s.p else Stage(s.i - 1, 1)

        def steps_at(table, q):
            return [k for k, v in table.items() if v == q]

        def run(eng, unit, follow, end):
            def body(i):
                for p in range(2):
                    s = Stage(i, p)
                    for q in range(NQ):
                        if unit:
                            unit(s, q)
                        if not s.first():
                            follow(back(s), q)
            passes(eng, body)
            if end:
                end(Stage(PASSES - 1, 1))

        block = ctx.enter_context(nc.Block())

        @block.sync
        def _(sp):
            def load(s):
                sp.dma_start(xh[s.p][:], scratch[f"xh{layer}"][:, s.tokens()]).then_inc(st_in[s.p], 16)
                sp.dma_start(xl[s.p][:], scratch[f"xl{layer}"][:, s.tokens()]).then_inc(st_in[s.p], 16)
                sp.dma_start(cw[s.p][:], scratch[f"cw{layer}"][0:SELK, s.tokens()]).then_inc(st_in[s.p], 16)

            def load_ep(s):
                sp.dma_start(sT[s.p][:], scratch[f"s{layer}"][:, s.tokens()]).then_inc(ep_in[s.p], 16)
                sp.dma_start(xres[s.p][:], x_t[:, bass.ds(s.i * (2 * TILES) + s.p * TILES, TILES), :]
                             ).then_inc(ep_in[s.p], 16)

            load(Stage(0, 0))
            half = UNITS // 2
            sp.dma_start(wup[:, 0:half, :], io[f"up{layer}"][:, 0:half, :]).then_inc(up_in, 16)
            sp.dma_start(wup[:, half:UNITS, :], io[f"up{layer}"][:, half:UNITS, :]).then_inc(up_in, 16)
            sp.dma_start(wdn[:, 0:UNITS, :], io[f"down{layer}"]).then_inc(dn_in, 16)
            if prep:
                sp.dma_start(wup[:, UNITS, 0:D // 2], io["ups"]).then_inc(up_in, 16)
                sp.dma_start(wdn[0:D // 2, UNITS, :], io["downs"]).then_inc(dn_in, 16)
                for dst, src in ((wg, "wg"), (bg, "bg"), (lnw, "lnw"), (lnb, "lnb"), (rw, "rw")):
                    sp.dma_start(dst[:], io[src]).then_inc(w_in, 16)
            load_ep(Stage(0, 0))
            load(Stage(0, 1))
            load_ep(Stage(0, 1))

            def follow(b, q):
                more = not (isinstance(b.i, int) and b.i >= PASSES - 1)
                nxt = Stage(b.i + 1, b.p)
                if q == 0 and more:
                    sp.wait_ge(up_done, b.at(NQ, NQ))
                    sp.wait_ge(c_done, b.at(NSEL, NSEL))
                    apart(sp)
                    load(nxt)
                if q == 6:
                    sp.wait_ge(dve_rel, b.at(ND, 1))
                    apart(sp)
                    sp.dma_start(out_t[:, bass.ds(b.i * (2 * TILES) + b.p * TILES, TILES), :], xnew[:]
                                 ).then_inc(x_out, 16)
                    if more:
                        load_ep(nxt)
                if prep and q == 16:
                    sp.wait_ge(split, b.at(2, 2))
                    apart(sp)
                    sp.dma_start(scratch["xh1"][:, b.tokens()], oh[:]).then_inc(parts_out, 16)
                    sp.dma_start(scratch["xl1"][:, b.tokens()], ol[:]).then_inc(parts_out, 16)
                    sp.wait_ge(act_rel, b.at(NA, ACT_USES.index("logits") + 1))
                    apart(sp)
                    sp.dma_start(scratch["lg"][:, bass.ds(b.i * (2 * TILES) + b.p * TILES, TILES), :], lg[:]
                                 ).then_inc(lg_out, 16)
                if prep and q == 28:
                    sp.wait_ge(s_done, b.at(1, 1))
                    apart(sp)
                    sp.dma_start(scratch["s1"][:, b.tokens()], s1[:]).then_inc(s_out, 16)

            def end(b):
                for q in range(NQ):
                    follow(b, q)
                sp.wait_ge(x_out, 16 * BATCH)
                if prep:
                    sp.wait_ge(parts_out, 32 * BATCH)
                    sp.wait_ge(lg_out, 16 * BATCH)
                    sp.wait_ge(s_out, 16 * BATCH)

            run(sp, None, follow, end)

        @block.gpsimd
        def _(pool):
            pool.memset(sel[:], 0.0).then_inc(cst, 1)
            for k, half in enumerate((0, SELK // 2)):
                pool.wait_ge(cst, 1 + k)
                pattern = [[-1, NSEL], [0, P]] if layer else [[-2, NSEL], [-1, 2], [0, P // 2]]
                v = sel[:] if layer else sel[:].rearrange("r n (a m) -> r n a m", a=2)
                pool.affine_select(out=v, in_=v, compare_op=ALU.not_equal, fill=1.0, base=-half,
                                   pattern=pattern, channel_multiplier=1).then_inc(cst, 1)
            if not prep:
                return
            pool.memset(zeros[:], 0.0).then_inc(cst, 1)
            pool.memset(neghalf[:], -0.5).then_inc(cst, 1)

            def follow(b, q):
                if q == 5:
                    pool.wait_ge(ln_eps, b.at(1, 1))
                    pool.tensor_tensor(rstd[:], vareps[:], neghalf[:], ALU.pow).then_inc(ln_rstd, 1)
                if q == 8:
                    pool.wait_ge(act_rel, b.at(NA, ACT_USES.index("xnT") + 1))
                    if not b.first():
                        pool.wait_ge(parts_out, b.at(32, 0))
                    pool.tensor_tensor(oh[:], xnT[:], zeros[:], ALU.add).then_inc(split, 1)
                    pool.wait_ge(split, b.at(2, 1))
                    pool.tensor_tensor(ol[:], xnT[:], oh[:], ALU.subtract).then_inc(split, 1)
                if q == 14:
                    pool.wait_ge(gate_lin, b.at(3, 2))
                    pool.wait_ge(act_rel, b.at(NA, ACT_USES.index("z") + 1))
                    if not b.first():
                        pool.wait_ge(scan_done, b.at(1, 0))
                    pool.tensor_tensor(iz[:], gl[1][:], tg[2][:], ALU.mult).then_inc(iz_done, 1)
                if q == 19:
                    pool.wait_ge(c_eps, b.at(1, 1))
                    pool.tensor_tensor(crstd[:], cvareps[:], neghalf[:], ALU.pow).then_inc(c_rstd, 1)
                if q == 25:
                    pool.wait_ge(act_rel, b.at(NA, ACT_USES.index("nT") + 1))
                    pool.wait_ge(gate_lin, b.at(3, 3))
                    if not b.first():
                        pool.wait_ge(s_out, b.at(16, 0))
                    pool.tensor_tensor(s1[:], gl[2][:], hT[:], ALU.mult).then_inc(s_done, 1)

            pool.wait_ge(cst, 5)
            run(pool, None, follow, lambda b: [follow(b, q) for q in range(NQ)])

        @block.scalar
        def _(act):
            def unit(s, q):
                k = turn(s, q) % 2
                act.wait_ge(up_done, s.at(NQ, q + 1))
                if not (s.first() and q < 2):
                    act.wait_ge(mul_done, s.at(NQ, q - 1))
                act.activation(silu[0:rows(q), k, :], hps[0:rows(q), k, :], ACT.Silu, scale=1.0 / WS
                               ).then_inc(silu_done, 1)

            def use(b, name):
                k = USES.index(name)
                act.wait_ge(m_full, b.at(NU, k + 1))
                return mps[:, k % 3, :]

            def follow(b, q):
                for name in steps_at(ACT_AT, q):
                    if name == "g":
                        act.wait_ge(dn_done, b.at(NQ, NQ))
                        if not b.first():
                            act.wait_ge(prod_done, b.at(1, 0))
                        act.activation(gT[:], yps[:], ACT.Silu).then_inc(g_done, 1)
                    elif not prep:
                        continue
                    elif name == "xnT":
                        src = use(b, name)
                        if not b.first():
                            act.wait_ge(split, b.at(2, 0))
                        act.activation(xnT[:], src, ACT.Copy).then_inc(act_rel, 1)
                    elif name == "logits":
                        src = use(b, name)
                        if not b.first():
                            act.wait_ge(lg_out, b.at(16, 0))
                        act.activation(lg[:].rearrange("p t e -> p (t e)"), src[:, 0:TILES * E1], ACT.Copy
                                       ).then_inc(act_rel, 1)
                    elif name in "fizo":
                        src = use(b, name)
                        n, w = "fizo".index(name), "fioz".index(name)
                        if not b.first() and name == "z":
                            act.wait_ge(iz_done, b.at(1, 0))
                        elif not b.first():
                            act.wait_ge(gate_lin, b.at(3, 0))
                        act.activation(tg[n][:], src, ACT.Tanh, scale=1.0 if name == "z" else 0.5,
                                       bias=bgh[:, w:w + 1]).then_inc(act_rel, 1)
                    elif name == "nT":
                        src = use(b, name)
                        if not b.first():
                            act.wait_ge(s_done, b.at(1, 0))
                        act.activation(hT[:], src, ACT.Tanh, scale=lnw[:], bias=lnb[:]).then_inc(act_rel, 1)

            if prep:
                act.wait_ge(w_in, 16 * W_LOADS)
                act.activation(bgh[:, 0:3], bg[:, 0:3], ACT.Copy, scale=0.5).then_inc(h_done, 1)
                act.activation(bgh[:, 3:4], bg[:, 3:4], ACT.Copy).then_inc(h_done, 1)
                act.wait_ge(h_done, 2)
            run(act, unit, follow, lambda b: [follow(b, q) for q in range(NQ)])

        @block.tensor
        def _(pe):
            def down(s, q):
                pe.wait_ge(mul_done, s.at(NQ, q + 1))
                if q == 0 and not s.first():
                    pe.wait_ge(g_done, s.at(1, 0))
                if q == 0 and not prep:
                    pe.matmul(yps[:], identh[:], xh[s.p][:], start=True, stop=False)
                    pe.matmul(yps[:], identh[:], xl[s.p][:], start=False, stop=False)
                pe.matmul(yps[:], wdn[0:rows(q), q, :], hid[0:rows(q), turn(s, q) % HW, :],
                          start=(q == 0 and prep), stop=(q == NQ - 1)).then_inc(dn_done, 1)

            def unit(s, q):
                if q == 0:
                    pe.wait_ge(st_in[s.p], s.own(48, 48))
                if q < UNITS and q % UPC == 0:
                    n = q // UPC
                    if not (s.first() and n < 2):
                        pe.wait_ge(mul_done, s.at(NQ, (n - 1) * UPC - (NQ - UNITS if n < 2 else 0)))
                    pe.matmul(cps[:, n % 2, :], sel[:, n, :], cw[s.p][:], start=True, stop=True
                              ).then_inc(c_done, 1)
                if not (s.first() and q < 2):
                    pe.wait_ge(silu_done, s.at(NQ, q - 1))
                bank = hps[0:rows(q), turn(s, q) % 2, :]
                high, low = wuh[:, q, 0:rows(q)], wul[:, q, 0:rows(q)]
                pe.matmul(bank, high, xh[s.p][:], start=True, stop=False)
                pe.matmul(bank, high, xl[s.p][:], start=False, stop=False)
                pe.matmul(bank, low, xh[s.p][:], start=False, stop=True).then_inc(up_done, 1)
                if q >= 2:
                    down(s, q - 2)
                elif not s.first():
                    down(back(s), NQ - 2 + q)

            def bank_free(b, name):
                k = USES.index(name)
                old = USES[k - 3] if k >= 3 else USES[k - 3 + NU] if prep else "prodT"
                prev = k < 3
                if prev and b.first():
                    return
                sem_, n, m = ((act_rel, NA, ACT_USES.index(old)) if old in ACT_USES else
                              (dve_rel, ND, DVE_USES.index(old)))
                pe.wait_ge(sem_, b.at(n, m + 1 - (n if prev else 0)))

            def follow(b, q):
                for name in steps_at(PE_AT, q):
                    if name not in USES:
                        continue
                    k = USES.index(name)
                    bank = mps[:, k % 3, :]
                    bank_free(b, name)
                    if name == "prodT":
                        pe.wait_ge(prod_done, b.at(1, 1))
                        for t in range(TILES):
                            op = pe.transpose(bank[:, t * P:t * P + P], prod[:, t * P:t * P + P], ident[:])
                    elif name == "xnT":
                        pe.wait_ge(xn_ready, b.at(TILES, TILES))
                        for t in range(TILES):
                            op = pe.transpose(bank[:, t * P:t * P + P], xn[:, t, :], ident[:])
                    elif name == "logits":
                        pe.wait_ge(act_rel, b.at(NA, ACT_USES.index("xnT") + 1))
                        for t in range(TILES):
                            op = pe.matmul(bank[:, t * E1:t * E1 + E1], xnT[:, t * P:t * P + P], rw[:],
                                           start=True, stop=True)
                    elif name in "fizo":
                        op = pe.matmul(bank, wg[:, "fioz".index(name), :], xnT[:], start=True, stop=True)
                    elif name == "cT":
                        pe.wait_ge(scan_done, b.at(1, 1))
                        for t in range(TILES):
                            op = pe.transpose(bank[:, t * P:t * P + P], cell[:, t * P:t * P + P], ident[:])
                    elif name == "nT":
                        pe.wait_ge(dve_rel, b.at(ND, 2))
                        for t in range(TILES):
                            op = pe.transpose(bank[:, t * P:t * P + P], cn[:, t, :], ident[:])
                    op.then_inc(m_full, 1)

            def end(b):
                down(b, NQ - 2)
                down(b, NQ - 1)
                for q in range(NQ):
                    follow(b, q)

            pe.wait_ge(cst, 3)
            pe.wait_ge(wsplit, 6 if prep else 4)
            pe.wait_ge(dn_in, 32 if prep else 16)
            if prep:
                pe.wait_ge(w_in, 16 * W_LOADS)
            run(pe, unit, follow, end)

        @block.vector
        def _(dve):
            half = UNITS // 2
            dve.wait_ge(up_in, 48 if prep else 32)
            for k in range(2):
                r = slice(k * half, k * half + half)
                dve.tensor_scalar(wuh[:, r, :], wup[:, r, :], WS, None, ALU.mult).then_inc(wsplit, 1)
                dve.wait_ge(wsplit, 2 * k + 1)
                dve.scalar_tensor_tensor(wul[:, r, :], wup[:, r, :], WS, wuh[:, r, :], ALU.mult, ALU.subtract
                                         ).then_inc(wsplit, 1)
            if prep:
                r = (slice(None), UNITS, slice(0, D // 2))
                dve.tensor_scalar(wuh[r], wup[r], WS, None, ALU.mult).then_inc(wsplit, 1)
                dve.wait_ge(wsplit, 5)
                dve.scalar_tensor_tensor(wul[r], wup[r], WS, wuh[r], ALU.mult, ALU.subtract
                                         ).then_inc(wsplit, 1)

            def unit(s, q):
                k = turn(s, q)
                dve.wait_ge(silu_done, s.at(NQ, q + 1))
                if q < UNITS and q % UPC == 0:
                    dve.wait_ge(c_done, s.at(NSEL, q // UPC + 1))
                if not (s.first() and q < HW):
                    dve.wait_ge(dn_done, s.at(NQ, q - HW + 1))
                if q < UNITS:
                    dve.tensor_tensor(hid[:, k % HW, :], silu[:, k % 2, :], cps[:, (q // UPC) % 2, :], ALU.mult
                                      ).then_inc(mul_done, 1)
                else:
                    dve.tensor_scalar(hid[0:rows(q), k % HW, :], silu[0:rows(q), k % 2, :], 1.0, None, ALU.mult
                                      ).then_inc(mul_done, 1)

            def follow(b, q):
                for name in steps_at(DVE_AT, q):
                    if name == "prod":
                        dve.wait_ge(g_done, b.at(1, 1))
                        dve.wait_ge(ep_in[b.p], b.own(32, 32))
                        if not b.first():
                            dve.wait_ge(m_full, b.at(NU, 1 - NU))
                        dve.tensor_tensor(prod[:], gT[:], sT[b.p][:], ALU.mult).then_inc(prod_done, 1)
                    elif name == "xadd":
                        dve.wait_ge(m_full, b.at(NU, 1))
                        if not b.first():
                            dve.wait_ge(x_out, b.at(16, 0))
                        dve.tensor_tensor(xnew[:].rearrange("p t d -> p (t d)"),
                                          xres[b.p][:].rearrange("p t d -> p (t d)"), mps[:, 0, :], ALU.add
                                          ).then_inc(dve_rel, 1)
                    elif not prep:
                        continue
                    elif name == "stats":
                        dve.wait_ge(dve_rel, b.at(ND, 1))
                        if not b.first():
                            dve.wait_ge(ln_rstd, b.at(1, 0))
                        apart(dve)
                        for t in range(TILES):
                            dve.bn_stats(stats[:, t, :], xnew[:, t, :]).then_inc(ln_stats, 1)
                        dve.wait_ge(ln_stats, b.at(TILES, TILES))
                        apart(dve)
                        for t in range(TILES):
                            dve.bn_aggr(mv[:, t, :], stats[:, t, :]).then_inc(ln_aggr, 1)
                        dve.wait_ge(ln_aggr, b.at(TILES, TILES))
                        dve.tensor_scalar(vareps[:], mv[:, :, 1:2], LN_EPS, None, ALU.add).then_inc(ln_eps, 1)
                    elif name == "norm":
                        dve.wait_ge(ln_rstd, b.at(1, 1))
                        if not b.first():
                            dve.wait_ge(m_full, b.at(NU, 2 - NU))
                        for t in range(TILES):
                            dve.tensor_scalar(xn[:, t, :], xnew[:, t, :], mv[:, t, 0:1], rstd[:, t, :],
                                              ALU.subtract, ALU.mult).then_inc(xn_ready, 1)
                    elif name == "lin":
                        for k, g in enumerate("fio"):
                            dve.wait_ge(act_rel, b.at(NA, ACT_USES.index(g) + 1))
                            if g == "o" and not b.first():
                                dve.wait_ge(s_done, b.at(1, 0))
                            dve.tensor_scalar(gl[k][:], tg["fizo".index(g)][:], 0.5, 0.5, ALU.mult, ALU.add
                                              ).then_inc(gate_lin, 1)
                    elif name == "scan":
                        dve.wait_ge(iz_done, b.at(1, 1))
                        if not b.first():
                            dve.wait_ge(m_full, b.at(NU, USES.index("cT") + 1 - NU))
                        dve.tensor_tensor_scan(cell[:], gl[0][:], iz[:], 0.0, ALU.mult, ALU.add
                                               ).then_inc(scan_done, 1)
                    elif name == "cstats":
                        dve.wait_ge(m_full, b.at(NU, USES.index("cT") + 1))
                        bank = mps[:, USES.index("cT") % 3, :]
                        if not b.first():
                            dve.wait_ge(c_rstd, b.at(1, 0))
                        apart(dve)
                        for t in range(TILES):
                            dve.bn_stats(cstats[:, t, :], bank[:, t * P:t * P + P]).then_inc(c_stats, 1)
                        dve.wait_ge(c_stats, b.at(TILES, TILES))
                        apart(dve)
                        for t in range(TILES):
                            dve.bn_aggr(cmv[:, t, :], cstats[:, t, :]).then_inc(c_aggr, 1)
                        dve.wait_ge(c_aggr, b.at(TILES, TILES))
                        dve.tensor_scalar(cvareps[:], cmv[:, :, 1:2], LN_EPS, None, ALU.add).then_inc(c_eps, 1)
                    elif name == "cnorm":
                        bank = mps[:, USES.index("cT") % 3, :]
                        dve.wait_ge(c_rstd, b.at(1, 1))
                        if not b.first():
                            dve.wait_ge(m_full, b.at(NU, 0))
                        for t in range(TILES):
                            op = dve.tensor_scalar(cn[:, t, :], bank[:, t * P:t * P + P], cmv[:, t, 0:1],
                                                   crstd[:, t, :], ALU.subtract, ALU.mult)
                        op.then_inc(dve_rel, 1)

            run(dve, unit, follow, lambda b: [follow(b, q) for q in range(NQ)])



def route_phase(nc, scratch, identh):
    with ExitStack() as ctx:
        ALL = NTOK // P

        def sb(name, shape, dt=F32):
            return ctx.enter_context(nc.sbuf_tensor("r_" + name, shape, dt))

        def sem(name):
            return ctx.enter_context(nc.semaphore("r_" + name))

        grid = [P, ALL, E1]
        lg, shifted, expo, probs, others = (sb(n, grid) for n in ("lg", "shifted", "expo", "probs", "others"))
        priority = sb("priority", [P, 1, E1])
        top, total, inverse = (sb(n, [P, ALL, 1]) for n in ("top", "total", "inverse"))
        best = [sb(f"best{k}", [P, ALL, 1]) for k in range(K1)]
        first = [sb(f"first{k}", [P, ALL, 1]) for k in range(K1)]
        equal = [sb(f"equal{k}", grid) for k in range(K1)]
        rated = [sb(f"rated{k}", grid) for k in range(K1)]
        chosen = [sb(f"chosen{k}", grid) for k in range(K1)]
        selected = sb("selected", grid)
        selh = sb("selh", grid, BF16)
        pair_sum, pair_inv = sb("pair_sum", [P, ALL, 1]), sb("pair_inv", [P, ALL, 1])
        upto, before, rank, keep = (sb(n, grid) for n in ("upto", "before", "rank", "keep"))
        share, kept, cw = (sb(n, grid) for n in ("share", "kept", "cw"))
        cwhl = sb("cwhl", [P, ALL, 2, E1], F16)
        cwT = sb("cwT", [2 * E1, NTOK], F16)
        ones = sb("ones", [P, P], BF16)
        onesf = sb("onesf", [P, ALL])
        earlier = sb("earlier", [P, P], BF16)
        counts = ctx.enter_context(nc.psum_tensor("r_counts", [P, 2, 512], F32))
        tps = ctx.enter_context(nc.psum_tensor("r_tps", [2 * E1, NTOK], F16))

        lg_in, init, masks = sem("lg_in"), sem("init"), sem("masks")
        ones_set = sem("ones_set")
        step = sem("step")
        exp_done, counted, transposed, copied, out = (sem(n) for n in (
            "exp_done", "counted", "transposed", "copied", "out"))
        block = ctx.enter_context(nc.Block())
        SHIFTED, SELH, SPLIT = 2, 18, 29

        @block.sync
        def _(sp):
            sp.dma_start(lg[:], scratch["lg"]).then_inc(lg_in, 16)
            sp.wait_ge(copied, 4)
            sp.dma_start(scratch["cw1"], cwT[:]).then_inc(out, 16)
            sp.wait_ge(out, 16)

        @block.gpsimd
        def _(pool):
            pool.memset(ones[:], 1.0).then_inc(ones_set, 1)
            pool.memset(earlier[:], 1.0).then_inc(ones_set, 1)
            pool.wait_ge(ones_set, 2)
            pool.affine_select(out=earlier[:], in_=earlier[:], compare_op=ALU.is_ge, fill=0.0, base=-1,
                               pattern=[[1, P]], channel_multiplier=-1).then_inc(masks, 1)

        @block.scalar
        def _(act):
            act.wait_ge(step, SHIFTED)
            act.activation(expo[:], shifted[:], ACT.Exp).then_inc(exp_done, 1)
            for k in range(4):
                act.wait_ge(transposed, k + 1)
                r = slice(k * NTOK // 4, (k + 1) * NTOK // 4)
                act.activation(cwT[:, r], tps[:, r], ACT.Copy).then_inc(copied, 1)

        @block.tensor
        def _(pe):
            pe.wait_ge(masks, 1)
            pe.wait_ge(step, SELH)
            flat = selh[:].rearrange("p t e -> p (t e)")
            pe.matmul(counts[:, 0, 0:ALL * E1], earlier[:], flat, start=True, stop=True).then_inc(counted, 1)
            pe.matmul(counts[:, 1, 0:ALL * E1], ones[:], flat, start=True, stop=True).then_inc(counted, 1)
            pe.wait_ge(step, SPLIT)
            for t in range(ALL):
                op = pe.transpose(tps[:, t * P:t * P + P], cwhl[:, t].rearrange("p a e -> p (a e)"), identh[:])
                if t % (ALL // 4) == ALL // 4 - 1:
                    op.then_inc(transposed, 1)

        @block.vector
        def _(dve):
            n = 0

            def done(op):
                nonlocal n
                op.then_inc(step, 1)
                n += 1
                dve.wait_ge(step, n)

            wide = lambda t: t[:].broadcast_to(grid)
            dve.memset(onesf[:], 1.0).then_inc(init, 1)
            for e in range(E1):
                dve.memset(priority[:, :, e:e + 1], float(E1 - e)).then_inc(init, 1)
            dve.wait_ge(init, 1 + E1)
            dve.wait_ge(lg_in, 16)
            done(dve.tensor_reduce(top[:], lg[:], AX.X, ALU.max))
            done(dve.tensor_tensor(shifted[:], lg[:], wide(top), ALU.subtract))
            assert n == SHIFTED
            dve.wait_ge(exp_done, 1)
            done(dve.tensor_reduce(total[:], expo[:], AX.X, ALU.add))
            done(dve.reciprocal(inverse[:], total[:]))
            done(dve.tensor_tensor(probs[:], expo[:], wide(inverse), ALU.mult))
            for k in range(K1):
                src = others if k else probs
                done(dve.tensor_reduce(best[k][:], src[:], AX.X, ALU.max))
                done(dve.tensor_tensor(equal[k][:], src[:], wide(best[k]), ALU.is_equal))
                done(dve.tensor_tensor(rated[k][:], equal[k][:], priority[:].broadcast_to(grid), ALU.mult))
                done(dve.tensor_reduce(first[k][:], rated[k][:], AX.X, ALU.max))
                done(dve.tensor_tensor(chosen[k][:], rated[k][:], wide(first[k]), ALU.is_equal))
                if not k:
                    done(dve.scalar_tensor_tensor(others[:], chosen[0][:], -2.0, probs[:], ALU.mult, ALU.add))
            done(dve.tensor_tensor(selected[:], chosen[0][:], chosen[1][:], ALU.add))
            done(dve.tensor_scalar(selh[:], selected[:], 1.0, None, ALU.mult))
            assert n == SELH
            done(dve.tensor_tensor(pair_sum[:], best[0][:], best[1][:], ALU.add))
            done(dve.reciprocal(pair_inv[:], pair_sum[:]))
            done(dve.tensor_tensor(share[:], probs[:], wide(pair_inv), ALU.mult))
            done(dve.tensor_tensor(kept[:], share[:], selected[:], ALU.mult))
            dve.wait_ge(counted, 2)
            tile_counts = counts[:, 1, 0:ALL * E1].rearrange("p (t e) -> p t e", e=E1)
            for e in range(E1 - 1):
                dve.tensor_tensor_scan(upto[:, :, e], onesf[:], tile_counts[:, :, e], 0.0, ALU.mult, ALU.add
                                       )
            done(dve.tensor_tensor_scan(upto[:, :, E1 - 1], onesf[:], tile_counts[:, :, E1 - 1], 0.0, ALU.mult,
                                        ALU.add))
            done(dve.tensor_tensor(before[:], upto[:], tile_counts, ALU.subtract))
            done(dve.tensor_tensor(rank[:], before[:], counts[:, 0, 0:ALL * E1].rearrange(
                "p (t e) -> p t e", e=E1), ALU.add))
            done(dve.tensor_scalar(keep[:], rank[:], float(CAPACITY), None, ALU.is_lt))
            done(dve.tensor_tensor(cw[:], kept[:], keep[:], ALU.mult))
            done(dve.tensor_scalar(cwhl[:, :, 0, :], cw[:], 1.0, None, ALU.mult))
            done(dve.tensor_tensor(cwhl[:, :, 1, :], cw[:], cwhl[:, :, 0, :], ALU.subtract))
            assert n == SPLIT



def build_program(nc, io):
    def dram(name, shape, dt=F32):
        return nc.dram_tensor("t_" + name, shape, dt, kind="Internal").ap()

    scratch = {
        "parts": dram("parts", [2, 3, TILES, P, TOK // TILES], BF16),
        "lg": dram("lg", [P, NTOK // P, E1]), "x1": dram("x1", [NTOK, D]),
        "cw0": dram("cw0", [2 * E0, NTOK], F16), "cw1": dram("cw1", [2 * E1, NTOK], F16)}
    for layer in range(2):
        for part in ("xh", "xl"):
            scratch[f"{part}{layer}"] = dram(f"{part}{layer}", [P, NTOK], F16)
        scratch[f"s{layer}"] = dram(f"s{layer}", [P, NTOK])

    with ExitStack() as ctx:
        ident = ctx.enter_context(nc.sbuf_tensor("ident", [P, P], F32))
        identh = ctx.enter_context(nc.sbuf_tensor("identh", [P, P], F16))
        consts_ready = ctx.enter_context(nc.semaphore("consts_ready"))

        with nc.Block() as block:
            @block.gpsimd
            def _(pool):
                pool.memset(ident[:], 0.0).then_inc(consts_ready, 1)
                pool.memset(identh[:], 0.0).then_inc(consts_ready, 1)
                pool.wait_ge(consts_ready, 2)
                for m in (ident, identh):
                    pool.affine_select(out=m[:], in_=m[:], compare_op=ALU.not_equal, fill=1.0, base=0,
                                       pattern=[[-1, P]], channel_multiplier=1).then_inc(consts_ready, 1)

        attention_phase(nc, io, scratch, ident, identh, consts_ready)
        mixture_phase(nc, io, scratch, ident, identh, 0)
        route_phase(nc, scratch, identh)
        mixture_phase(nc, io, scratch, ident, identh, 1)


def kernel(**inputs):
    import concourse.bacc as bacc
    from concourse.bass_utils import run_bass_kernel_spmd

    def permuted(w):
        return w.reshape(-1, CH, DH).transpose(0, 2, 1).reshape(-1, D)

    a = {k: np.asarray(v) for k, v in inputs.items()}
    arrays = {
        "x": a["L0_attn_x"].reshape(NTOK, D),
        "wq": permuted(a["L0_attn_Wq"]), "wk": permuted(a["L0_attn_Wk"]),
        "wv": a["L0_attn_Wv"], "wf": a["L0_attn_Wf"],
        "bq": permuted(a["L0_attn_bq"]).reshape(D, 1), "bk": permuted(a["L0_attn_bk"]).reshape(D, 1),
        "bf": a["L0_attn_bf"].reshape(D, 1), "bv": a["L0_attn_bv"].reshape(1, D),
        "cent": a["L0_ffn_centroids"].T, "ebias": a["L0_ffn_expert_biases"].reshape(1, E0),
        "ups": a["L0_ffn_Ws_up"], "downs": a["L0_ffn_Ws_down"],
        "up0": a["L0_ffn_W_up"].transpose(1, 0, 2).reshape(D, UNITS, P),
        "down0": a["L0_ffn_W_down"].reshape(UNITS, P, D).transpose(1, 0, 2),
        "wg": a["L1_attn_W"].T.reshape(D, 4, D), "bg": a["L1_attn_b"].reshape(4, D).T,
        "lnw": a["L1_attn_ln_w"].reshape(D, 1), "lnb": a["L1_attn_ln_b"].reshape(D, 1),
        "rw": a["L1_ffn_router_w"].T,
        "up1": a["L1_ffn_w1"].transpose(1, 0, 2).reshape(D, UNITS, P),
        "down1": a["L1_ffn_w2"].reshape(UNITS, P, D).transpose(1, 0, 2)}
    arrays = {k: np.ascontiguousarray(v) for k, v in arrays.items()}

    nc = bacc.Bacc("TRN2", target_bir_lowering=False, num_devices=1)
    io = {k: nc.dram_tensor(k, v.shape, mybir.dt.from_np(v.dtype), kind="ExternalInput").ap()
          for k, v in arrays.items()}
    io["out"] = nc.dram_tensor("out", [NTOK, D], F32, kind="ExternalOutput").ap()
    build_program(nc, io)
    r = run_bass_kernel_spmd(nc, [arrays], core_ids=[0])
    return r.results[0]["out"].reshape(BATCH, SEQ, D)
```

```python
import numpy as np

import concourse.bass as bass
from concourse import mybir
from contextlib import ExitStack

ALU = mybir.AluOpType
ACT = mybir.ActivationFunctionType
AX = mybir.AxisListType
F32 = mybir.dt.float32
BF16 = mybir.dt.bfloat16
F16 = mybir.dt.float16

P = 128
D = 128
BATCH, SEQ = 8, 512
NTOK = BATCH * SEQ
TOK = 512
TILES = TOK // P
PASSES = BATCH // 2
CH, DH = 16, 8
GT = 32
NG = P // GT
KT = CH * GT // P
SCALE = 8.0
LN_EPS = 1e-5
E0, K0 = 64, 8
E1, K1 = 8, 2
CAPACITY = int(1.25 * NTOK * K1 / E1) + 1
UNITS = 32
WS = 64.0
TERMS = [(a, b) for a in range(3) for b in range(3)]
ROWS = DH * len(TERMS)
MROW = 96
KROWS = MROW + 2


class Stage:

    def __init__(self, i, p):
        self.i, self.p = i, p

    def at(self, per, k):
        return self.i * (2 * per) + (self.p * per + k)

    def own(self, per, k):
        return self.i * per + k

    def next(self):
        return Stage(self.i, 1) if self.p == 0 else Stage(self.i + 1, 0)

    def tokens(self):
        return bass.ds(self.i * (2 * TOK) + self.p * TOK, TOK)

    def first(self):
        return isinstance(self.i, int) and self.i == 0 and self.p == 0

    def last(self):
        return isinstance(self.i, int) and self.i == PASSES - 1 and self.p == 1


def passes(eng, body):
    body(0)
    with eng.Fori(1, PASSES - 1) as i:
        body(i)
    body(PASSES - 1)


def apart(eng):
    eng.nop(nofuse=True)



def attention_phase(nc, io, scratch, ident, identh, consts_ready, sel, sel_built):
    with ExitStack() as ctx:
        def sb(name, shape, dt=F32):
            return ctx.enter_context(nc.sbuf_tensor(name, shape, dt))

        def sem(name):
            return ctx.enter_context(nc.semaphore(name))

        wq, wk, wv, wf = (sb(f"a_w{n}", [P, D]) for n in "qkvf")
        bq, bk, bf = (sb(f"a_b{n}", [P, 1]) for n in "qkf")
        bv = sb("a_bv", [P, KT, DH])
        cent = sb("a_cent", [P, E0])
        ebias = sb("a_ebias", [P, E0])
        xin = [sb(f"a_xin{p}", [P, TILES, D]) for p in range(2)]
        xn = [sb(f"a_xn{p}", [P, TILES, D]) for p in range(2)]
        stats = sb("a_stats", [P, TILES, 6])
        meanvar = sb("a_meanvar", [P, TILES, 2])
        rstd = sb("a_rstd", [P, TILES, 1])
        vareps = sb("a_vareps", [P, TILES, 1])
        cvareps = sb("a_cvareps", [P, 1])
        neghalf = sb("a_neghalf", [P, TILES])
        xnT = sb("a_xnT", [P, TOK])
        xh = sb("a_xh", [P, TOK], F16)
        xl = sb("a_xl", [P, TOK], F16)
        full = [sb(f"a_{n}32", [P, TOK]) for n in "qk"]
        rest = [sb(f"a_{n}rest", [P, TOK]) for n in "qk"]
        parts = [sb(f"a_{n}parts", [P, 3, TOK], BF16) for n in "qk"]
        stack = [[sb(f"a_{n}stack{p}", [KROWS, TILES, CH * GT, NG], BF16) for p in range(2)] for n in "qk"]
        mrow = sb("a_mrow", [KROWS, 4, 8, NG, GT], BF16)
        vtmp = sb("a_vtmp", [P, TOK // GT, KT, DH])
        vst = [sb(f"a_vst{p}", [P, TOK // GT, KT, 32]) for p in range(2)]
        probs = sb("a_probs", [P, 2, NG, 512])
        mx = [sb(f"a_mx{p}", [P, 16]) for p in range(2)]
        zeros = sb("a_zeros", [P, TOK])
        ones = sb("a_ones", [P, E0])
        mneg = sb("a_mneg", [P, 2, 32], BF16)
        mT = sb("a_mT", [P, 2, 32], BF16)
        oT = sb("a_oT", [P, CH, 32])
        rden = sb("a_rden", [P, CH, 1])
        ctx_sb = sb("a_ctx", [P, D])
        res = sb("a_res", [P, D])
        xlast = sb("a_xlast", [P, D])
        cstats = sb("a_cstats", [P, 6])
        cmv = sb("a_cmv", [P, 2])
        crstd = sb("a_crstd", [P, 1])
        cn = sb("a_cn", [P, D])
        cT = sb("a_cT", [P, TOK])
        sT = sb("a_sT", [P, TOK])
        aff = sb("a_aff", [P, TILES, E0])
        biased = sb("a_biased", [P, TILES, E0])
        best = sb("a_best", [P, TILES, 8])
        dropped = sb("a_dropped", [P, TILES, E0])
        mask = sb("a_mask", [P, TILES, E0])
        esig = sb("a_esig", [P, TILES, E0])
        esum = sb("a_esum", [P, TILES, E0])
        sig = sb("a_sig", [P, TILES, E0])
        wsel = sb("a_wsel", [P, TILES, E0])
        wsum = sb("a_wsum", [P, TILES, 1])
        wsume = sb("a_wsume", [P, TILES, 1])
        wrec = sb("a_wrec", [P, TILES, 1])
        cw = sb("a_cw", [P, TILES, E0])
        cwhl = sb("a_cwhl", [P, TILES, 2, E0], F16)
        cwT = sb("a_cwT", [P, TOK], F16)

        score = ctx.enter_context(nc.psum_tensor("a_score", [P, 2, 512], F32))
        mxps = ctx.enter_context(nc.psum_tensor("a_mxps", [P, 2, 2, 512], F32))
        ops = ctx.enter_context(nc.psum_tensor("a_ops", [P, 512], F32))
        misc = ctx.enter_context(nc.psum_tensor("a_misc", [P, 512], F32))
        misch = misc[:].bitcast(F16)

        w_in = sem("a_w_in")
        x_in = [sem(f"a_x_in{p}") for p in range(2)]
        ln_eps, c_eps = sem("a_ln_eps"), sem("a_c_eps")
        ln_stats, ln_aggr, ln_rstd = sem("a_ln_stats"), sem("a_ln_aggr"), sem("a_ln_rstd")
        xn_ready = sem("a_xn_ready")
        misc_full, misc_free = sem("a_misc_full"), sem("a_misc_free")
        split = sem("a_split")
        x_out = sem("a_x_out")
        qk_in = [sem(f"a_qk_in{p}") for p in range(2)]
        parts_out = sem("a_parts_out")
        init = sem("a_init")
        v_ready = sem("a_v_ready")
        score_full, exp_done = sem("a_score_full"), sem("a_exp_done")
        mx_full, mx_done = sem("a_mx_full"), sem("a_mx_done")
        mneg_done, mT_done = sem("a_mneg_done"), sem("a_mT_done")
        m_in, m_placed = sem("a_m_in"), sem("a_m_placed")
        pv_done = sem("a_pv_done")
        o_out, den_done = sem("a_o_out"), sem("a_den_done")
        kept = sem("a_kept")
        ctx_done, res_done = sem("a_ctx_done"), sem("a_res_done")
        c_stats, c_aggr, c_rstd, cn_done = (sem(f"a_c_{n}") for n in ("stats", "aggr", "rstd", "norm"))
        s_out = sem("a_s_out")
        biased_done, best_done, drop_done = sem("a_biased"), sem("a_best_done"), sem("a_drop_done")
        esig_done, pool_r, dve_r = sem("a_esig_done"), sem("a_pool_router"), sem("a_dve_router")
        cw_out = sem("a_cw_out")

        W_LOADS = 4 + 3 + NG + 2
        SLOTS_OF_STACK = 2 * len(TERMS)

        MID = ["xnT", "q", "k", "cn3p", "sTp", "V", "logits", "cn0", "cn1", "cwT", "cn2"]
        FIRST = [x for x in MID if x not in ("cn3p", "sTp")]
        START = ["xnT", "q", "k", "V", "logits", "cwT"]
        LAST = ["cn3p", "sTp", "cn0", "cn1", "cn2", "cn3", "sT"]

        def misc_use(s, name):
            if s is None:
                return START.index(name)
            if s.first():
                return len(START) + FIRST.index(name)
            if s.last():
                return len(START) - 2 + len(MID) * (BATCH - 1) + LAST.index(name)
            return s.at(len(MID), len(START) - 2 + MID.index(name))

        SLOTS = {(0, 1): ["xnT"], (0, 2): ["q"], (0, 3): ["k", "cn3p"], (1, 0): ["sTp"], (1, 1): ["V"],
                 (1, 2): ["logits"], (1, 3): ["cn0"], (2, 3): ["cn1"], (3, 1): ["cwT"], (3, 3): ["cn2"]}

        def slot(s, tau, kt):
            names = SLOTS.get((tau, kt), [])
            skip = ("cn3p", "sTp") if s.first() else ()
            if s.last():
                skip = ("xnT", "q", "k", "V", "logits", "cwT")
            return [x for x in names if x not in skip]

        def mx_pairs(s, tau, kt):
            ahead = tau + 1 if kt < 2 else tau + 2
            js = (4, 5) if kt == 0 else (6, 7) if kt == 1 else (0, 1) if kt == 2 else (2, 3)
            if s.last() and ahead > TILES - 1:
                return []
            return [(ahead, j) for j in js]

        def period(f):
            def body(i):
                for p in range(2):
                    for tau in range(TILES):
                        f(Stage(i, p), tau)
            return body

        NONE = Stage(0, 0)

        block = ctx.enter_context(nc.Block())

        @block.sync
        def _(sp):
            x_t = io["x"].rearrange("(n p) d -> p n d", p=P)

            def load_x(s):
                apart(sp)
                sp.dma_start(xin[s.p][:], x_t[:, bass.ds(s.i * (2 * TILES) + s.p * TILES, TILES), :]
                             ).then_inc(x_in[s.p], 16)

            def stack_in(n, side):
                if not (isinstance(n.i, int) and n.i == 0 and n.p == 0):
                    b = Stage(n.i, 0) if n.p else Stage(n.i - 1, 1)
                    sp.wait_ge(qk_in[b.p], b.own(16 * SLOTS_OF_STACK, 16 * SLOTS_OF_STACK))
                    apart(sp)
                sp.wait_ge(split, n.at(12, 5 * side + 5))
                apart(sp)
                there = scratch["parts"][side]
                for a in range(3):
                    sp.dma_start(there[a].rearrange("n r x -> r n x"),
                                 parts[side][:, a, :].rearrange("p (n x) -> p n x", n=TILES)
                                 ).then_inc(parts_out, 16)
                sp.wait_ge(parts_out, n.at(96, 48 * side + 48))
                for r, term in enumerate(TERMS):
                    sp.dma_start(stack[side][n.p][DH * r:DH * r + DH].rearrange("j n c g -> j n (c g)"),
                                 there[term[side]].rearrange("n (j c) x -> j n (c x)", j=DH)
                                 ).then_inc(qk_in[n.p], 16)

            def x_parts_out(n):
                sp.wait_ge(split, n.at(12, 12))
                apart(sp)
                sp.dma_start(scratch["xh0"][:, n.tokens()], xh[:]).then_inc(x_out, 16)
                sp.dma_start(scratch["xl0"][:, n.tokens()], xl[:]).then_inc(x_out, 16)

            def max_rows(s, tau):
                if not (s.first() and tau == 0):
                    sp.wait_ge(m_placed, s.at(4 * TILES, 4 * tau))
                    apart(sp)
                sp.wait_ge(mT_done, s.at(TILES, tau + 1))
                for a in range(2):
                    sp.dma_start(mrow[MROW + a:MROW + a + 1].rearrange("o q r g t -> o (q r g t)"), mT[:, a, :]
                                 ).then_inc(m_in, 16)

            def cw_store(s, n):
                sp.wait_ge(misc_free, misc_use(s, "cwT") + 1)
                apart(sp)
                sp.dma_start(scratch["cw0"][:, n.tokens()], cwT[:]).then_inc(cw_out, 16)

            def s_store(s, name, prev):
                sp.wait_ge(misc_free, misc_use(s, name) + 1)
                apart(sp)
                sp.dma_start(scratch["s0"][:, prev], sT[:]).then_inc(s_out, 16)

            for dst, src in ((wq, "wq"), (wk, "wk"), (wv, "wv"), (wf, "wf"), (bq, "bq"), (bk, "bk"), (bf, "bf"),
                             (cent, "cent")):
                sp.dma_start(dst[:], io[src]).then_inc(w_in, 16)
            sp.dma_start(ebias[:], io["ebias"].broadcast_to([P, E0])).then_inc(w_in, 16)
            for cq in range(NG):
                sp.dma_start(bv[GT * cq:GT * cq + GT, :, :],
                             io["bv"].rearrange("o (k c j) -> o k c j", c=4, j=DH)[:, :, cq, :]
                             .broadcast_to([GT, KT, DH])).then_inc(w_in, 16)
            load_x(Stage(0, 0))
            load_x(Stage(0, 1))
            sp.wait_ge(init, 14)
            stack_in(NONE, 0)
            stack_in(NONE, 1)
            x_parts_out(NONE)
            cw_store(None, NONE)
            max_rows(NONE, 0)

            def step(s, tau):
                n = s.next()
                more = not s.last()
                if tau == 0:
                    if more and not (isinstance(s.i, int) and s.i == PASSES - 1):
                        sp.wait_ge(xn_ready, s.at(TILES, TILES))
                        load_x(Stage(s.i + 1, s.p))
                if tau == 1 and more:
                    if not s.first():
                        sp.wait_ge(score_full, s.at(64, 0))
                    stack_in(n, 0)
                if more or tau < TILES - 1:
                    max_rows(s, tau + 1)
                if tau == 1 and more:
                    stack_in(n, 1)
                    x_parts_out(n)
                if tau == 1 and not s.first():
                    prev = bass.ds(s.i * (2 * TOK) + (s.p - 1) * TOK, TOK)
                    s_store(s, "sTp", prev)
                if tau == 3 and more:
                    cw_store(s, n)

            passes(sp, period(step))
            s_store(Stage(PASSES - 1, 1), "sT", slice(NTOK - TOK, NTOK))
            sp.wait_ge(s_out, 16 * BATCH)
            sp.wait_ge(cw_out, 16 * BATCH)
            sp.wait_ge(x_out, 32 * BATCH)

        @block.gpsimd
        def _(pool):
            def inverse_std(n):
                pool.wait_ge(ln_eps, n.at(1, 1))
                pool.tensor_tensor(rstd[:], vareps[:], neghalf[:, 0:TILES].unsqueeze(2), ALU.pow
                                   ).then_inc(ln_rstd, 1)

            def split3(s, n, side):
                pool.wait_ge(misc_free, misc_use(s, "qk"[side]) + 1)
                if s is not None:
                    pool.wait_ge(parts_out, n.at(96, 0))
                f, r, pt, base = full[side], rest[side], parts[side], 5 * side
                pool.tensor_tensor(pt[:, 0, :], f[:], zeros[:], ALU.add).then_inc(split, 1)
                pool.wait_ge(split, n.at(12, base + 1))
                pool.tensor_tensor(r[:], f[:], pt[:, 0, :], ALU.subtract).then_inc(split, 1)
                pool.wait_ge(split, n.at(12, base + 2))
                pool.tensor_tensor(pt[:, 1, :], r[:], zeros[:], ALU.add).then_inc(split, 1)
                pool.wait_ge(split, n.at(12, base + 3))
                pool.tensor_tensor(f[:], r[:], pt[:, 1, :], ALU.subtract).then_inc(split, 1)
                pool.wait_ge(split, n.at(12, base + 4))
                pool.tensor_tensor(pt[:, 2, :], f[:], zeros[:], ALU.add).then_inc(split, 1)

            def split_x(s, n):
                pool.wait_ge(misc_free, misc_use(s, "xnT") + 1)
                if s is not None:
                    pool.wait_ge(x_out, n.at(32, 0))
                pool.tensor_tensor(xh[:], xnT[:], zeros[:], ALU.add).then_inc(split, 1)
                pool.wait_ge(split, n.at(12, 11))
                pool.tensor_tensor(xl[:], xnT[:], xh[:], ALU.subtract).then_inc(split, 1)

            def values(s, n):
                pool.wait_ge(misc_free, misc_use(s, "V") + 1)
                if s is not None:
                    pool.wait_ge(pv_done, s.at(16, 0))
                pool.tensor_tensor(vst[n.p][:, :, :, 0:DH], vtmp[:],
                                   bv[:].unsqueeze(1).broadcast_to([P, TOK // GT, KT, DH]), ALU.add
                                   ).then_inc(v_ready, 1)

            def router_bias(s, n):
                pool.wait_ge(misc_free, misc_use(s, "logits") + 1)
                pool.tensor_tensor(biased[:], aff[:], ebias[:].unsqueeze(1).broadcast_to([P, TILES, E0]),
                                   ALU.add).then_inc(biased_done, 1)

            def router_sum(n):
                pool.wait_ge(esig_done, n.at(1, 1))
                pool.tensor_tensor(esum[:], esig[:], ones[:].unsqueeze(1).broadcast_to([P, TILES, E0]), ALU.add
                                   ).then_inc(pool_r, 1)
                pool.wait_ge(dve_r, n.at(5, 2))
                pool.tensor_tensor(wsel[:], sig[:], mask[:], ALU.mult).then_inc(pool_r, 1)

            def router_weights(s, n):
                pool.wait_ge(dve_r, n.at(5, 5))
                pool.tensor_tensor(cw[:], wsel[:], wrec[:].broadcast_to([P, TILES, E0]), ALU.mult
                                   ).then_inc(pool_r, 1)
                pool.wait_ge(pool_r, n.at(5, 3))
                pool.tensor_tensor(cwhl[:, :, 0, :], cw[:], zeros[:, 0:TILES * E0].rearrange(
                    "p (t e) -> p t e", t=TILES), ALU.add).then_inc(pool_r, 1)
                pool.wait_ge(pool_r, n.at(5, 4))
                pool.tensor_tensor(cwhl[:, :, 1, :], cw[:], cwhl[:, :, 0, :], ALU.subtract).then_inc(pool_r, 1)

            def context(s, tau):
                pool.wait_ge(den_done, s.at(TILES, tau + 1))
                pool.tensor_tensor(ctx_sb[:].rearrange("p (c j) -> p c j", c=CH), oT[:, :, 0:DH],
                                   rden[:].broadcast_to([P, CH, DH]), ALU.mult).then_inc(ctx_done, 1)
                pool.wait_ge(ctx_done, s.at(TILES, tau + 1))
                if tau == TILES - 1:
                    pool.wait_ge(kept, s.at(1, 1))
                row = xlast[:] if tau == TILES - 1 else xn[s.p][:, tau, :]
                pool.tensor_tensor(res[:], ctx_sb[:], row, ALU.add).then_inc(res_done, 1)

            def context_norm(s, tau):
                pool.wait_ge(c_eps, s.at(TILES, tau + 1))
                pool.tensor_tensor(crstd[:], cvareps[:], neghalf[:, 0:1], ALU.pow).then_inc(c_rstd, 1)

            build_selectors(pool, sel, sel_built)
            pool.wait_ge(w_in, 16 * W_LOADS)
            pool.wait_ge(init, 14)
            inverse_std(NONE)
            split3(None, NONE, 0)
            split3(None, NONE, 1)
            split_x(None, NONE)
            values(None, NONE)
            router_bias(None, NONE)
            router_sum(NONE)
            router_weights(None, NONE)

            def back(s):
                return Stage(s.i, 0) if s.p else Stage(s.i - 1, 1)

            def step(s, tau):
                n, more = s.next(), not s.last()
                if tau == 0 and more:
                    inverse_std(n)
                if not (s.first() and tau == 0):
                    before = (s, tau - 1) if tau else (back(s), TILES - 1)
                    context(*before)
                    context_norm(*before)
                if tau == TILES - 1:
                    pool.tensor_tensor(xlast[:], xn[s.p][:, tau, :], zeros[:, 0:D], ALU.add).then_inc(kept, 1)
                if not more:
                    return
                if tau == 0:
                    split3(s, n, 0)
                    split3(s, n, 1)
                    split_x(s, n)
                if tau == 1:
                    values(s, n)
                    router_bias(s, n)
                if tau == 2:
                    router_sum(n)
                    router_weights(s, n)

            passes(pool, period(step))
            context(Stage(PASSES - 1, 1), TILES - 1)
            context_norm(Stage(PASSES - 1, 1), TILES - 1)

        @block.scalar
        def _(act):
            def take(s, name, n):
                act.wait_ge(misc_full, misc_use(s, name) + 1)
                if name == "xnT":
                    if s is not None:
                        act.wait_ge(split, n.at(12, 0))
                    op = act.activation(xnT[:], misc[:], ACT.Copy)
                elif name in ("q", "k"):
                    side = "qk".index(name)
                    op = act.activation(full[side][:].rearrange("p (n t g) -> p n t g", t=GT, g=NG),
                                        misc[:].rearrange("p (n g t) -> p n t g", t=GT, g=NG),
                                        ACT.Identity, bias=(bq, bk)[side][:])
                elif name == "V":
                    if s is not None:
                        act.wait_ge(v_ready, n.at(1, 0))
                    op = act.activation(vtmp[:].rearrange("p g k j -> p (g k j)"), misc[:], ACT.Copy)
                elif name == "logits":
                    if s is not None:
                        act.wait_ge(biased_done, n.at(1, 0))
                        act.wait_ge(esig_done, n.at(1, 0))
                    op = act.activation(aff[:].rearrange("p t e -> p (t e)"), misc[:, :TILES * E0], ACT.Copy)
                elif name == "cwT":
                    if s is not None:
                        act.wait_ge(cw_out, n.at(16, 0))
                    op = act.activation(cwT[:], misch[:, :TOK], ACT.Copy)
                elif name[:2] == "cn":
                    t = int(name[2])
                    op = act.activation(cT[:, t * P:t * P + P], misc[:, :P], ACT.Copy)
                else:
                    if name == "sTp" and not (isinstance(s.i, int) and s.i == 0 and s.p == 1) or name == "sT":
                        done = s.at(16, -16) if name == "sTp" else s.at(16, 0)
                        act.wait_ge(s_out, done)
                    op = act.activation(sT[:], misc[:], ACT.Identity, bias=bf[:])
                op.then_inc(misc_free, 1)
                if name == "logits":
                    act.wait_ge(misc_free, misc_use(s, name) + 1)
                    if s is not None:
                        act.wait_ge(pool_r, n.at(5, 1 - 5))
                    act.activation(esig[:], aff[:], ACT.Exp, scale=-1.0).then_inc(esig_done, 1)

            def place_maxima(s, tau):
                where, at = (s if tau < TILES else s.next()), tau % TILES
                act.wait_ge(m_in, s.at(32 * TILES, 32 * tau + 32))
                for qt in range(4):
                    act.activation(stack[0][where.p][MROW:KROWS, at, qt * P:qt * P + P, :].rearrange(
                        "a (q t) g -> a q t g", q=4), mrow[MROW:KROWS, :, qt, :, :].rearrange("a q g t -> a q t g"),
                        ACT.Copy).then_inc(m_placed, 1)

            act.wait_ge(w_in, 16 * W_LOADS)
            for name in START[:-1]:
                take(None, name, NONE)
            take(None, "cwT", NONE)
            place_maxima(NONE, 0)

            def step(s, tau):
                for kt in range(KT):
                    if kt == 3 and not (s.last() and tau == TILES - 1):
                        place_maxima(s, tau + 1)
                    for g in range(NG):
                        act.wait_ge(score_full, s.at(64, 16 * tau + 4 * kt + g + 1))
                        if g == 0 and not (s.first() and 4 * tau + kt < 2):
                            act.wait_ge(pv_done, s.at(16, 4 * tau + kt - 1))
                        act.activation(probs[:, kt % 2, g, :], score[:, g % 2, :], ACT.Exp, scale=SCALE
                                       ).then_inc(exp_done, 1)
                    for name in slot(s, tau, kt):
                        take(s, name, s.next())

            passes(act, period(step))
            last = Stage(PASSES - 1, 1)
            take(last, "cn3", last)
            take(last, "sT", last)

        @block.tensor
        def _(pe):
            def use(s, name):
                v = misc_use(s, name)
                if not (isinstance(v, int) and v == 0):
                    pe.wait_ge(misc_free, v)

            def fill(s, name, n):
                use(s, name)
                if name == "xnT":
                    pe.wait_ge(xn_ready, n.at(TILES, TILES))
                    for t in range(TILES):
                        op = pe.transpose(misc[:, t * P:t * P + P], xn[n.p][:, t, :], ident[:])
                elif name in ("q", "k"):
                    if name == "q":
                        pe.wait_ge(misc_free, misc_use(s, "xnT") + 1)
                    if s is not None:
                        pe.wait_ge(split, n.at(12, 0))
                    op = pe.matmul(misc[:], (wq if name == "q" else wk)[:], xnT[:], start=True, stop=True)
                elif name == "V":
                    w = wv[:].rearrange("d (k c j) -> d c k j", c=4, j=DH)
                    for g in range(TOK // GT):
                        for cq in range(4):
                            op = pe.matmul(misc[GT * cq:GT * cq + GT, g * GT:g * GT + GT].rearrange(
                                "p (k j) -> p k j", k=KT), xnT[:, g * GT:g * GT + GT], w[:, cq],
                                start=True, stop=True, skip_group_check=True)
                elif name == "logits":
                    for t in range(TILES):
                        op = pe.matmul(misc[:, t * E0:t * E0 + E0], xnT[:, t * P:t * P + P], cent[:],
                                       start=True, stop=True)
                elif name == "cwT":
                    pe.wait_ge(pool_r, n.at(5, 5))
                    for t in range(TILES):
                        op = pe.transpose(misch[:, t * P:t * P + P],
                                          cwhl[:, t, :, :].rearrange("p a e -> p (a e)"), identh[:])
                elif name[:2] == "cn":
                    t = int(name[2])
                    back = -1 if name[-1] == "p" else t
                    pe.wait_ge(cn_done, s.at(TILES, back + 1))
                    op = pe.transpose(misc[:, :P], cn[:], ident[:])
                else:
                    pe.wait_ge(misc_free, misc_use(s, "cn3p" if name == "sTp" else "cn3") + 1)
                    op = pe.matmul(misc[:], wf[:], cT[:], start=True, stop=True)
                op.then_inc(misc_full, 1)

            def maxima(s, ahead, j):
                where = s if ahead < TILES else s.next()
                at = ahead % TILES
                if j == 0 and at == 0:
                    pe.wait_ge(qk_in[where.p], where.own(16 * SLOTS_OF_STACK, 16 * SLOTS_OF_STACK))
                if not (s.first() and 8 * ahead + j < 2):
                    pe.wait_ge(mx_done, s.at(32, 8 * ahead + j - 1))
                qt = j // 2
                for k in range(2):
                    g = 2 * (j % 2) + k
                    op = pe.matmul(mxps[:, j % 2, k, :], stack[0][where.p][0:ROWS, at, qt * P:qt * P + P, g],
                                   stack[1][where.p][0:ROWS, at, :, g], start=True, stop=True)
                op.then_inc(mx_full, 1)

            def scores(s, tau, kt, g):
                if kt == 0 and g == 0:
                    pe.wait_ge(m_placed, s.at(4 * TILES, 4 * tau + 4))
                if not (s.first() and 16 * tau + 4 * kt + g < 2):
                    pe.wait_ge(exp_done, s.at(64, 16 * tau + 4 * kt + g - 1))
                pe.matmul(score[:, g % 2, :], stack[1][s.p][0:KROWS, tau, kt * P:kt * P + P, g],
                          stack[0][s.p][0:KROWS, tau, :, g], start=True, stop=True
                          ).then_inc(score_full, 1)

            def weighted(s, tau, kt, half):
                pe.wait_ge(exp_done, s.at(64, 16 * tau + 4 * kt + 4))
                if kt == 0:
                    if tau == 0:
                        pe.wait_ge(v_ready, s.at(1, 1))
                    if not (s.first() and tau == 0):
                        pe.wait_ge(o_out, s.at(TILES, tau))
                for g in range(NG):
                    op = pe.matmul(ops[GT * g:GT * g + GT, :], vst[half][:, tau * NG + g, kt, :],
                                   probs[:, kt % 2, g, :], start=(kt == 0), stop=(kt == KT - 1),
                                   skip_group_check=True)
                op.then_inc(pv_done, 1)

            pe.wait_ge(consts_ready, 4)
            pe.wait_ge(w_in, 16 * W_LOADS)
            for name in START:
                fill(None, name, NONE)
            pe.wait_ge(init, 14)
            for j in range(8):
                maxima(NONE, 0, j)
            for j in range(4):
                maxima(NONE, 1, j)

            def step(s, tau):
                for kt in range(KT):
                    pairs = mx_pairs(s, tau, kt)
                    scores(s, tau, kt, 0)
                    if pairs:
                        maxima(s, *pairs[0])
                    scores(s, tau, kt, 1)
                    if kt:
                        weighted(s, tau, kt - 1, s.p)
                    elif tau:
                        weighted(s, tau - 1, KT - 1, s.p)
                    elif not s.first():
                        weighted(Stage(s.i, 0) if s.p else Stage(s.i - 1, 1), TILES - 1, KT - 1, 1 - s.p)
                    scores(s, tau, kt, 2)
                    if pairs:
                        maxima(s, *pairs[1])
                    scores(s, tau, kt, 3)
                    for name in slot(s, tau, kt):
                        fill(s, name, s.next())

            passes(pe, period(step))
            last = Stage(PASSES - 1, 1)
            weighted(last, TILES - 1, KT - 1, 1)
            fill(last, "cn3", last)
            fill(last, "sT", last)

        @block.vector
        def _(dve):
            def statistics(n):
                dve.wait_ge(x_in[n.p], n.own(16, 16))
                for t in range(TILES):
                    dve.bn_stats(stats[:, t, :], xin[n.p][:, t, :]).then_inc(ln_stats, 1)
                dve.wait_ge(ln_stats, n.at(TILES, TILES))
                if not (isinstance(n.i, int) and n.i == 0 and n.p == 0):
                    dve.wait_ge(xn_ready, n.at(TILES, 0))
                apart(dve)
                for t in range(TILES):
                    dve.bn_aggr(meanvar[:, t, :], stats[:, t, :]).then_inc(ln_aggr, 1)
                dve.wait_ge(ln_aggr, n.at(TILES, TILES))
                dve.tensor_scalar(vareps[:], meanvar[:, :, 1:2], LN_EPS, None, ALU.add).then_inc(ln_eps, 1)

            def normalise(n):
                dve.wait_ge(ln_rstd, n.at(1, 1))
                for t in range(TILES):
                    dve.tensor_scalar(xn[n.p][:, t, :], xin[n.p][:, t, :], meanvar[:, t, 0:1], rstd[:, t, :],
                                      ALU.subtract, ALU.mult).then_inc(xn_ready, 1)

            def context_norm(s, tau):
                dve.wait_ge(c_rstd, s.at(TILES, tau + 1))
                dve.tensor_scalar(cn[:], res[:], cmv[:, 0:1], crstd[:], ALU.subtract, ALU.mult
                                  ).then_inc(cn_done, 1)

            def maximum(s, ahead, j):
                dve.wait_ge(mx_full, s.at(32, 8 * ahead + j + 1))
                c = (j // 2) * 4 + 2 * (j % 2)
                dve.tensor_reduce(mx[ahead % 2][:, c:c + 2], mxps[:, j % 2, :, :], AX.X, ALU.max
                                  ).then_inc(mx_done, 1)

            def minus_maximum(s, ahead):
                m = mx[ahead % 2]
                dve.wait_ge(mx_done, s.at(32, 8 * ahead + 8))
                dve.tensor_scalar(mneg[:, 0, 0:16], m[:], -1.0, None, ALU.mult).then_inc(mneg_done, 1)
                dve.wait_ge(mneg_done, s.at(2 * TILES, 2 * ahead + 1))
                dve.scalar_tensor_tensor(mneg[:, 1, 0:16], m[:], -1.0, mneg[:, 0, 0:16], ALU.mult, ALU.subtract
                                         ).then_inc(mneg_done, 1)
                dve.wait_ge(mneg_done, s.at(2 * TILES, 2 * ahead + 2))
                if not (s.first() and ahead == 0):
                    dve.wait_ge(m_in, s.at(32 * TILES, 32 * ahead))
                dve.transpose(mT[:].rearrange("p a t -> p (a t)"), mneg[:].rearrange("p a t -> p (a t)")).then_inc(mT_done, 1)

            def context(s, tau):
                dve.wait_ge(pv_done, s.at(16, 4 * tau + 4))
                if not (s.first() and tau == 0):
                    dve.wait_ge(ctx_done, s.at(TILES, tau))
                dve.transpose(oT[:].rearrange("p c j -> p (c j)"), ops[:]).then_inc(o_out, 1)
                dve.wait_ge(o_out, s.at(TILES, tau + 1))
                dve.reciprocal(rden[:], oT[:, :, DH:DH + 1]).then_inc(den_done, 1)

            def context_stats(s, tau):
                dve.wait_ge(res_done, s.at(TILES, tau + 1))
                dve.bn_stats(cstats[:], res[:]).then_inc(c_stats, 1)
                dve.wait_ge(c_stats, s.at(TILES, tau + 1))
                if not (s.first() and tau == 0):
                    dve.wait_ge(cn_done, s.at(TILES, tau))
                apart(dve)
                dve.bn_aggr(cmv[:], cstats[:]).then_inc(c_aggr, 1)
                dve.wait_ge(c_aggr, s.at(TILES, tau + 1))
                dve.tensor_scalar(cvareps[:], cmv[:, 1:2], LN_EPS, None, ALU.add).then_inc(c_eps, 1)

            def choose(n):
                dve.wait_ge(biased_done, n.at(1, 1))
                if not (isinstance(n.i, int) and n.i == 0 and n.p == 0):
                    dve.wait_ge(pool_r, n.at(5, 0))
                apart(dve)
                for t in range(TILES):
                    dve.max(best[:, t, :], biased[:, t, :]).then_inc(best_done, 1)
                dve.wait_ge(best_done, n.at(TILES, TILES))
                apart(dve)
                for t in range(TILES):
                    dve.match_replace(dropped[:, t, :], best[:, t, :], biased[:, t, :], -3.0e38
                                      ).then_inc(drop_done, 1)
                dve.wait_ge(drop_done, n.at(TILES, TILES))
                dve.tensor_tensor(mask[:], dropped[:], biased[:], ALU.not_equal).then_inc(dve_r, 1)

            def sigmoid(n):
                dve.wait_ge(pool_r, n.at(5, 1))
                dve.reciprocal(sig[:], esum[:]).then_inc(dve_r, 1)

            def weights(n):
                dve.wait_ge(pool_r, n.at(5, 2))
                dve.tensor_reduce(wsum[:], wsel[:], AX.X, ALU.add).then_inc(dve_r, 1)
                dve.wait_ge(dve_r, n.at(5, 3))
                dve.tensor_scalar(wsume[:], wsum[:], 1e-8, None, ALU.add).then_inc(dve_r, 1)
                dve.wait_ge(dve_r, n.at(5, 4))
                dve.reciprocal(wrec[:], wsume[:]).then_inc(dve_r, 1)

            for p in range(2):
                for side in range(2):
                    dve.memset(stack[side][p][64:96], 0.0).then_inc(init, 1)
                dve.memset(stack[1][p][MROW:KROWS], 1.0).then_inc(init, 1)
                dve.memset(vst[p][:], 0.0).then_inc(init, 1)
            dve.memset(mneg[:], 0.0).then_inc(init, 1)
            dve.memset(neghalf[:], -0.5).then_inc(init, 1)
            dve.memset(zeros[:], 0.0).then_inc(init, 1)
            dve.memset(ones[:], 1.0).then_inc(init, 1)
            dve.wait_ge(init, 12)
            for p in range(2):
                dve.memset(vst[p][:, :, :, DH:DH + 1], 1.0).then_inc(init, 1)
            statistics(NONE)
            normalise(NONE)
            choose(NONE)
            sigmoid(NONE)
            weights(NONE)
            for j in range(8):
                maximum(NONE, 0, j)
            minus_maximum(NONE, 0)
            for j in range(4):
                maximum(NONE, 1, j)

            def step(s, tau):
                n, more = s.next(), not s.last()
                before = (s, tau - 1) if tau else (Stage(s.i, 0) if s.p else Stage(s.i - 1, 1), TILES - 1)
                for kt in range(KT):
                    if tau == 0 and kt == 0 and more:
                        statistics(n)
                    pairs = mx_pairs(s, tau, kt)
                    if pairs:
                        maximum(s, *pairs[0])
                    if kt == 0 and not (s.first() and tau == 0):
                        context(*before)
                    if tau == 0 and kt == 0 and more:
                        normalise(n)
                    if pairs:
                        maximum(s, *pairs[1])
                    if kt == 2 and not (s.first() and tau == 0):
                        context_norm(*before)
                    if kt == 1 and pairs:
                        minus_maximum(s, tau + 1)
                    if kt == 1 and not (s.first() and tau == 0):
                        context_stats(*before)
                    if more and tau == 2:
                        if kt == 0:
                            choose(n)
                        if kt == 1:
                            sigmoid(n)
                        if kt == 2:
                            weights(n)

            passes(dve, period(step))
            last = Stage(PASSES - 1, 1)
            context(last, TILES - 1)
            context_stats(last, TILES - 1)
            context_norm(last, TILES - 1)



UPC = (1, 4)
NQ = (UNITS + 1, UNITS)
SHARED = D // 2
RING = (6, 8)
LAG = 3
CHUNK = 8
JOBS = 2 * UNITS // CHUNK
YS = WS * WS

USES = (["prodT", "xnT", "logits", "f", "i", "z", "o", "rank", "cT", "cwT", "nT"], ["prodT"])
DVE_USES = ["prodT", "rank", "cT"]
ACT_USES = [u for u in USES[0] if u not in DVE_USES]
NBANKS = 3
PE_AT = {"prodT": 6, "xnT": 13, "logits": 14, "f": 15, "i": 16, "z": 17, "o": 18, "cT": 23, "rank": 24,
         "nT": 29, "cwT": 30}
ACT_AT = {"g": 2, "xnT": 13, "logits": 14, "f": 15, "i": 16, "z": 17, "o": 18, "share": 19, "nT": 29,
          "cwT": 30}
DVE_AT = {"prod": 3, "xadd": 6, "stats": 7, "norm": 10, "top0": 15, "lin_f": 16, "lin_i": 17, "top1": 18,
          "lin_o": 19, "scan": 20, "share": 21, "count": 22, "cstats": 23, "cnorm": 26, "cut": 27}
USES = (sorted(USES[0], key=lambda u: (PE_AT[u], USES[0].index(u))), USES[1])
DVE_USES = [u for u in USES[0] if u in DVE_USES]
ACT_USES = [u for u in USES[0] if u in ACT_USES]
POOL_AT = {"rstd": 8, "split": 14, "iz": 18, "crstd": 24, "s1": 30}
PER = {"unit": NQ, "c": (UNITS // UPC[0], UNITS // UPC[1]), "once": (1, 1), "prep": (1, 0),
       "st_in": (48, 48), "ep_in": (32, 32), "m_full": (len(USES[0]), 1), "x_out": (16, 16),
       "act_rel": (len(ACT_USES), 0), "dve_rel": (len(DVE_USES), 1), "dma": (16, 0), "parts": (32, 0),
       "tiles": (TILES, 0), "two": (2, 0), "three": (3, 0)}


class Turn(Stage):

    def __init__(self, layer, i, p):
        Stage.__init__(self, i, p)
        self.layer = layer

    def n(self, counter, k):
        return self.layer * BATCH * PER[counter][0] + self.at(PER[counter][self.layer], k)

    def half(self, counter, k):
        return self.layer * PASSES * PER[counter][0] + self.own(PER[counter][self.layer], k)

    def first(self):
        return self.layer == 0 and Stage.first(self)

    def back(self):
        if self.p:
            return Turn(self.layer, self.i, 0)
        if self.layer and isinstance(self.i, int) and self.i == 0:
            return Turn(0, PASSES - 1, 1)
        return Turn(self.layer, self.i - 1, 1)

    def after_next(self):
        if isinstance(self.i, int) and self.i == PASSES - 1:
            return Turn(1, 0, self.p) if self.layer == 0 else None
        return Turn(self.layer, self.i + 1, self.p)

    def place(self, q):
        return self.p * NQ[self.layer] + q

    def tiles(self):
        return bass.ds(self.i * (2 * TILES) + self.p * TILES, TILES)


def rows(q):
    return P if q < UNITS else SHARED


def steps_at(table, q):
    return [k for k, v in table.items() if v == q]


def run_stages(eng, unit, follow):
    for layer in range(2):
        def body(i):
            for p in range(2):
                s = Turn(layer, i, p)
                for q in range(NQ[layer]):
                    if unit:
                        unit(s, q)
                    if not s.first() and follow:
                        follow(s.back(), q)
        passes(eng, body)


def build_selectors(pool, sel, built):
    for layer in range(2):
        pool.memset(sel[layer][:], 0.0).then_inc(built, 1)
        for k, half in enumerate((0, (E0, E1)[layer])):
            pool.wait_ge(built, 3 * layer + 1 + k)
            pattern = [[-1, UNITS // UPC[1]], [0, P]] if layer else [[-2, UNITS], [-1, 2], [0, P // 2]]
            v = sel[layer][:] if layer else sel[layer][:].rearrange("r n (a m) -> r n a m", a=2)
            pool.affine_select(out=v, in_=v, compare_op=ALU.not_equal, fill=WS, base=-half,
                               pattern=pattern, channel_multiplier=1).then_inc(built, 1)


def mixture_phase(nc, io, scratch, ident, identh, sel):
    with ExitStack() as ctx:
        def sb(name, shape, dt=F32):
            return ctx.enter_context(nc.sbuf_tensor("m_" + name, shape, dt))

        def sem(name):
            return ctx.enter_context(nc.semaphore("m_" + name))

        wuh, wul, wdh, wdl = ([sb(f"{n}{k}", [P, NQ[k], P], F16) for k in range(2)]
                              for n in ("wuh", "wul", "wdh", "wdl"))
        raw = [sb(f"raw{k}", [P, CHUNK, P]) for k in range(2)]
        raw_up, raw_down = sb("raw_up", [P, SHARED]), sb("raw_down", [SHARED, P])
        liftid = sb("liftid", [P, P], F16)
        xh = [sb(f"xh{p}", [P, TOK], F16) for p in range(2)]
        xl = [sb(f"xl{p}", [P, TOK], F16) for p in range(2)]
        cw = [sb(f"cw{p}", [P, TOK], F16) for p in range(2)]
        sT = [sb(f"sT{p}", [P, TOK]) for p in range(2)]
        xres = [sb(f"xres{p}", [P, TILES, D]) for p in range(2)]
        silu = sb("silu", [P, 2, TOK])
        hid = sb("hid", [P, 2, TOK])
        hidh, hidl = sb("hidh", [P, max(RING), TOK], F16), sb("hidl", [P, max(RING), TOK], F16)
        gT, prod = sb("gT", [P, TOK]), sb("prod", [P, TOK])
        xnew = sb("xnew", [P, TILES, D])
        wg, bg, bgh = sb("wg", [P, 4, D]), sb("bg", [P, 4]), sb("bgh", [P, 4])
        lnw, lnb, rw = sb("lnw", [P, 1]), sb("lnb", [P, 1]), sb("rw", [P, E1])
        zeros, neghalf = sb("zeros", [P, TOK]), sb("neghalf", [P, TILES, 1])
        stats, mv = sb("stats", [P, TILES, 6]), sb("mv", [P, TILES, 2])
        cstats, cmv = sb("cstats", [P, TILES, 6]), sb("cmv", [P, TILES, 2])
        vareps, rstd, cvareps, crstd = (sb(n, [P, TILES, 1]) for n in ("vareps", "rstd", "cvareps", "crstd"))
        xn, xnT = sb("xn", [P, TILES, D]), sb("xnT", [P, TOK])
        oh, ol = sb("oh", [P, TOK], F16), sb("ol", [P, TOK], F16)
        tg = {g: sb("tanh_" + g, [P, TOK]) for g in "fizo"}
        gl = {g: sb("gate_" + g, [P, TOK]) for g in "fio"}
        iz, cell, hT, s1 = (sb(n, [P, TOK]) for n in ("iz", "cell", "hT", "s1"))
        cn = sb("cn", [P, TILES, D])
        grid = [P, TILES, E1]
        lg, others = sb("lg", grid), sb("others", grid)
        priority = sb("priority", [P, 1, E1])
        best, prior = ([sb(f"{n}{k}", [P, TILES, 1]) for k in range(K1)] for n in ("best", "prior"))
        equal, rated, chosen, weighed = ([sb(f"{n}{k}", grid) for k in range(K1)]
                                         for n in ("equal", "rated", "chosen", "weighed"))
        share = [sb(f"share{k}", [P, TILES, 1]) for k in range(K1)]
        gap, tgap = sb("gap", [P, TILES, 1]), sb("tgap", [P, TILES, 1])
        cwall, cwcut = sb("cwall", grid), sb("cwcut", grid)
        selh = sb("selh", grid, BF16)
        taken = sb("taken", [P, TILES + 1, E1], BF16)
        ones, earlier = sb("ones", [P, P], BF16), sb("earlier", [P, P], BF16)
        cwhl = sb("cwhl", [P, TILES, 2, E1], F16)
        cwT = sb("cwT", [2 * E1, TOK], F16)

        hps = ctx.enter_context(nc.psum_tensor("m_h", [P, 2, 512], F32))
        cps = ctx.enter_context(nc.psum_tensor("m_c", [P, 2, 512], F32))
        yps = ctx.enter_context(nc.psum_tensor("m_y", [P, 512], F32))
        mps = ctx.enter_context(nc.psum_tensor("m_m", [P, NBANKS, 512], F32))

        w_in, raw_in, shared_in = sem("w_in"), [sem(f"raw_in{k}") for k in range(2)], sem("shared_in")
        cst, dcst = sem("cst"), sem("dcst")
        wsplit = sem("wsplit")
        st_in = [sem(f"st_in{p}") for p in range(2)]
        ep_in = [sem(f"ep_in{p}") for p in range(2)]
        up_done, c_done, dn_done = sem("up_done"), sem("c_done"), sem("dn_done")
        silu_done, mul_done, hi_done, lo_done = (sem(n + "_done") for n in ("silu", "mul", "hi", "lo"))
        g_done, prod_done, x_out = sem("g_done"), sem("prod_done"), sem("x_out")
        m_full = sem("m_full")
        act_rel, dve_rel = sem("act_rel"), sem("dve_rel")
        ln_stats, ln_aggr, ln_eps, ln_rstd = (sem("ln_" + n) for n in ("stats", "aggr", "eps", "rstd"))
        xn_ready, split, parts_out = sem("xn_ready"), sem("split"), sem("parts_out")
        gate_lin, iz_done, scan_done = sem("gate_lin"), sem("iz_done"), sem("scan_done")
        c_stats, c_aggr, c_eps, c_rstd = (sem("c_" + n) for n in ("stats", "aggr", "eps", "rstd"))
        bias_done, s_done, s_out = sem("bias_done"), sem("s_done"), sem("s_out")
        top, tgap_done, shared_out, counting, cut = (sem(n) for n in ("top", "tgap", "shares", "counting", "cut"))
        cw_out = sem("cw_out")

        W_LOADS = 5
        TOPS = 6 + 5 + 1
        SHARES = 2 + 2 + 2
        COUNTS = 1 + TILES
        PER.update(top=(TOPS, 0), shares=(SHARES, 0), counting=(COUNTS, 0))

        def bank(b, name):
            return mps[:, USES[b.layer].index(name) % NBANKS, :]

        JOB_AT = {(0, 0, 0, 1): 2, (0, 0, 0, 3): 3, (0, 0, 0, 8): 4, (0, 0, 0, 10): 5, (0, 0, 0, 16): 6,
                  (0, 0, 0, 18): 7, (0, 0, 0, 24): 8}
        for j in range(JOBS):
            JOB_AT[(0, PASSES - 1, j // 4, (1, 5, 12, 24)[j % 4])] = JOBS + 1 + j

        def job_at(s, q):
            return JOB_AT.get((s.layer, s.i, s.p, q)) if isinstance(s.i, int) else None

        def chunk(j):
            layer = int(j > JOBS)
            k = j - layer * (JOBS + 1)
            return layer, k % 2, slice(k // 2 * CHUNK, k // 2 * CHUNK + CHUNK), k % 2

        block = ctx.enter_context(nc.Block())

        @block.sync
        def _(sp):
            def load(s):
                n = s.layer
                if n:
                    before = Turn(0, s.i, s.p)
                    sp.wait_ge(parts_out, before.n("parts", 32))
                    apart(sp)
                    sp.wait_ge(cw_out, before.n("dma", 16))
                    apart(sp)
                sp.dma_start(xh[s.p][:], scratch[f"xh{n}"][:, s.tokens()]).then_inc(st_in[s.p], 16)
                sp.dma_start(xl[s.p][:], scratch[f"xl{n}"][:, s.tokens()]).then_inc(st_in[s.p], 16)
                r = slice(0, 2 * (E0, E1)[n])
                sp.dma_start(cw[s.p][r], scratch[f"cw{n}"][:, s.tokens()]).then_inc(st_in[s.p], 16)

            def load_ep(s):
                n = s.layer
                if n:
                    before = Turn(0, s.i, s.p)
                    sp.wait_ge(s_out, before.n("dma", 16))
                    apart(sp)
                    sp.wait_ge(x_out, before.n("x_out", 16))
                    apart(sp)
                sp.dma_start(sT[s.p][:], scratch[f"s{n}"][:, s.tokens()]).then_inc(ep_in[s.p], 16)
                x_t = (scratch["x1"] if n else io["x"]).rearrange("(n p) d -> p n d", p=P)
                sp.dma_start(xres[s.p][:], x_t[:, s.tiles(), :]).then_inc(ep_in[s.p], 16)

            def load_chunk(j):
                layer, side, units, k = chunk(j)
                src = io[("up", "down")[side] + str(layer)]
                sp.dma_start(raw[k][:], src[:, units, :]).then_inc(raw_in[k], 16)

            load_chunk(0)
            load(Turn(0, 0, 0))
            load_chunk(1)
            for dst, src in ((wg, "wg"), (bg, "bg"), (lnw, "lnw"), (lnb, "lnb"), (rw, "rw")):
                sp.dma_start(dst[:], io[src]).then_inc(w_in, 16)
            sp.dma_start(raw_up[:], io["ups"]).then_inc(shared_in, 16)
            sp.dma_start(raw_down[:], io["downs"]).then_inc(shared_in, 16)
            for j in range(2, JOBS):
                sp.wait_ge(wsplit, 2 * (j - 1))
                load_chunk(j)
                if j == 3:
                    load(Turn(0, 0, 1))
            load_ep(Turn(0, 0, 0))
            load_ep(Turn(0, 0, 1))
            for k in range(2):
                sp.wait_ge(wsplit, 2 * (JOBS - 1 + k))
                load_chunk(JOBS + 1 + k)

            def unit(s, q):
                j = job_at(s, q)
                if j is not None and JOBS < j <= 2 * JOBS - 2:
                    sp.wait_ge(wsplit, 2 * j + 4)
                    load_chunk(j + 2)

            def follow(b, q):
                nxt = b.after_next()
                if q == 0 and nxt:
                    sp.wait_ge(up_done, b.n("unit", NQ[b.layer]))
                    apart(sp)
                    sp.wait_ge(c_done, b.n("c", PER["c"][b.layer]))
                    apart(sp)
                    load(nxt)
                if q == 7:
                    sp.wait_ge(dve_rel, b.n("dve_rel", 1))
                    apart(sp)
                    out_t = (io["out"] if b.layer else scratch["x1"]).rearrange("(n p) d -> p n d", p=P)
                    sp.dma_start(out_t[:, b.tiles(), :], xnew[:]).then_inc(x_out, 16)
                    if nxt:
                        load_ep(nxt)
                if b.layer:
                    return
                if q == 16:
                    sp.wait_ge(split, b.n("two", 2))
                    apart(sp)
                    sp.dma_start(scratch["xh1"][:, b.tokens()], oh[:]).then_inc(parts_out, 16)
                    sp.dma_start(scratch["xl1"][:, b.tokens()], ol[:]).then_inc(parts_out, 16)
                if q == 31:
                    sp.wait_ge(act_rel, b.n("act_rel", ACT_USES.index("cwT") + 1))
                    apart(sp)
                    sp.dma_start(scratch["cw1"][:, b.tokens()], cwT[:]).then_inc(cw_out, 16)
                if q == 31:
                    sp.wait_ge(s_done, b.n("prep", 1))
                    apart(sp)
                    sp.dma_start(scratch["s1"][:, b.tokens()], s1[:]).then_inc(s_out, 16)

            run_stages(sp, unit, follow)
            for q in range(UNITS):
                follow(Turn(1, PASSES - 1, 1), q)
            sp.wait_ge(x_out, 2 * 16 * BATCH)
            sp.wait_ge(parts_out, 32 * BATCH)
            sp.wait_ge(cw_out, 16 * BATCH)
            sp.wait_ge(s_out, 16 * BATCH)

        @block.gpsimd
        def _(pool):
            pool.memset(ones[:], 1.0).then_inc(cst, 1)
            pool.memset(earlier[:], 1.0).then_inc(cst, 1)
            pool.memset(liftid[:], 0.0).then_inc(cst, 1)
            pool.wait_ge(cst, 3)
            pool.affine_select(out=earlier[:], in_=earlier[:], compare_op=ALU.is_ge, fill=0.0, base=-1,
                               pattern=[[1, P]], channel_multiplier=-1).then_inc(cst, 1)
            pool.affine_select(out=liftid[:], in_=liftid[:], compare_op=ALU.not_equal, fill=YS, base=0,
                               pattern=[[-1, P]], channel_multiplier=1).then_inc(cst, 1)

            def unit(s, q):
                k, r, r0 = s.place(q), RING[s.layer], rows(q)
                pool.wait_ge(hi_done, s.n("unit", q + 1))
                if not (s.first() and q < min(RING)):
                    pool.wait_ge(dn_done, s.n("unit", q - min(RING) + 1))
                pool.tensor_tensor(hidl[0:r0, k % r, :], hid[0:r0, k % 2, :], hidh[0:r0, k % r, :],
                                   ALU.subtract).then_inc(lo_done, 1)

            def follow(b, q):
                if b.layer:
                    return
                for name in steps_at(POOL_AT, q):
                    if name == "rstd":
                        pool.wait_ge(ln_eps, b.n("prep", 1))
                        pool.tensor_tensor(rstd[:], vareps[:], neghalf[:], ALU.pow).then_inc(ln_rstd, 1)
                    elif name == "split":
                        pool.wait_ge(act_rel, b.n("act_rel", ACT_USES.index("xnT") + 1))
                        if not b.first():
                            pool.wait_ge(parts_out, b.n("parts", 0))
                        pool.tensor_tensor(oh[:], xnT[:], zeros[:], ALU.add).then_inc(split, 1)
                        pool.wait_ge(split, b.n("two", 1))
                        pool.tensor_tensor(ol[:], xnT[:], oh[:], ALU.subtract).then_inc(split, 1)
                    elif name == "iz":
                        pool.wait_ge(gate_lin, b.n("three", 2))
                        pool.wait_ge(act_rel, b.n("act_rel", ACT_USES.index("z") + 1))
                        if not b.first():
                            pool.wait_ge(scan_done, b.n("prep", 0))
                        pool.tensor_tensor(iz[:], gl["i"][:], tg["z"][:], ALU.mult).then_inc(iz_done, 1)
                    elif name == "crstd":
                        pool.wait_ge(c_eps, b.n("prep", 1))
                        pool.tensor_tensor(crstd[:], cvareps[:], neghalf[:], ALU.pow).then_inc(c_rstd, 1)
                    elif name == "s1":
                        pool.wait_ge(act_rel, b.n("act_rel", ACT_USES.index("nT") + 1))
                        pool.wait_ge(gate_lin, b.n("three", 3))
                        if not b.first():
                            pool.wait_ge(s_out, b.n("dma", 0))
                        pool.tensor_tensor(s1[:], gl["o"][:], hT[:], ALU.mult).then_inc(s_done, 1)

            pool.wait_ge(dcst, 3 + E1)
            run_stages(pool, unit, follow)

        @block.scalar
        def _(act):
            def unit(s, q):
                k = s.place(q) % 2
                act.wait_ge(up_done, s.n("unit", q + 1))
                if not (s.first() and q < 2):
                    act.wait_ge(mul_done, s.n("unit", q - 1))
                act.activation(silu[0:rows(q), k, :], hps[0:rows(q), k, :], ACT.Silu, scale=1.0 / WS
                               ).then_inc(silu_done, 1)

            def follow(b, q):
                for name in steps_at(ACT_AT, q):
                    if name == "g":
                        act.wait_ge(dn_done, b.n("unit", NQ[b.layer]))
                        if not b.first():
                            act.wait_ge(prod_done, b.n("once", 0))
                        act.activation(gT[:], yps[:], ACT.Silu, scale=1.0 / YS).then_inc(g_done, 1)
                        continue
                    if b.layer:
                        continue
                    if name == "share":
                        act.wait_ge(top, b.n("top", TOPS))
                        if not b.first():
                            act.wait_ge(shared_out, b.n("shares", 0))
                        act.activation(tgap[:], gap[:], ACT.Tanh, scale=0.5).then_inc(tgap_done, 1)
                        continue
                    act.wait_ge(m_full, b.n("m_full", USES[0].index(name) + 1))
                    src = bank(b, name)
                    if name == "xnT":
                        if not b.first():
                            act.wait_ge(split, b.n("two", 0))
                        act.activation(xnT[:], src, ACT.Copy).then_inc(act_rel, 1)
                    elif name == "logits":
                        if not b.first():
                            act.wait_ge(top, b.n("top", 0))
                        act.activation(lg[:].rearrange("p t e -> p (t e)"), src[:, 0:TILES * E1], ACT.Copy
                                       ).then_inc(act_rel, 1)
                    elif name in "fizo":
                        w = "fioz".index(name)
                        if not b.first():
                            if name == "z":
                                act.wait_ge(iz_done, b.n("prep", 0))
                            else:
                                act.wait_ge(gate_lin, b.n("three", 0))
                        act.activation(tg[name][:], src, ACT.Tanh, scale=1.0 if name == "z" else 0.5,
                                       bias=bgh[:, w:w + 1]).then_inc(act_rel, 1)
                    elif name == "cwT":
                        if not b.first():
                            act.wait_ge(cw_out, b.n("dma", 0))
                        act.activation(cwT[:], src.bitcast(F16)[0:2 * E1, 0:TOK], ACT.Copy).then_inc(act_rel, 1)
                    elif name == "nT":
                        if not b.first():
                            act.wait_ge(s_done, b.n("prep", 0))
                        act.activation(hT[:], src, ACT.Tanh, scale=lnw[:], bias=lnb[:]).then_inc(act_rel, 1)

            act.wait_ge(w_in, 16 * W_LOADS)
            act.activation(bgh[:, 0:3], bg[:, 0:3], ACT.Copy, scale=0.5).then_inc(bias_done, 1)
            act.activation(bgh[:, 3:4], bg[:, 3:4], ACT.Copy).then_inc(bias_done, 1)
            act.wait_ge(bias_done, 2)
            run_stages(act, unit, follow)
            follow(Turn(1, PASSES - 1, 1), ACT_AT["g"])

        @block.tensor
        def _(pe):
            def down(s, q):
                n, r, r0 = s.layer, s.place(q) % RING[s.layer], rows(q)
                pe.wait_ge(lo_done, s.n("unit", q + 1))
                if s.first() and q < UNITS and q % CHUNK == 0:
                    pe.wait_ge(wsplit, 4 * (q // CHUNK) + 4)
                if s.first() and q == UNITS:
                    pe.wait_ge(wsplit, 2 * JOBS + 4)
                if q == 0 and not s.first():
                    pe.wait_ge(g_done, s.n("once", 0))
                if q == 0 and n:
                    pe.matmul(yps[:], liftid[:], xh[s.p][:], start=True, stop=False)
                    pe.matmul(yps[:], liftid[:], xl[s.p][:], start=False, stop=False)
                pe.matmul(yps[:], wdh[n][0:r0, q, :], hidh[0:r0, r, :], start=(q == 0 and not n), stop=False)
                pe.matmul(yps[:], wdl[n][0:r0, q, :], hidh[0:r0, r, :], start=False, stop=False)
                pe.matmul(yps[:], wdh[n][0:r0, q, :], hidl[0:r0, r, :], start=False, stop=(q == NQ[n] - 1)
                          ).then_inc(dn_done, 1)

            def unit(s, q):
                n, k = s.layer, s.place(q) % 2
                if q == 0:
                    pe.wait_ge(st_in[s.p], s.half("st_in", 48))
                    if n and isinstance(s.i, int) and s.i == 0 and s.p == 0:
                        pe.wait_ge(wsplit, 2 * (2 * JOBS + 1) + 2)
                if s.first() and q < UNITS and q % CHUNK == 0:
                    pe.wait_ge(wsplit, 4 * (q // CHUNK) + 2)
                if s.first() and q == UNITS:
                    pe.wait_ge(wsplit, 2 * JOBS + 4)
                if q < UNITS and q % UPC[n] == 0:
                    c = q // UPC[n]
                    if not (s.first() and c < 2):
                        ago = (c - 1) * UPC[n] - (NQ[n] - UNITS if c < 2 else 0)
                        if n and c < 2 and isinstance(s.i, int) and s.i == 0 and s.p == 0:
                            ago = -1
                        pe.wait_ge(mul_done, s.n("unit", ago))
                    r = slice(0, 2 * (E0, E1)[n])
                    pe.matmul(cps[:, c % 2, :], sel[n][:, c, :], cw[s.p][r], start=True, stop=True
                              ).then_inc(c_done, 1)
                if not (s.first() and q < 2):
                    pe.wait_ge(silu_done, s.n("unit", q - 1))
                dst, high, low = hps[0:rows(q), k, :], wuh[n][:, q, 0:rows(q)], wul[n][:, q, 0:rows(q)]
                pe.matmul(dst, high, xh[s.p][:], start=True, stop=False)
                pe.matmul(dst, high, xl[s.p][:], start=False, stop=False)
                pe.matmul(dst, low, xh[s.p][:], start=False, stop=True).then_inc(up_done, 1)
                if q >= LAG:
                    down(s, q - LAG)
                elif not s.first():
                    b = s.back()
                    down(b, NQ[b.layer] - LAG + q)

            def bank_free(b, name):
                if b.layer:
                    if isinstance(b.i, int) and b.i == 0 and b.p == 0:
                        pe.wait_ge(act_rel, BATCH * len(ACT_USES))
                    pe.wait_ge(dve_rel, b.n("dve_rel", 0))
                    return
                order = USES[0]
                k = order.index(name)
                same = [j for j in range(len(order)) if j % NBANKS == k % NBANKS]
                prev = k < NBANKS
                old = order[same[-1] if prev else k - NBANKS]
                if prev and b.first():
                    return
                if old in ACT_USES:
                    pe.wait_ge(act_rel, b.n("act_rel", ACT_USES.index(old) + 1 - prev * len(ACT_USES)))
                else:
                    pe.wait_ge(dve_rel, b.n("dve_rel", DVE_USES.index(old) + 1 - prev * len(DVE_USES)))

            def follow(b, q):
                for name in [u for u in USES[b.layer] if PE_AT[u] == q]:
                    dst = bank(b, name)
                    bank_free(b, name)
                    if name == "prodT":
                        pe.wait_ge(prod_done, b.n("once", 1))
                        for t in range(TILES):
                            op = pe.transpose(dst[:, t * P:t * P + P], prod[:, t * P:t * P + P], ident[:])
                    elif name == "xnT":
                        pe.wait_ge(xn_ready, b.n("tiles", TILES))
                        for t in range(TILES):
                            op = pe.transpose(dst[:, t * P:t * P + P], xn[:, t, :], ident[:])
                    elif name == "logits":
                        pe.wait_ge(act_rel, b.n("act_rel", ACT_USES.index("xnT") + 1))
                        for t in range(TILES):
                            op = pe.matmul(dst[:, t * E1:t * E1 + E1], xnT[:, t * P:t * P + P], rw[:],
                                           start=True, stop=True)
                    elif name in "fizo":
                        op = pe.matmul(dst, wg[:, "fioz".index(name), :], xnT[:], start=True, stop=True)
                    elif name == "rank":
                        pe.wait_ge(counting, b.n("counting", COUNTS))
                        pe.matmul(dst[:, 0:TILES * E1], earlier[:], selh[:].rearrange("p t e -> p (t e)"),
                                  start=True, stop=False)
                        op = pe.matmul(dst[:, 0:TILES * E1], ones[:],
                                       taken[:, 0:TILES, :].rearrange("p t e -> p (t e)"), start=False, stop=True)
                    elif name == "cT":
                        pe.wait_ge(scan_done, b.n("prep", 1))
                        for t in range(TILES):
                            op = pe.transpose(dst[:, t * P:t * P + P], cell[:, t * P:t * P + P], ident[:])
                    elif name == "cwT":
                        pe.wait_ge(cut, b.n("two", 2))
                        half = dst.bitcast(F16)[0:2 * E1]
                        for t in range(TILES):
                            op = pe.transpose(half[:, t * P:t * P + P],
                                              cwhl[:, t].rearrange("p a e -> p (a e)"), identh[:])
                    elif name == "nT":
                        pe.wait_ge(dve_rel, b.n("dve_rel", DVE_USES.index("cT") + 1))
                        for t in range(TILES):
                            op = pe.transpose(dst[:, t * P:t * P + P], cn[:, t, :], ident[:])
                    op.then_inc(m_full, 1)

            pe.wait_ge(cst, 5)
            pe.wait_ge(w_in, 16 * W_LOADS)
            run_stages(pe, unit, follow)
            last = Turn(1, PASSES - 1, 1)
            for k in range(LAG):
                down(last, NQ[1] - LAG + k)
            follow(last, PE_AT["prodT"])

        @block.vector
        def _(dve):
            def lift(j, side, layer, src, cut_):
                high, low = ((wuh, wul), (wdh, wdl))[side]
                dve.tensor_scalar(high[layer][cut_], src[:], WS, None, ALU.mult).then_inc(wsplit, 1)
                dve.wait_ge(wsplit, 2 * j + 1)
                dve.scalar_tensor_tensor(low[layer][cut_], src[:], WS, high[layer][cut_], ALU.mult, ALU.subtract
                                         ).then_inc(wsplit, 1)

            def do_job(j):
                if j == JOBS:
                    dve.wait_ge(shared_in, 32)
                    lift(j, 0, 0, raw_up, (slice(None), UNITS, slice(0, SHARED)))
                    lift(j + 1, 1, 0, raw_down, (slice(0, SHARED), UNITS, slice(None)))
                    return
                layer, side, units, k = chunk(j)
                order = (j - layer) // 2 + 1
                dve.wait_ge(raw_in[k], 16 * order)
                lift(j + layer, side, layer, raw[k], (slice(None), units, slice(None)))

            def unit(s, q):
                k, r, r0 = s.place(q), RING[s.layer], rows(q)
                dve.wait_ge(silu_done, s.n("unit", q + 1))
                if q < UNITS and q % UPC[s.layer] == 0:
                    dve.wait_ge(c_done, s.n("c", q // UPC[s.layer] + 1))
                if not (s.first() and q < 2):
                    dve.wait_ge(lo_done, s.n("unit", q - 1))
                if q < UNITS:
                    dve.tensor_tensor(hid[:, k % 2, :], silu[:, k % 2, :], cps[:, (q // UPC[s.layer]) % 2, :],
                                      ALU.mult).then_inc(mul_done, 1)
                else:
                    dve.tensor_scalar(hid[0:r0, k % 2, :], silu[0:r0, k % 2, :], WS, None, ALU.mult
                                      ).then_inc(mul_done, 1)
                dve.wait_ge(mul_done, s.n("unit", q + 1))
                if not (s.first() and q < min(RING)):
                    dve.wait_ge(dn_done, s.n("unit", q - min(RING) + 1))
                dve.tensor_scalar(hidh[0:r0, k % r, :], hid[0:r0, k % 2, :], 1.0, None, ALU.mult
                                  ).then_inc(hi_done, 1)
                j = job_at(s, q)
                if j is not None:
                    do_job(j)

            def wide(t):
                return t[:].broadcast_to(grid)

            def follow(b, q):
                for name in steps_at(DVE_AT, q):
                    if name == "prod":
                        dve.wait_ge(g_done, b.n("once", 1))
                        dve.wait_ge(ep_in[b.p], b.half("ep_in", 32))
                        if not b.first():
                            dve.wait_ge(m_full, b.n("m_full", 1 - PER["m_full"][b.layer]))
                        dve.tensor_tensor(prod[:], gT[:], sT[b.p][:], ALU.mult).then_inc(prod_done, 1)
                    elif name == "xadd":
                        dve.wait_ge(m_full, b.n("m_full", 1))
                        if not b.first():
                            dve.wait_ge(x_out, b.n("x_out", 0))
                        dve.tensor_tensor(xnew[:].rearrange("p t d -> p (t d)"),
                                          xres[b.p][:].rearrange("p t d -> p (t d)"), bank(b, "prodT"), ALU.add
                                          ).then_inc(dve_rel, 1)
                    elif b.layer:
                        continue
                    elif name == "stats":
                        dve.wait_ge(dve_rel, b.n("dve_rel", 1))
                        if not b.first():
                            dve.wait_ge(ln_rstd, b.n("prep", 0))
                        apart(dve)
                        for t in range(TILES):
                            dve.bn_stats(stats[:, t, :], xnew[:, t, :]).then_inc(ln_stats, 1)
                        dve.wait_ge(ln_stats, b.n("tiles", TILES))
                        apart(dve)
                        for t in range(TILES):
                            dve.bn_aggr(mv[:, t, :], stats[:, t, :]).then_inc(ln_aggr, 1)
                        dve.wait_ge(ln_aggr, b.n("tiles", TILES))
                        dve.tensor_scalar(vareps[:], mv[:, :, 1:2], LN_EPS, None, ALU.add).then_inc(ln_eps, 1)
                    elif name == "norm":
                        dve.wait_ge(ln_rstd, b.n("prep", 1))
                        if not b.first():
                            dve.wait_ge(m_full, b.n("m_full", 2 - len(USES[0])))
                        for t in range(TILES):
                            dve.tensor_scalar(xn[:, t, :], xnew[:, t, :], mv[:, t, 0:1], rstd[:, t, :],
                                              ALU.subtract, ALU.mult).then_inc(xn_ready, 1)
                    elif name in ("lin_f", "lin_i", "lin_o"):
                        g = name[-1]
                        dve.wait_ge(act_rel, b.n("act_rel", ACT_USES.index(g) + 1))
                        if g == "o" and not b.first():
                            dve.wait_ge(s_done, b.n("prep", 0))
                        if g == "i" and not b.first():
                            dve.wait_ge(iz_done, b.n("prep", 0))
                        dve.tensor_scalar(gl[g][:], tg[g][:], 0.5, 0.5, ALU.mult, ALU.add).then_inc(gate_lin, 1)
                    elif name == "scan":
                        dve.wait_ge(iz_done, b.n("prep", 1))
                        if not b.first():
                            dve.wait_ge(m_full, b.n("m_full", USES[0].index("cT") + 1 - len(USES[0])))
                        dve.tensor_tensor_scan(cell[:], gl["f"][:], iz[:], 0.0, ALU.mult, ALU.add
                                               ).then_inc(scan_done, 1)
                    elif name == "cstats":
                        dve.wait_ge(m_full, b.n("m_full", USES[0].index("cT") + 1))
                        if not b.first():
                            dve.wait_ge(c_rstd, b.n("prep", 0))
                        apart(dve)
                        for t in range(TILES):
                            dve.bn_stats(cstats[:, t, :], bank(b, "cT")[:, t * P:t * P + P]).then_inc(c_stats, 1)
                        dve.wait_ge(c_stats, b.n("tiles", TILES))
                        apart(dve)
                        for t in range(TILES):
                            dve.bn_aggr(cmv[:, t, :], cstats[:, t, :]).then_inc(c_aggr, 1)
                        dve.wait_ge(c_aggr, b.n("tiles", TILES))
                        dve.tensor_scalar(cvareps[:], cmv[:, :, 1:2], LN_EPS, None, ALU.add).then_inc(c_eps, 1)
                    elif name == "cnorm":
                        dve.wait_ge(c_rstd, b.n("prep", 1))
                        if not b.first():
                            dve.wait_ge(m_full, b.n("m_full", 0))
                        for t in range(TILES):
                            op = dve.tensor_scalar(cn[:, t, :], bank(b, "cT")[:, t * P:t * P + P], cmv[:, t, 0:1],
                                                   crstd[:, t, :], ALU.subtract, ALU.mult)
                        op.then_inc(dve_rel, 1)
                    elif name in ("top0", "top1"):
                        k = int(name[-1])
                        n = 6 * k
                        src = others if k else lg
                        if k:
                            dve.wait_ge(top, b.n("top", 6))
                        else:
                            dve.wait_ge(act_rel, b.n("act_rel", ACT_USES.index("logits") + 1))
                        dve.tensor_reduce(best[k][:], src[:], AX.X, ALU.max).then_inc(top, 1)
                        dve.wait_ge(top, b.n("top", n + 1))
                        dve.tensor_tensor(equal[k][:], src[:], wide(best[k]), ALU.is_equal).then_inc(top, 1)
                        dve.wait_ge(top, b.n("top", n + 2))
                        dve.tensor_tensor(rated[k][:], equal[k][:], priority[:].broadcast_to(grid), ALU.mult
                                          ).then_inc(top, 1)
                        dve.wait_ge(top, b.n("top", n + 3))
                        dve.tensor_reduce(prior[k][:], rated[k][:], AX.X, ALU.max).then_inc(top, 1)
                        dve.wait_ge(top, b.n("top", n + 4))
                        dve.tensor_tensor(chosen[k][:], rated[k][:], wide(prior[k]), ALU.is_equal
                                          ).then_inc(top, 1)
                        if k:
                            if not b.first():
                                dve.wait_ge(tgap_done, b.n("prep", 0))
                            dve.tensor_tensor(gap[:], best[0][:], best[1][:], ALU.subtract).then_inc(top, 1)
                        else:
                            dve.wait_ge(top, b.n("top", 5))
                            dve.scalar_tensor_tensor(others[:], chosen[0][:], -3.0e38, lg[:], ALU.mult, ALU.add
                                                     ).then_inc(top, 1)
                    elif name == "share":
                        dve.wait_ge(tgap_done, b.n("prep", 1))
                        for k, sign in enumerate((0.5, -0.5)):
                            dve.tensor_scalar(share[k][:], tgap[:], sign, 0.5, ALU.mult, ALU.add
                                              ).then_inc(shared_out, 1)
                        for k in range(K1):
                            dve.wait_ge(shared_out, b.n("shares", 1 + 2 * k))
                            dve.tensor_tensor(weighed[k][:], chosen[k][:], wide(share[k]), ALU.mult
                                              ).then_inc(shared_out, 1)
                        dve.wait_ge(shared_out, b.n("shares", 4))
                        dve.tensor_tensor(cwall[:], weighed[0][:], weighed[1][:], ALU.add).then_inc(shared_out, 1)
                        if not b.first():
                            dve.wait_ge(m_full, b.n("m_full", USES[0].index("rank") + 1 - len(USES[0])))
                        dve.tensor_tensor(selh[:], chosen[0][:], chosen[1][:], ALU.add).then_inc(shared_out, 1)
                    elif name == "count":
                        dve.wait_ge(shared_out, b.n("shares", 6))
                        dve.tensor_scalar(taken[:, 0, :], taken[:, TILES, :], 1.0, None, ALU.mult
                                          ).then_inc(counting, 1)
                        for t in range(TILES):
                            dve.wait_ge(counting, b.n("counting", t + 1))
                            dve.tensor_tensor(taken[:, t + 1, :], taken[:, t, :], selh[:, t, :], ALU.add
                                              ).then_inc(counting, 1)
                    elif name == "cut":
                        dve.wait_ge(m_full, b.n("m_full", USES[0].index("rank") + 1))
                        dve.scalar_tensor_tensor(cwcut[:], bank(b, "rank")[:, 0:TILES * E1].rearrange(
                            "p (t e) -> p t e", e=E1), float(CAPACITY), cwall[:], ALU.is_lt, ALU.mult
                            ).then_inc(dve_rel, 1)
                        dve.wait_ge(dve_rel, b.n("dve_rel", DVE_USES.index("rank") + 1))
                        if not b.first():
                            dve.wait_ge(m_full, b.n("m_full", USES[0].index("cwT") + 1 - len(USES[0])))
                        dve.tensor_scalar(cwhl[:, :, 0, :], cwcut[:], 1.0, None, ALU.mult).then_inc(cut, 1)
                        dve.wait_ge(cut, b.n("two", 1))
                        dve.tensor_tensor(cwhl[:, :, 1, :], cwcut[:], cwhl[:, :, 0, :], ALU.subtract
                                          ).then_inc(cut, 1)

            do_job(0)
            do_job(1)
            dve.memset(zeros[:], 0.0).then_inc(dcst, 1)
            dve.memset(neghalf[:], -0.5).then_inc(dcst, 1)
            dve.memset(taken[:], 0.0).then_inc(dcst, 1)
            for e in range(E1):
                dve.memset(priority[:, :, e:e + 1], float(E1 - e)).then_inc(dcst, 1)
            dve.wait_ge(dcst, 3 + E1)
            run_stages(dve, unit, follow)
            last = Turn(1, PASSES - 1, 1)
            follow(last, DVE_AT["prod"])
            follow(last, DVE_AT["xadd"])



def build_program(nc, io):
    def dram(name, shape, dt=F32):
        return nc.dram_tensor("t_" + name, shape, dt, kind="Internal").ap()

    scratch = {
        "parts": dram("parts", [2, 3, TILES, P, TOK // TILES], BF16),
        "x1": dram("x1", [NTOK, D]),
        "cw0": dram("cw0", [2 * E0, NTOK], F16), "cw1": dram("cw1", [2 * E1, NTOK], F16)}
    for layer in range(2):
        for part in ("xh", "xl"):
            scratch[f"{part}{layer}"] = dram(f"{part}{layer}", [P, NTOK], F16)
        scratch[f"s{layer}"] = dram(f"s{layer}", [P, NTOK])

    with ExitStack() as ctx:
        ident = ctx.enter_context(nc.sbuf_tensor("ident", [P, P], F32))
        identh = ctx.enter_context(nc.sbuf_tensor("identh", [P, P], F16))
        sel = [ctx.enter_context(nc.sbuf_tensor(f"sel{k}", [2 * (E0, E1)[k], UNITS // UPC[k], P], F16))
               for k in range(2)]
        sel_built = ctx.enter_context(nc.semaphore("sel_built"))
        consts_ready = ctx.enter_context(nc.semaphore("consts_ready"))

        with nc.Block() as block:
            @block.gpsimd
            def _(pool):
                pool.memset(ident[:], 0.0).then_inc(consts_ready, 1)
                pool.memset(identh[:], 0.0).then_inc(consts_ready, 1)
                pool.wait_ge(consts_ready, 2)
                for m in (ident, identh):
                    pool.affine_select(out=m[:], in_=m[:], compare_op=ALU.not_equal, fill=1.0, base=0,
                                       pattern=[[-1, P]], channel_multiplier=1).then_inc(consts_ready, 1)

        attention_phase(nc, io, scratch, ident, identh, consts_ready, sel, sel_built)
        mixture_phase(nc, io, scratch, ident, identh, sel)


def kernel(**inputs):
    import concourse.bacc as bacc
    from concourse.bass_utils import run_bass_kernel_spmd

    def permuted(w):
        return w.reshape(-1, CH, DH).transpose(0, 2, 1).reshape(-1, D)

    a = {k: np.asarray(v) for k, v in inputs.items()}
    arrays = {
        "x": a["L0_attn_x"].reshape(NTOK, D),
        "wq": permuted(a["L0_attn_Wq"]), "wk": permuted(a["L0_attn_Wk"]),
        "wv": a["L0_attn_Wv"], "wf": a["L0_attn_Wf"],
        "bq": permuted(a["L0_attn_bq"]).reshape(D, 1), "bk": permuted(a["L0_attn_bk"]).reshape(D, 1),
        "bf": a["L0_attn_bf"].reshape(D, 1), "bv": a["L0_attn_bv"].reshape(1, D),
        "cent": a["L0_ffn_centroids"].T, "ebias": a["L0_ffn_expert_biases"].reshape(1, E0),
        "ups": a["L0_ffn_Ws_up"], "downs": a["L0_ffn_Ws_down"],
        "up0": a["L0_ffn_W_up"].transpose(1, 0, 2).reshape(D, UNITS, P),
        "down0": a["L0_ffn_W_down"].reshape(UNITS, P, D).transpose(1, 0, 2),
        "wg": a["L1_attn_W"].T.reshape(D, 4, D), "bg": a["L1_attn_b"].reshape(4, D).T,
        "lnw": a["L1_attn_ln_w"].reshape(D, 1), "lnb": a["L1_attn_ln_b"].reshape(D, 1),
        "rw": a["L1_ffn_router_w"].T,
        "up1": a["L1_ffn_w1"].transpose(1, 0, 2).reshape(D, UNITS, P),
        "down1": a["L1_ffn_w2"].reshape(UNITS, P, D).transpose(1, 0, 2)}
    arrays = {k: np.ascontiguousarray(v) for k, v in arrays.items()}

    nc = bacc.Bacc("TRN2", target_bir_lowering=False, num_devices=1)
    io = {k: nc.dram_tensor(k, v.shape, mybir.dt.from_np(v.dtype), kind="ExternalInput").ap()
          for k, v in arrays.items()}
    io["out"] = nc.dram_tensor("out", [NTOK, D], F32, kind="ExternalOutput").ap()
    build_program(nc, io)
    r = run_bass_kernel_spmd(nc, [arrays], core_ids=[0])
    return r.results[0]["out"].reshape(BATCH, SEQ, D)
```

```python
import numpy as np

import concourse.bass as bass
from concourse import mybir
from contextlib import ExitStack

ALU = mybir.AluOpType
ACT = mybir.ActivationFunctionType
AX = mybir.AxisListType
F32 = mybir.dt.float32
BF16 = mybir.dt.bfloat16
F16 = mybir.dt.float16

P = 128
D = 128
BATCH, SEQ = 8, 512
NTOK = BATCH * SEQ
TOK = 512
TILES = TOK // P
PASSES = BATCH // 2
CH, DH = 16, 8
GT = 32
NG = P // GT
KT = CH * GT // P
SCALE = 8.0
LN_EPS = 1e-5
E0, K0 = 64, 8
E1, K1 = 8, 2
CAPACITY = int(1.25 * NTOK * K1 / E1) + 1
UNITS = 32
WS = 64.0
TERMS = [(a, b) for a in range(3) for b in range(3)]
ROWS = DH * len(TERMS)
MROW = 96
KROWS = MROW + 2


class Stage:

    def __init__(self, i, p):
        self.i, self.p = i, p

    def at(self, per, k):
        return self.i * (2 * per) + (self.p * per + k)

    def own(self, per, k):
        return self.i * per + k

    def next(self):
        return Stage(self.i, 1) if self.p == 0 else Stage(self.i + 1, 0)

    def tokens(self):
        return bass.ds(self.i * (2 * TOK) + self.p * TOK, TOK)

    def first(self):
        return isinstance(self.i, int) and self.i == 0 and self.p == 0

    def last(self):
        return isinstance(self.i, int) and self.i == PASSES - 1 and self.p == 1


def passes(eng, body):
    body(0)
    with eng.Fori(1, PASSES - 1) as i:
        body(i)
    body(PASSES - 1)


def apart(eng):
    eng.nop(nofuse=True)



def attention_phase(nc, io, scratch, ident, identh, consts_ready, sel, sel_built):
    with ExitStack() as ctx:
        def sb(name, shape, dt=F32):
            return ctx.enter_context(nc.sbuf_tensor(name, shape, dt))

        def sem(name):
            return ctx.enter_context(nc.semaphore(name))

        wq, wk, wv, wf = (sb(f"a_w{n}", [P, D]) for n in "qkvf")
        bq, bk, bf = (sb(f"a_b{n}", [P, 1]) for n in "qkf")
        bv = sb("a_bv", [P, KT, DH])
        cent = sb("a_cent", [P, E0])
        ebias = sb("a_ebias", [P, E0])
        xin = [sb(f"a_xin{p}", [P, TILES, D]) for p in range(2)]
        xn = [sb(f"a_xn{p}", [P, TILES, D]) for p in range(2)]
        stats = sb("a_stats", [P, TILES, 6])
        meanvar = sb("a_meanvar", [P, TILES, 2])
        rstd = sb("a_rstd", [P, TILES, 1])
        vareps = sb("a_vareps", [P, TILES, 1])
        cvareps = sb("a_cvareps", [P, 1])
        neghalf = sb("a_neghalf", [P, TILES])
        xnT = sb("a_xnT", [P, TOK])
        xh = sb("a_xh", [P, TOK], F16)
        xl = sb("a_xl", [P, TOK], F16)
        full = [sb(f"a_{n}32", [P, TOK]) for n in "qk"]
        rest = [sb(f"a_{n}rest", [P, TOK]) for n in "qk"]
        parts = [sb(f"a_{n}parts", [P, 3, TOK], BF16) for n in "qk"]
        stack = [[sb(f"a_{n}stack{p}", [KROWS, TILES, CH * GT, NG], BF16) for p in range(2)] for n in "qk"]
        mrow = sb("a_mrow", [KROWS, 4, 8, NG, GT], BF16)
        vtmp = sb("a_vtmp", [P, TOK // GT, KT, DH])
        vst = [sb(f"a_vst{p}", [P, TOK // GT, KT, 32]) for p in range(2)]
        probs = sb("a_probs", [P, 2, NG, 512])
        mx = [sb(f"a_mx{p}", [P, 16]) for p in range(2)]
        zeros = sb("a_zeros", [P, TOK])
        ones = sb("a_ones", [P, 2 * TOK], BF16)
        mneg = sb("a_mneg", [P, 2, 32], BF16)
        mT = sb("a_mT", [P, 2, 32], BF16)
        oT = sb("a_oT", [P, CH, 32])
        rden = sb("a_rden", [P, CH, 1])
        ctx_sb = sb("a_ctx", [P, D])
        res = sb("a_res", [P, D])
        xlast = sb("a_xlast", [P, D])
        cstats = sb("a_cstats", [P, 6])
        cmv = sb("a_cmv", [P, 2])
        crstd = sb("a_crstd", [P, 1])
        cn = sb("a_cn", [P, D])
        cT = sb("a_cT", [P, TOK])
        sT = sb("a_sT", [P, TOK])
        aff = sb("a_aff", [P, TILES, E0])
        biased = sb("a_biased", [P, TILES, E0])
        best = sb("a_best", [P, TILES, 8])
        dropped = sb("a_dropped", [P, TILES, E0])
        mask = sb("a_mask", [P, TILES, E0])
        esig = sb("a_esig", [P, TILES, E0])
        wsel = sb("a_wsel", [P, TILES, E0])
        wsum = sb("a_wsum", [P, TILES, 1])
        wsume = sb("a_wsume", [P, TILES, 1])
        wrec = sb("a_wrec", [P, TILES, 1])
        cw = sb("a_cw", [P, TILES, E0])
        cwhl = sb("a_cwhl", [P, TILES, 2, E0], F16)
        cwT = sb("a_cwT", [P, TOK], F16)

        score = ctx.enter_context(nc.psum_tensor("a_score", [P, 2, 512], F32))
        mxps = ctx.enter_context(nc.psum_tensor("a_mxps", [P, 2, 2, 512], F32))
        ops = ctx.enter_context(nc.psum_tensor("a_ops", [P, 512], F32))
        misc = ctx.enter_context(nc.psum_tensor("a_misc", [P, 512], F32))
        misch = misc[:].bitcast(F16)

        w_in = sem("a_w_in")
        x_in = [sem(f"a_x_in{p}") for p in range(2)]
        ln_eps, c_eps = sem("a_ln_eps"), sem("a_c_eps")
        ln_stats, ln_aggr, ln_rstd = sem("a_ln_stats"), sem("a_ln_aggr"), sem("a_ln_rstd")
        xn_ready = sem("a_xn_ready")
        misc_full, misc_free = sem("a_misc_full"), sem("a_misc_free")
        split = sem("a_split")
        x_out = sem("a_x_out")
        qk_in = [sem(f"a_qk_in{p}") for p in range(2)]
        parts_out = sem("a_parts_out")
        small = sem("a_small")
        init = [sem(f"a_init{p}") for p in range(2)]
        vinit = [sem(f"a_vinit{p}") for p in range(2)]
        v_ready = sem("a_v_ready")
        score_full, exp_done = sem("a_score_full"), sem("a_exp_done")
        mx_full, mx_done = sem("a_mx_full"), sem("a_mx_done")
        mneg_done, mT_done = sem("a_mneg_done"), sem("a_mT_done")
        m_in, m_placed = sem("a_m_in"), sem("a_m_placed")
        pv_done = sem("a_pv_done")
        o_out, den_done = sem("a_o_out"), sem("a_den_done")
        kept = sem("a_kept")
        ctx_done, res_done = sem("a_ctx_done"), sem("a_res_done")
        c_stats, c_aggr, c_rstd, cn_done = (sem(f"a_c_{n}") for n in ("stats", "aggr", "rstd", "norm"))
        s_out = sem("a_s_out")
        biased_done, best_done, drop_done = sem("a_biased"), sem("a_best_done"), sem("a_drop_done")
        esig_done, pool_r, dve_r = sem("a_esig_done"), sem("a_pool_router"), sem("a_dve_router")
        cw_out = sem("a_cw_out")

        W_LOADS = 4 + 3 + NG + 2
        STACK_LOADS = len(TERMS) + 3

        MID = ["xnT", "q", "k", "cn3p", "V", "logits", "sTp", "cn0", "cn1", "cwT", "cn2"]
        FIRST = [x for x in MID if x not in ("cn3p", "sTp")]
        START = ["xnT", "q", "k", "V", "logits", "cwT"]
        LAST = ["cn3p", "sTp", "cn0", "cn1", "cn2", "cn3", "sT"]

        def misc_use(s, name):
            if s is None:
                return START.index(name)
            if s.first():
                return len(START) + FIRST.index(name)
            if s.last():
                return len(START) - 2 + len(MID) * (BATCH - 1) + LAST.index(name)
            return s.at(len(MID), len(START) - 2 + MID.index(name))

        SLOTS = {(0, 1): ["xnT"], (0, 2): ["q"], (0, 3): ["k"], (1, 0): ["cn3p"], (1, 1): ["V"],
                 (1, 2): ["logits"], (1, 3): ["sTp"], (2, 0): ["cn0"], (2, 3): ["cn1"], (3, 1): ["cwT"], (3, 3): ["cn2"]}

        def slot(s, tau, kt):
            names = SLOTS.get((tau, kt), [])
            skip = ("cn3p", "sTp") if s.first() else ()
            if s.last():
                skip = ("xnT", "q", "k", "V", "logits", "cwT")
            return [x for x in names if x not in skip]

        def mx_pairs(s, tau, kt):
            ahead = tau + 1 if kt == 0 else tau + 2
            js = ((6, 7), (0, 1), (2, 3), (4, 5))[kt]
            if s.last() and ahead > TILES - 1:
                return []
            return [(ahead, j) for j in js]

        def period(f):
            def body(i):
                for p in range(2):
                    for tau in range(TILES):
                        f(Stage(i, p), tau)
            return body

        NONE = Stage(0, 0)
        PLACES = [(2, 1), (2, 3), (3, 1), (3, 2)]

        block = ctx.enter_context(nc.Block())

        @block.sync
        def _(sp):
            x_t = io["x"].rearrange("(n p) d -> p n d", p=P)

            def load_x(s):
                apart(sp)
                sp.dma_start(xin[s.p][:], x_t[:, bass.ds(s.i * (2 * TILES) + s.p * TILES, TILES), :]
                             ).then_inc(x_in[s.p], 16)

            def constant_rows(p):
                sp.wait_ge(small, 4)
                reps = TILES * CH * GT * NG // (2 * TOK)
                for side in range(2):
                    sp.dma_start(stack[side][p][ROWS:MROW].rearrange("r n c g -> r (n c g)").rearrange(
                        "r (k x) -> r k x", k=reps), zeros[ROWS:MROW].bitcast(BF16).unsqueeze(1).broadcast_to(
                        [MROW - ROWS, reps, 2 * TOK])).then_inc(init[p], 16)
                sp.dma_start(stack[1][p][MROW:KROWS].rearrange("r n c g -> r (n c g)").rearrange(
                    "r (k x) -> r k x", k=reps), ones[MROW:KROWS].unsqueeze(1).broadcast_to(
                    [KROWS - MROW, reps, 2 * TOK])).then_inc(init[p], 16)

            def parts_to_dram(n, side):
                if not (isinstance(n.i, int) and n.i == 0 and n.p == 0):
                    b = Stage(n.i, 0) if n.p else Stage(n.i - 1, 1)
                    sp.wait_ge(qk_in[b.p], b.own(16 * STACK_LOADS, 16 * STACK_LOADS))
                    apart(sp)
                sp.wait_ge(split, n.at(8, 3 * side + 3))
                apart(sp)
                for a in range(3):
                    sp.dma_start(scratch["parts"][side, :, a].rearrange("n r x -> r n x"),
                                 parts[side][:, a, :].rearrange("p (n x) -> p n x", n=TILES)
                                 ).then_inc(parts_out, 16)

            def stack_in(n, side, which=range(3)):
                sp.wait_ge(parts_out, n.at(96, 48 * side + 48))
                there = scratch["parts"][side]
                for a in which:
                    if side:
                        sp.dma_start(stack[1][n.p][3 * DH * a:3 * DH * (a + 1)].rearrange("r n c g -> r n (c g)"),
                                     there.rearrange("n a (j c) x -> (a j) n (c x)", j=DH)
                                     ).then_inc(qk_in[n.p], 16)
                        continue
                    for b in range(3):
                        r = DH * (3 * a + b)
                        sp.dma_start(stack[0][n.p][r:r + DH].rearrange("j n c g -> j n (c g)"),
                                     there[:, a].rearrange("n (j c) x -> j n (c x)", j=DH)
                                     ).then_inc(qk_in[n.p], 16)

            def x_parts_out(n):
                sp.wait_ge(split, n.at(8, 8))
                apart(sp)
                sp.dma_start(scratch["xh0"][:, n.tokens()], xh[:]).then_inc(x_out, 16)
                sp.dma_start(scratch["xl0"][:, n.tokens()], xl[:]).then_inc(x_out, 16)

            def max_rows(s, tau):
                if not (s.first() and tau == 0):
                    sp.wait_ge(m_placed, s.at(4 * TILES, 4 * tau))
                    apart(sp)
                sp.wait_ge(mT_done, s.at(TILES, tau + 1))
                for a in range(2):
                    sp.dma_start(mrow[MROW + a:MROW + a + 1].rearrange("o q r g t -> o (q r g t)"), mT[:, a, :]
                                 ).then_inc(m_in, 16)

            def cw_store(s, n):
                sp.wait_ge(misc_free, misc_use(s, "cwT") + 1)
                apart(sp)
                sp.dma_start(scratch["cw0"][:, n.tokens()], cwT[:]).then_inc(cw_out, 16)

            def s_store(s, name, prev):
                sp.wait_ge(misc_free, misc_use(s, name) + 1)
                apart(sp)
                sp.dma_start(scratch["s0"][:, prev], sT[:]).then_inc(s_out, 16)

            load_x(Stage(0, 0))
            for dst, src in ((wq, "wq"), (wk, "wk"), (wv, "wv"), (wf, "wf"), (bq, "bq"), (bk, "bk"), (bf, "bf"),
                             (cent, "cent")):
                sp.dma_start(dst[:], io[src]).then_inc(w_in, 16)
            sp.dma_start(ebias[:], io["ebias"].broadcast_to([P, E0])).then_inc(w_in, 16)
            for cq in range(NG):
                sp.dma_start(bv[GT * cq:GT * cq + GT, :, :],
                             io["bv"].rearrange("o (k c j) -> o k c j", c=4, j=DH)[:, :, cq, :]
                             .broadcast_to([GT, KT, DH])).then_inc(w_in, 16)
            load_x(Stage(0, 1))
            constant_rows(0)
            parts_to_dram(NONE, 0)
            sp.wait_ge(init[0], 16 * 3)
            stack_in(NONE, 0, (0,))
            parts_to_dram(NONE, 1)
            stack_in(NONE, 0, (1, 2))
            stack_in(NONE, 1)
            constant_rows(1)
            x_parts_out(NONE)
            cw_store(None, NONE)
            max_rows(NONE, 0)

            def step(s, tau):
                n = s.next()
                more = not s.last()
                if tau == 0:
                    if more and not (isinstance(s.i, int) and s.i == PASSES - 1):
                        sp.wait_ge(xn_ready, s.at(TILES, TILES))
                        load_x(Stage(s.i + 1, s.p))
                if more or tau < TILES - 1:
                    max_rows(s, tau + 1)
                if tau == 0 and more:
                    if not s.first():
                        sp.wait_ge(score_full, s.at(64, 0))
                    else:
                        sp.wait_ge(init[1], 16 * 3)
                    parts_to_dram(n, 0)
                if tau == 1 and more:
                    stack_in(n, 0, (0,))
                    parts_to_dram(n, 1)
                    stack_in(n, 0, (1, 2))
                    stack_in(n, 1)
                    x_parts_out(n)
                if tau == 1 and not s.first():
                    prev = bass.ds(s.i * (2 * TOK) + (s.p - 1) * TOK, TOK)
                    s_store(s, "sTp", prev)
                if tau == 3 and more:
                    cw_store(s, n)

            passes(sp, period(step))
            s_store(Stage(PASSES - 1, 1), "sT", slice(NTOK - TOK, NTOK))
            sp.wait_ge(s_out, 16 * BATCH)
            sp.wait_ge(cw_out, 16 * BATCH)
            sp.wait_ge(x_out, 32 * BATCH)

        @block.gpsimd
        def _(pool):
            def inverse_std(n):
                pool.wait_ge(ln_eps, n.at(1, 1))
                pool.tensor_tensor(rstd[:], vareps[:], neghalf[:, 0:TILES].unsqueeze(2), ALU.pow
                                   ).then_inc(ln_rstd, 1)

            def split3(s, n, side):
                pool.wait_ge(misc_free, misc_use(s, "qk"[side]) + 1)
                if s is not None:
                    pool.wait_ge(parts_out, n.at(96, 0))
                f, r, pt, base = full[side], rest[side], parts[side], 3 * side
                pool.tensor_tensor(r[:], f[:], pt[:, 0, :], ALU.subtract).then_inc(split, 1)
                pool.wait_ge(split, n.at(8, base + 1))
                pool.tensor_tensor(pt[:, 1, :], r[:], zeros[:], ALU.add).then_inc(split, 1)
                pool.wait_ge(split, n.at(8, base + 2))
                pool.tensor_tensor(pt[:, 2, :], r[:], pt[:, 1, :], ALU.subtract).then_inc(split, 1)

            def split_x(s, n):
                pool.wait_ge(misc_free, misc_use(s, "xnT") + 1)
                if s is not None:
                    pool.wait_ge(x_out, n.at(32, 0))
                pool.tensor_tensor(xh[:], xnT[:], zeros[:], ALU.add).then_inc(split, 1)
                pool.wait_ge(split, n.at(8, 7))
                pool.tensor_tensor(xl[:], xnT[:], xh[:], ALU.subtract).then_inc(split, 1)

            def values(s, n):
                pool.wait_ge(misc_free, misc_use(s, "V") + 1)
                if s is not None:
                    if not s.first():
                        pool.wait_ge(pv_done, s.at(16, 0))
                if s is None:
                    pool.wait_ge(vinit[0], 2)
                elif s.first():
                    pool.wait_ge(vinit[1], 2)
                pool.tensor_tensor(vst[n.p][:, :, :, 0:DH], vtmp[:],
                                   bv[:].unsqueeze(1).broadcast_to([P, TOK // GT, KT, DH]), ALU.add
                                   ).then_inc(v_ready, 1)

            def router_bias(s, n):
                pool.wait_ge(misc_free, misc_use(s, "logits") + 1)
                pool.tensor_tensor(biased[:], aff[:], ebias[:].unsqueeze(1).broadcast_to([P, TILES, E0]),
                                   ALU.add).then_inc(biased_done, 1)

            def router_weights(s, n):
                pool.wait_ge(dve_r, n.at(5, 5))
                pool.tensor_tensor(cw[:], wsel[:], wrec[:].broadcast_to([P, TILES, E0]), ALU.mult
                                   ).then_inc(pool_r, 1)
                pool.wait_ge(pool_r, n.at(3, 1))
                pool.tensor_tensor(cwhl[:, :, 0, :], cw[:], zeros[:, 0:TILES * E0].rearrange(
                    "p (t e) -> p t e", t=TILES), ALU.add).then_inc(pool_r, 1)
                pool.wait_ge(pool_r, n.at(3, 2))
                pool.tensor_tensor(cwhl[:, :, 1, :], cw[:], cwhl[:, :, 0, :], ALU.subtract).then_inc(pool_r, 1)

            def context(s, tau):
                pool.wait_ge(den_done, s.at(TILES, tau + 1))
                pool.tensor_tensor(ctx_sb[:].rearrange("p (c j) -> p c j", c=CH), oT[:, :, 0:DH],
                                   rden[:].broadcast_to([P, CH, DH]), ALU.mult).then_inc(ctx_done, 1)
                pool.wait_ge(ctx_done, s.at(TILES, tau + 1))
                if tau == TILES - 1:
                    pool.wait_ge(kept, s.at(1, 1))
                row = xlast[:] if tau == TILES - 1 else xn[s.p][:, tau, :]
                pool.tensor_tensor(res[:], ctx_sb[:], row, ALU.add).then_inc(res_done, 1)

            def context_norm(s, tau):
                pool.wait_ge(c_eps, s.at(TILES, tau + 1))
                pool.tensor_tensor(crstd[:], cvareps[:], neghalf[:, 0:1], ALU.pow).then_inc(c_rstd, 1)
                if not (s.first() and tau == 0):
                    pool.wait_ge(misc_full, misc_use(s, f"cn{tau - 1}" if tau else "cn3p") + 1)
                pool.wait_ge(c_rstd, s.at(TILES, tau + 1))
                apart(pool)
                pool.tensor_scalar(cn[:], res[:], cmv[:, 0:1], crstd[:], ALU.subtract, ALU.mult
                                   ).then_inc(cn_done, 1)

            pool.wait_ge(small, 4)
            inverse_std(NONE)
            pool.wait_ge(w_in, 16 * W_LOADS)
            split3(None, NONE, 0)
            split3(None, NONE, 1)
            split_x(None, NONE)
            values(None, NONE)
            router_bias(None, NONE)
            router_weights(None, NONE)

            def back(s):
                return Stage(s.i, 0) if s.p else Stage(s.i - 1, 1)

            def step(s, tau):
                n, more = s.next(), not s.last()
                if tau == 0 and more:
                    inverse_std(n)
                if not (s.first() and tau == 0):
                    before = (s, tau - 1) if tau else (back(s), TILES - 1)
                    context(*before)
                    context_norm(*before)
                if tau == TILES - 1:
                    pool.tensor_tensor(xlast[:], xn[s.p][:, tau, :], zeros[:, 0:D], ALU.add).then_inc(kept, 1)
                if s.last():
                    for k in ((0,), (1,), (2,), (3, 4, 5))[tau]:
                        build_selectors(pool, sel, sel_built, k)
                if not more:
                    return
                if tau == 0:
                    split3(s, n, 0)
                    split3(s, n, 1)
                    split_x(s, n)
                if tau == 1:
                    values(s, n)
                    router_bias(s, n)
                if tau == 2:
                    router_weights(s, n)

            passes(pool, period(step))
            context(Stage(PASSES - 1, 1), TILES - 1)
            context_norm(Stage(PASSES - 1, 1), TILES - 1)

        @block.scalar
        def _(act):
            def take(s, name, n):
                act.wait_ge(misc_full, misc_use(s, name) + 1)
                if name == "xnT":
                    if s is not None:
                        act.wait_ge(split, n.at(8, 0))
                    op = act.activation(xnT[:], misc[:], ACT.Copy)
                elif name in ("q", "k"):
                    side = "qk".index(name)
                    if s is not None:
                        act.wait_ge(parts_out, n.at(96, 0))
                    for dst in (parts[side][:, 0, :], full[side][:]):
                        op = act.activation(dst.rearrange("p (n t g) -> p n t g", t=GT, g=NG),
                                            misc[:].rearrange("p (n g t) -> p n t g", t=GT, g=NG),
                                            ACT.Identity, bias=(bq, bk)[side][:])
                elif name == "logits":
                    if s is not None:
                        act.wait_ge(biased_done, n.at(1, 0))
                        act.wait_ge(esig_done, n.at(1, 0))
                    op = act.activation(aff[:].rearrange("p t e -> p (t e)"), misc[:, :TILES * E0], ACT.Copy)
                elif name == "cwT":
                    if s is not None:
                        act.wait_ge(cw_out, n.at(16, 0))
                    op = act.activation(cwT[:], misch[:, :TOK], ACT.Copy)
                elif name[:2] == "cn":
                    t = int(name[2])
                    op = act.activation(cT[:, t * P:t * P + P], misc[:, :P], ACT.Copy)
                else:
                    if name == "sTp" and not (isinstance(s.i, int) and s.i == 0 and s.p == 1) or name == "sT":
                        done = s.at(16, -16) if name == "sTp" else s.at(16, 0)
                        act.wait_ge(s_out, done)
                    op = act.activation(sT[:], misc[:], ACT.Identity, bias=bf[:])
                op.then_inc(misc_free, 1)
                if name == "logits":
                    act.wait_ge(misc_free, misc_use(s, name) + 1)
                    if s is not None:
                        act.wait_ge(dve_r, n.at(5, 2 - 5))
                    act.activation(esig[:], aff[:], ACT.Tanh, scale=0.5).then_inc(esig_done, 1)

            def place_maxima(s, tau, qts):
                where, at = (s if tau < TILES else s.next()), tau % TILES
                act.wait_ge(m_in, s.at(32 * TILES, 32 * tau + 32))
                for qt in qts:
                    act.activation(stack[0][where.p][MROW:KROWS, at, qt * P:qt * P + P, :].rearrange(
                        "a (q t) g -> a q t g", q=4), mrow[MROW:KROWS, :, qt, :, :].rearrange("a q g t -> a q t g"),
                        ACT.Copy).then_inc(m_placed, 1)

            take(None, START[0], NONE)
            act.wait_ge(w_in, 16 * W_LOADS)
            for name in START[1:]:
                if name != "V":
                    take(None, name, NONE)
            place_maxima(NONE, 0, range(4))

            def step(s, tau):
                for kt in range(KT):
                    for g in range(NG):
                        act.wait_ge(score_full, s.at(64, 16 * tau + 4 * kt + g + 1))
                        if g == 0 and not (s.first() and 4 * tau + kt < 2):
                            act.wait_ge(pv_done, s.at(16, 4 * tau + kt - 1))
                        act.activation(probs[:, kt % 2, g, :], score[:, g % 2, :], ACT.Exp, scale=SCALE
                                       ).then_inc(exp_done, 1)
                        if (kt, g) in PLACES and not (s.last() and tau == TILES - 1):
                            place_maxima(s, tau + 1, [PLACES.index((kt, g))])
                    for name in slot(s, tau, kt):
                        if name != "V":
                            take(s, name, s.next())

            passes(act, period(step))
            last = Stage(PASSES - 1, 1)
            take(last, "cn3", last)
            take(last, "sT", last)

        @block.tensor
        def _(pe):
            def use(s, name):
                v = misc_use(s, name)
                if not (isinstance(v, int) and v == 0):
                    pe.wait_ge(misc_free, v)

            def fill(s, name, n):
                use(s, name)
                if name == "xnT":
                    pe.wait_ge(xn_ready, n.at(TILES, TILES))
                    for t in range(TILES):
                        op = pe.transpose(misc[:, t * P:t * P + P], xn[n.p][:, t, :], ident[:])
                elif name in ("q", "k"):
                    if name == "q":
                        pe.wait_ge(misc_free, misc_use(s, "xnT") + 1)
                    if s is not None:
                        pe.wait_ge(split, n.at(8, 0))
                    op = pe.matmul(misc[:], (wq if name == "q" else wk)[:], xnT[:], start=True, stop=True)
                elif name == "V":
                    op = pe.matmul(misc[:], wv[:], xnT[:], start=True, stop=True)
                elif name == "logits":
                    for t in range(TILES):
                        op = pe.matmul(misc[:, t * E0:t * E0 + E0], xnT[:, t * P:t * P + P], cent[:],
                                       start=True, stop=True)
                elif name == "cwT":
                    pe.wait_ge(pool_r, n.at(3, 3))
                    for t in range(TILES):
                        op = pe.transpose(misch[:, t * P:t * P + P],
                                          cwhl[:, t, :, :].rearrange("p a e -> p (a e)"), identh[:])
                elif name[:2] == "cn":
                    t = int(name[2])
                    back = -1 if name[-1] == "p" else t
                    pe.wait_ge(cn_done, s.at(TILES, back + 1))
                    op = pe.transpose(misc[:, :P], cn[:], ident[:])
                else:
                    pe.wait_ge(misc_free, misc_use(s, "cn3p" if name == "sTp" else "cn3") + 1)
                    op = pe.matmul(misc[:], wf[:], cT[:], start=True, stop=True)
                op.then_inc(misc_full, 1)

            def maxima(s, ahead, j):
                where = s if ahead < TILES else s.next()
                at = ahead % TILES
                if j == 0 and at == 0:
                    pe.wait_ge(qk_in[where.p], where.own(16 * STACK_LOADS, 16 * STACK_LOADS))
                if not (s.first() and 8 * ahead + j < 2):
                    pe.wait_ge(mx_done, s.at(32, 8 * ahead + j - 1))
                qt = j // 2
                for k in range(2):
                    g = 2 * (j % 2) + k
                    op = pe.matmul(mxps[:, j % 2, k, :], stack[0][where.p][0:ROWS, at, qt * P:qt * P + P, g],
                                   stack[1][where.p][0:ROWS, at, :, g], start=True, stop=True)
                op.then_inc(mx_full, 1)

            def scores(s, tau, kt, g):
                if kt == 0 and g == 0:
                    pe.wait_ge(m_placed, s.at(4 * TILES, 4 * tau + 4))
                if not (s.first() and 16 * tau + 4 * kt + g < 2):
                    pe.wait_ge(exp_done, s.at(64, 16 * tau + 4 * kt + g - 1))
                pe.matmul(score[:, g % 2, :], stack[1][s.p][0:KROWS, tau, kt * P:kt * P + P, g],
                          stack[0][s.p][0:KROWS, tau, :, g], start=True, stop=True
                          ).then_inc(score_full, 1)

            def weighted(s, tau, kt, half):
                pe.wait_ge(exp_done, s.at(64, 16 * tau + 4 * kt + 4))
                if kt == 0:
                    if tau == 0:
                        pe.wait_ge(v_ready, s.at(1, 1))
                    if not (s.first() and tau == 0):
                        pe.wait_ge(o_out, s.at(TILES, tau))
                for g in range(NG):
                    op = pe.matmul(ops[GT * g:GT * g + GT, :], vst[half][:, tau * NG + g, kt, :],
                                   probs[:, kt % 2, g, :], start=(kt == 0), stop=(kt == KT - 1),
                                   skip_group_check=True)
                op.then_inc(pv_done, 1)

            pe.wait_ge(consts_ready, 4)
            fill(None, START[0], NONE)
            pe.wait_ge(w_in, 16 * W_LOADS)
            for name in START[1:]:
                fill(None, name, NONE)
            pe.wait_ge(init[0], 16 * 3)
            for j in range(8):
                maxima(NONE, 0, j)
            for j in range(6):
                maxima(NONE, 1, j)

            def step(s, tau):
                for kt in range(KT):
                    pairs = mx_pairs(s, tau, kt)
                    scores(s, tau, kt, 0)
                    if pairs:
                        maxima(s, *pairs[0])
                    scores(s, tau, kt, 1)
                    if kt:
                        weighted(s, tau, kt - 1, s.p)
                    elif tau:
                        weighted(s, tau - 1, KT - 1, s.p)
                    elif not s.first():
                        weighted(Stage(s.i, 0) if s.p else Stage(s.i - 1, 1), TILES - 1, KT - 1, 1 - s.p)
                    scores(s, tau, kt, 2)
                    if pairs:
                        maxima(s, *pairs[1])
                    scores(s, tau, kt, 3)
                    for name in slot(s, tau, kt):
                        fill(s, name, s.next())

            passes(pe, period(step))
            last = Stage(PASSES - 1, 1)
            weighted(last, TILES - 1, KT - 1, 1)
            fill(last, "cn3", last)
            fill(last, "sT", last)

        @block.vector
        def _(dve):
            def statistics(n):
                dve.wait_ge(x_in[n.p], n.own(16, 16))
                for t in range(TILES):
                    dve.bn_stats(stats[:, t, :], xin[n.p][:, t, :]).then_inc(ln_stats, 1)
                dve.wait_ge(ln_stats, n.at(TILES, TILES))
                if not (isinstance(n.i, int) and n.i == 0 and n.p == 0):
                    dve.wait_ge(xn_ready, n.at(TILES, 0))
                apart(dve)
                for t in range(TILES):
                    dve.bn_aggr(meanvar[:, t, :], stats[:, t, :]).then_inc(ln_aggr, 1)
                dve.wait_ge(ln_aggr, n.at(TILES, TILES))
                dve.tensor_scalar(vareps[:], meanvar[:, :, 1:2], LN_EPS, None, ALU.add).then_inc(ln_eps, 1)

            def normalise(n):
                dve.wait_ge(ln_rstd, n.at(1, 1))
                for t in range(TILES):
                    dve.tensor_scalar(xn[n.p][:, t, :], xin[n.p][:, t, :], meanvar[:, t, 0:1], rstd[:, t, :],
                                      ALU.subtract, ALU.mult).then_inc(xn_ready, 1)

            def transpose_values(s, n):
                dve.wait_ge(misc_full, misc_use(s, "V") + 1)
                if s is not None:
                    dve.wait_ge(v_ready, n.at(1, 0))
                dve.transpose(vtmp[:].rearrange("p g k j -> p (g k j)"), misc[:]).then_inc(misc_free, 1)

            def maximum(s, ahead, j):
                dve.wait_ge(mx_full, s.at(32, 8 * ahead + j + 1))
                c = (j // 2) * 4 + 2 * (j % 2)
                dve.tensor_reduce(mx[ahead % 2][:, c:c + 2], mxps[:, j % 2, :, :], AX.X, ALU.max
                                  ).then_inc(mx_done, 1)

            def minus_maximum(s, ahead):
                m = mx[ahead % 2]
                dve.wait_ge(mx_done, s.at(32, 8 * ahead + 8))
                dve.tensor_scalar(mneg[:, 0, 0:16], m[:], -1.0, None, ALU.mult).then_inc(mneg_done, 1)
                dve.wait_ge(mneg_done, s.at(2 * TILES, 2 * ahead + 1))
                dve.scalar_tensor_tensor(mneg[:, 1, 0:16], m[:], -1.0, mneg[:, 0, 0:16], ALU.mult, ALU.subtract
                                         ).then_inc(mneg_done, 1)
                dve.wait_ge(mneg_done, s.at(2 * TILES, 2 * ahead + 2))
                if not (s.first() and ahead == 0):
                    dve.wait_ge(m_in, s.at(32 * TILES, 32 * ahead))
                dve.transpose(mT[:].rearrange("p a t -> p (a t)"), mneg[:].rearrange("p a t -> p (a t)")).then_inc(mT_done, 1)

            def context(s, tau):
                dve.wait_ge(pv_done, s.at(16, 4 * tau + 4))
                if not (s.first() and tau == 0):
                    dve.wait_ge(ctx_done, s.at(TILES, tau))
                dve.transpose(oT[:].rearrange("p c j -> p (c j)"), ops[:]).then_inc(o_out, 1)

            def denominators(s, tau):
                dve.wait_ge(o_out, s.at(TILES, tau + 1))
                dve.reciprocal(rden[:], oT[:, :, DH:DH + 1]).then_inc(den_done, 1)

            def context_stats(s, tau):
                dve.wait_ge(res_done, s.at(TILES, tau + 1))
                dve.bn_stats(cstats[:], res[:]).then_inc(c_stats, 1)

            def context_meanvar(s, tau):
                dve.wait_ge(c_stats, s.at(TILES, tau + 1))
                if not (s.first() and tau == 0):
                    dve.wait_ge(cn_done, s.at(TILES, tau))
                apart(dve)
                dve.bn_aggr(cmv[:], cstats[:]).then_inc(c_aggr, 1)

            def context_vareps(s, tau):
                dve.wait_ge(c_aggr, s.at(TILES, tau + 1))
                dve.tensor_scalar(cvareps[:], cmv[:, 1:2], LN_EPS, None, ALU.add).then_inc(c_eps, 1)

            def largest(n):
                dve.wait_ge(biased_done, n.at(1, 1))
                apart(dve)
                for t in range(TILES):
                    dve.max(best[:, t, :], biased[:, t, :]).then_inc(best_done, 1)

            def choose(n):
                dve.wait_ge(best_done, n.at(TILES, TILES))
                apart(dve)
                for t in range(TILES):
                    dve.match_replace(dropped[:, t, :], best[:, t, :], biased[:, t, :], -3.0e38
                                      ).then_inc(drop_done, 1)

            def chosen_weights(n):
                dve.wait_ge(drop_done, n.at(TILES, TILES))
                dve.tensor_tensor(mask[:], dropped[:], biased[:], ALU.not_equal).then_inc(dve_r, 1)
                dve.wait_ge(dve_r, n.at(5, 1))
                dve.wait_ge(esig_done, n.at(1, 1))
                if not (isinstance(n.i, int) and n.i == 0 and n.p == 0):
                    dve.wait_ge(pool_r, n.at(3, 0))
                dve.scalar_tensor_tensor(wsel[:], esig[:], 1.0, mask[:], ALU.add, ALU.mult).then_inc(dve_r, 1)

            def weights(n):
                dve.wait_ge(dve_r, n.at(5, 2))
                dve.tensor_reduce(wsum[:], wsel[:], AX.X, ALU.add).then_inc(dve_r, 1)
                dve.wait_ge(dve_r, n.at(5, 3))
                dve.tensor_scalar(wsume[:], wsum[:], 2e-8, None, ALU.add).then_inc(dve_r, 1)
                dve.wait_ge(dve_r, n.at(5, 4))
                dve.reciprocal(wrec[:], wsume[:]).then_inc(dve_r, 1)

            def constant_values(p):
                dve.memset(vst[p][:], 0.0).then_inc(vinit[p], 1)
                dve.wait_ge(vinit[p], 1)
                dve.memset(vst[p][:, :, :, DH:DH + 1], 1.0).then_inc(vinit[p], 1)

            dve.memset(neghalf[:], -0.5).then_inc(small, 1)
            dve.memset(zeros[:], 0.0).then_inc(small, 1)
            dve.memset(ones[:], 1.0).then_inc(small, 1)
            dve.memset(mneg[:], 0.0).then_inc(small, 1)
            statistics(NONE)
            normalise(NONE)
            constant_values(0)
            dve.wait_ge(small, 4)
            transpose_values(None, NONE)
            largest(NONE)
            choose(NONE)
            chosen_weights(NONE)
            weights(NONE)
            constant_values(1)
            for j in range(8):
                maximum(NONE, 0, j)
            minus_maximum(NONE, 0)
            for j in range(6):
                maximum(NONE, 1, j)

            def step(s, tau):
                n, more = s.next(), not s.last()
                before = (s, tau - 1) if tau else (Stage(s.i, 0) if s.p else Stage(s.i - 1, 1), TILES - 1)
                later = not (s.first() and tau == 0)
                for kt in range(KT):
                    if tau == 0 and kt == 0 and more:
                        statistics(n)
                    pairs = mx_pairs(s, tau, kt)
                    if pairs:
                        maximum(s, *pairs[0])
                    if later and kt == 0:
                        context(*before)
                    if later and kt == 2:
                        context_meanvar(*before)
                    if tau == 0 and kt == 0 and more:
                        normalise(n)
                    if pairs:
                        maximum(s, *pairs[1])
                    if later and kt == 0:
                        denominators(*before)
                    if kt == 0 and pairs:
                        minus_maximum(s, tau + 1)
                    if later and kt == 1:
                        context_stats(*before)
                    if later and kt == 2:
                        context_vareps(*before)
                    if "V" in slot(s, tau, kt):
                        transpose_values(s, n)
                    if more and tau == 2:
                        (largest, choose, chosen_weights, weights)[kt](n)

            passes(dve, period(step))
            last = Stage(PASSES - 1, 1)
            for work in (context, denominators, context_stats, context_meanvar, context_vareps):
                work(last, TILES - 1)



UPC = (1, 4)
NQ = (UNITS + 1, UNITS)
SHARED = D // 2
RING = (6, 8)
LAG = 4
CHUNK = 8
JOBS = 2 * UNITS // CHUNK
YS = WS * WS

USES = (["prodT", "xnT", "logits", "f", "i", "z", "o", "rank", "cT", "cwT", "nT"], ["prodT"])
DVE_USES = ["prodT", "rank", "cT"]
ACT_USES = [u for u in USES[0] if u not in DVE_USES]
NBANKS = 3
PE_AT = {"prodT": 6, "xnT": 13, "logits": 14, "f": 15, "i": 16, "z": 17, "o": 18, "cT": 23, "rank": 24,
         "nT": 30, "cwT": 31}
ACT_AT = {"g": 3, "xnT": 13, "logits": 14, "f": 15, "i": 16, "z": 17, "o": 18, "share": 19, "nT": 30,
          "cwT": 31}
DVE_AT = {"prod": 4, "xadd": 6, "stats": 7, "norm": 10, "top0": 15, "lin_f": 16, "lin_i": 17, "top1": 18,
          "lin_o": 19, "scan": 20, "share": 21, "count": 22, "cstats": 24, "caggr": 25, "cnorm": 27, "cut": 28}
USES = (sorted(USES[0], key=lambda u: (PE_AT[u], USES[0].index(u))), USES[1])
DVE_USES = [u for u in USES[0] if u in DVE_USES]
ACT_USES = [u for u in USES[0] if u in ACT_USES]
POOL_AT = {"rstd": 8, "split": 14, "iz": 18, "crstd": 25, "s1": 31}
PER = {"unit": NQ, "c": (UNITS // UPC[0], UNITS // UPC[1]), "once": (1, 1), "prep": (1, 0),
       "st_in": (48, 48), "ep_in": (32, 32), "m_full": (len(USES[0]), 1), "x_out": (16, 16),
       "act_rel": (len(ACT_USES), 0), "dve_rel": (len(DVE_USES), 1), "dma": (16, 0), "parts": (32, 0),
       "tiles": (TILES, 0), "two": (2, 0), "three": (3, 0)}


class Turn(Stage):

    def __init__(self, layer, i, p):
        Stage.__init__(self, i, p)
        self.layer = layer

    def n(self, counter, k):
        return self.layer * BATCH * PER[counter][0] + self.at(PER[counter][self.layer], k)

    def half(self, counter, k):
        return self.layer * PASSES * PER[counter][0] + self.own(PER[counter][self.layer], k)

    def first(self):
        return self.layer == 0 and Stage.first(self)

    def back(self):
        if self.p:
            return Turn(self.layer, self.i, 0)
        if self.layer and isinstance(self.i, int) and self.i == 0:
            return Turn(0, PASSES - 1, 1)
        return Turn(self.layer, self.i - 1, 1)

    def after_next(self):
        if isinstance(self.i, int) and self.i == PASSES - 1:
            return Turn(1, 0, self.p) if self.layer == 0 else None
        return Turn(self.layer, self.i + 1, self.p)

    def place(self, q):
        return self.p * NQ[self.layer] + q

    def tiles(self):
        return bass.ds(self.i * (2 * TILES) + self.p * TILES, TILES)


def rows(q):
    return P if q < UNITS else SHARED


def steps_at(table, q):
    return [k for k, v in table.items() if v == q]


def run_stages(eng, unit, follow):
    for layer in range(2):
        def body(i):
            for p in range(2):
                s = Turn(layer, i, p)
                for q in range(NQ[layer]):
                    if unit:
                        unit(s, q)
                    if not s.first() and follow:
                        follow(s.back(), q)
        passes(eng, body)


def build_selectors(pool, sel, built, step):
    layer, k = divmod(step, 3)
    if k == 0:
        pool.memset(sel[layer][:], 0.0).then_inc(built, 1)
        return
    pool.wait_ge(built, step)
    pattern = [[-1, UNITS // UPC[1]], [0, P]] if layer else [[-2, UNITS], [-1, 2], [0, P // 2]]
    v = sel[layer][:] if layer else sel[layer][:].rearrange("r n (a m) -> r n a m", a=2)
    pool.affine_select(out=v, in_=v, compare_op=ALU.not_equal, fill=WS, base=(k - 1) * -(E0, E1)[layer],
                       pattern=pattern, channel_multiplier=1).then_inc(built, 1)


def mixture_phase(nc, io, scratch, ident, identh, sel):
    with ExitStack() as ctx:
        def sb(name, shape, dt=F32):
            return ctx.enter_context(nc.sbuf_tensor("m_" + name, shape, dt))

        def sem(name):
            return ctx.enter_context(nc.semaphore("m_" + name))

        wuh, wul, wdh, wdl = ([sb(f"{n}{k}", [P, NQ[k], P], F16) for k in range(2)]
                              for n in ("wuh", "wul", "wdh", "wdl"))
        raw = [sb(f"raw{k}", [P, CHUNK, P]) for k in range(2)]
        raw_up, raw_down = sb("raw_up", [P, SHARED]), sb("raw_down", [SHARED, P])
        liftid = sb("liftid", [P, P], F16)
        xh = [sb(f"xh{p}", [P, TOK], F16) for p in range(2)]
        xl = [sb(f"xl{p}", [P, TOK], F16) for p in range(2)]
        cw = [sb(f"cw{p}", [P, TOK], F16) for p in range(2)]
        sT = [sb(f"sT{p}", [P, TOK]) for p in range(2)]
        xres = [sb(f"xres{p}", [P, TILES, D]) for p in range(2)]
        silu = sb("silu", [P, max(RING), TOK])
        hid = sb("hid", [P, max(RING), TOK])
        hidh, hidl = sb("hidh", [P, max(RING), TOK], F16), sb("hidl", [P, max(RING), TOK], F16)
        gT, prod = sb("gT", [P, TOK]), sb("prod", [P, TOK])
        xnew = sb("xnew", [P, TILES, D])
        wg, bg, bgh = sb("wg", [P, 4, D]), sb("bg", [P, 4]), sb("bgh", [P, 4])
        lnw, lnb, rw = sb("lnw", [P, 1]), sb("lnb", [P, 1]), sb("rw", [P, E1])
        zeros, neghalf = sb("zeros", [P, TOK]), sb("neghalf", [P, TILES, 1])
        stats, mv = sb("stats", [P, TILES, 6]), sb("mv", [P, TILES, 2])
        cstats, cmv = sb("cstats", [P, TILES, 6]), sb("cmv", [P, TILES, 2])
        vareps, rstd, cvareps, crstd = (sb(n, [P, TILES, 1]) for n in ("vareps", "rstd", "cvareps", "crstd"))
        xn, xnT = sb("xn", [P, TILES, D]), sb("xnT", [P, TOK])
        oh, ol = sb("oh", [P, TOK], F16), sb("ol", [P, TOK], F16)
        tg = {g: sb("tanh_" + g, [P, TOK]) for g in "fizo"}
        gl = {g: sb("gate_" + g, [P, TOK]) for g in "fio"}
        iz, cell, hT, s1 = (sb(n, [P, TOK]) for n in ("iz", "cell", "hT", "s1"))
        cn = sb("cn", [P, TILES, D])
        grid = [P, TILES, E1]
        lg, others = sb("lg", grid), sb("others", grid)
        priority = sb("priority", [P, 1, E1])
        best, prior = ([sb(f"{n}{k}", [P, TILES, 1]) for k in range(K1)] for n in ("best", "prior"))
        equal, rated, chosen, weighed = ([sb(f"{n}{k}", grid) for k in range(K1)]
                                         for n in ("equal", "rated", "chosen", "weighed"))
        share = [sb(f"share{k}", [P, TILES, 1]) for k in range(K1)]
        gap, tgap = sb("gap", [P, TILES, 1]), sb("tgap", [P, TILES, 1])
        cwall, cwcut = sb("cwall", grid), sb("cwcut", grid)
        selh = sb("selh", grid, BF16)
        taken = sb("taken", [P, TILES + 1, E1], BF16)
        ones, earlier = sb("ones", [P, P], BF16), sb("earlier", [P, P], BF16)
        cwhl = sb("cwhl", [P, TILES, 2, E1], F16)
        cwT = sb("cwT", [2 * E1, TOK], F16)

        hps = ctx.enter_context(nc.psum_tensor("m_h", [P, 2, 512], F32))
        cps = ctx.enter_context(nc.psum_tensor("m_c", [P, 2, 512], F32))
        yps = ctx.enter_context(nc.psum_tensor("m_y", [P, 512], F32))
        mps = ctx.enter_context(nc.psum_tensor("m_m", [P, NBANKS, 512], F32))

        w_in, raw_in, shared_in = sem("w_in"), [sem(f"raw_in{k}") for k in range(2)], sem("shared_in")
        cst, dcst = sem("cst"), sem("dcst")
        wsplit = sem("wsplit")
        st_in = [sem(f"st_in{p}") for p in range(2)]
        ep_in = [sem(f"ep_in{p}") for p in range(2)]
        up_done, c_done, dn_done = sem("up_done"), sem("c_done"), sem("dn_done")
        silu_done, mul_done, hi_done, lo_done = (sem(n + "_done") for n in ("silu", "mul", "hi", "lo"))
        g_done, prod_done, x_out = sem("g_done"), sem("prod_done"), sem("x_out")
        m_full = sem("m_full")
        act_rel, dve_rel = sem("act_rel"), sem("dve_rel")
        ln_stats, ln_aggr, ln_eps, ln_rstd = (sem("ln_" + n) for n in ("stats", "aggr", "eps", "rstd"))
        xn_ready, split, parts_out = sem("xn_ready"), sem("split"), sem("parts_out")
        gate_lin, iz_done, scan_done = sem("gate_lin"), sem("iz_done"), sem("scan_done")
        c_stats, c_aggr, c_eps, c_rstd = (sem("c_" + n) for n in ("stats", "aggr", "eps", "rstd"))
        bias_done, s_done, s_out = sem("bias_done"), sem("s_done"), sem("s_out")
        top, tgap_done, shared_out, counting, cut = (sem(n) for n in ("top", "tgap", "shares", "counting", "cut"))
        cw_out = sem("cw_out")

        W_LOADS = 5
        TOPS = 6 + 5 + 1
        SHARES = 2 + 2 + 2
        COUNTS = 1 + TILES
        PER.update(top=(TOPS, 0), shares=(SHARES, 0), counting=(COUNTS, 0))

        def bank(b, name):
            return mps[:, USES[b.layer].index(name) % NBANKS, :]

        JOB_AT = {(0, 0, 0, 2): 2, (0, 0, 0, 5): 3, (0, 0, 0, 9): 4, (0, 0, 0, 13): 5, (0, 0, 0, 17): 6,
                  (0, 0, 0, 21): 7, (0, 0, 0, 26): 8}
        for j in range(JOBS):
            JOB_AT[(0, PASSES - 1, j // 4, (1, 5, 12, 24)[j % 4])] = JOBS + 1 + j

        def job_at(s, q):
            return JOB_AT.get((s.layer, s.i, s.p, q)) if isinstance(s.i, int) else None

        def chunk(j):
            layer = int(j > JOBS)
            k = j - layer * (JOBS + 1)
            return layer, k % 2, slice(k // 2 * CHUNK, k // 2 * CHUNK + CHUNK), k % 2

        block = ctx.enter_context(nc.Block())

        @block.sync
        def _(sp):
            def load(s):
                n = s.layer
                if n:
                    before = Turn(0, s.i, s.p)
                    sp.wait_ge(parts_out, before.n("parts", 32))
                    apart(sp)
                    sp.wait_ge(cw_out, before.n("dma", 16))
                    apart(sp)
                sp.dma_start(xh[s.p][:], scratch[f"xh{n}"][:, s.tokens()]).then_inc(st_in[s.p], 16)
                sp.dma_start(xl[s.p][:], scratch[f"xl{n}"][:, s.tokens()]).then_inc(st_in[s.p], 16)
                r = slice(0, 2 * (E0, E1)[n])
                sp.dma_start(cw[s.p][r], scratch[f"cw{n}"][:, s.tokens()]).then_inc(st_in[s.p], 16)

            def load_ep(s):
                n = s.layer
                if n:
                    before = Turn(0, s.i, s.p)
                    sp.wait_ge(s_out, before.n("dma", 16))
                    apart(sp)
                    sp.wait_ge(x_out, before.n("x_out", 16))
                    apart(sp)
                sp.dma_start(sT[s.p][:], scratch[f"s{n}"][:, s.tokens()]).then_inc(ep_in[s.p], 16)
                x_t = (scratch["x1"] if n else io["x"]).rearrange("(n p) d -> p n d", p=P)
                sp.dma_start(xres[s.p][:], x_t[:, s.tiles(), :]).then_inc(ep_in[s.p], 16)

            def load_chunk(j):
                layer, side, units, k = chunk(j)
                src = io[("up", "down")[side] + str(layer)]
                sp.dma_start(raw[k][:], src[:, units, :]).then_inc(raw_in[k], 16)

            load_chunk(0)
            load(Turn(0, 0, 0))
            load_chunk(1)
            for dst, src in ((wg, "wg"), (bg, "bg"), (lnw, "lnw"), (lnb, "lnb"), (rw, "rw")):
                sp.dma_start(dst[:], io[src]).then_inc(w_in, 16)
            sp.dma_start(raw_up[:], io["ups"]).then_inc(shared_in, 16)
            sp.dma_start(raw_down[:], io["downs"]).then_inc(shared_in, 16)
            for j in range(2, JOBS):
                sp.wait_ge(wsplit, 2 * (j - 1))
                load_chunk(j)
                if j == 3:
                    load(Turn(0, 0, 1))
            load_ep(Turn(0, 0, 0))
            load_ep(Turn(0, 0, 1))
            for k in range(2):
                sp.wait_ge(wsplit, 2 * (JOBS - 1 + k))
                load_chunk(JOBS + 1 + k)

            def unit(s, q):
                j = job_at(s, q)
                if j is not None and JOBS < j <= 2 * JOBS - 2:
                    sp.wait_ge(wsplit, 2 * j + 4)
                    load_chunk(j + 2)

            def follow(b, q):
                nxt = b.after_next()
                if q == 0 and nxt:
                    sp.wait_ge(up_done, b.n("unit", NQ[b.layer]))
                    apart(sp)
                    sp.wait_ge(c_done, b.n("c", PER["c"][b.layer]))
                    apart(sp)
                    load(nxt)
                if q == 7:
                    sp.wait_ge(dve_rel, b.n("dve_rel", 1))
                    apart(sp)
                    out_t = (io["out"] if b.layer else scratch["x1"]).rearrange("(n p) d -> p n d", p=P)
                    sp.dma_start(out_t[:, b.tiles(), :], xnew[:]).then_inc(x_out, 16)
                    if nxt:
                        load_ep(nxt)
                if b.layer:
                    return
                if q == 16:
                    sp.wait_ge(split, b.n("two", 2))
                    apart(sp)
                    sp.dma_start(scratch["xh1"][:, b.tokens()], oh[:]).then_inc(parts_out, 16)
                    sp.dma_start(scratch["xl1"][:, b.tokens()], ol[:]).then_inc(parts_out, 16)
                if q == 31:
                    sp.wait_ge(act_rel, b.n("act_rel", ACT_USES.index("cwT") + 1))
                    apart(sp)
                    sp.dma_start(scratch["cw1"][:, b.tokens()], cwT[:]).then_inc(cw_out, 16)
                if q == 31:
                    sp.wait_ge(s_done, b.n("prep", 1))
                    apart(sp)
                    sp.dma_start(scratch["s1"][:, b.tokens()], s1[:]).then_inc(s_out, 16)

            run_stages(sp, unit, follow)
            for q in range(UNITS):
                follow(Turn(1, PASSES - 1, 1), q)
            sp.wait_ge(x_out, 2 * 16 * BATCH)
            sp.wait_ge(parts_out, 32 * BATCH)
            sp.wait_ge(cw_out, 16 * BATCH)
            sp.wait_ge(s_out, 16 * BATCH)

        @block.gpsimd
        def _(pool):
            pool.memset(ones[:], 1.0).then_inc(cst, 1)
            pool.memset(earlier[:], 1.0).then_inc(cst, 1)
            pool.memset(liftid[:], 0.0).then_inc(cst, 1)
            pool.wait_ge(cst, 3)
            pool.affine_select(out=earlier[:], in_=earlier[:], compare_op=ALU.is_ge, fill=0.0, base=-1,
                               pattern=[[1, P]], channel_multiplier=-1).then_inc(cst, 1)
            pool.affine_select(out=liftid[:], in_=liftid[:], compare_op=ALU.not_equal, fill=YS, base=0,
                               pattern=[[-1, P]], channel_multiplier=1).then_inc(cst, 1)

            def unit(s, q):
                k, r, r0 = s.place(q), RING[s.layer], rows(q)
                pool.wait_ge(hi_done, s.n("unit", q + 1))
                if not (s.first() and q < min(RING)):
                    pool.wait_ge(dn_done, s.n("unit", q - min(RING) + 1))
                pool.tensor_tensor(hidl[0:r0, k % r, :], hid[0:r0, k % r, :], hidh[0:r0, k % r, :],
                                   ALU.subtract).then_inc(lo_done, 1)

            def follow(b, q):
                if b.layer:
                    return
                for name in steps_at(POOL_AT, q):
                    if name == "rstd":
                        pool.wait_ge(ln_eps, b.n("prep", 1))
                        pool.tensor_tensor(rstd[:], vareps[:], neghalf[:], ALU.pow).then_inc(ln_rstd, 1)
                    elif name == "split":
                        pool.wait_ge(act_rel, b.n("act_rel", ACT_USES.index("xnT") + 1))
                        if not b.first():
                            pool.wait_ge(parts_out, b.n("parts", 0))
                        pool.tensor_tensor(oh[:], xnT[:], zeros[:], ALU.add).then_inc(split, 1)
                        pool.wait_ge(split, b.n("two", 1))
                        pool.tensor_tensor(ol[:], xnT[:], oh[:], ALU.subtract).then_inc(split, 1)
                    elif name == "iz":
                        pool.wait_ge(gate_lin, b.n("three", 2))
                        pool.wait_ge(act_rel, b.n("act_rel", ACT_USES.index("z") + 1))
                        if not b.first():
                            pool.wait_ge(scan_done, b.n("prep", 0))
                        pool.tensor_tensor(iz[:], gl["i"][:], tg["z"][:], ALU.mult).then_inc(iz_done, 1)
                    elif name == "crstd":
                        pool.wait_ge(c_eps, b.n("prep", 1))
                        pool.tensor_tensor(crstd[:], cvareps[:], neghalf[:], ALU.pow).then_inc(c_rstd, 1)
                    elif name == "s1":
                        pool.wait_ge(act_rel, b.n("act_rel", ACT_USES.index("nT") + 1))
                        pool.wait_ge(gate_lin, b.n("three", 3))
                        if not b.first():
                            pool.wait_ge(s_out, b.n("dma", 0))
                        pool.tensor_tensor(s1[:], gl["o"][:], hT[:], ALU.mult).then_inc(s_done, 1)

            pool.wait_ge(dcst, 3 + E1)
            run_stages(pool, unit, follow)

        @block.scalar
        def _(act):
            def unit(s, q):
                k = s.place(q)
                act.wait_ge(up_done, s.n("unit", q + 1))
                if not (s.first() and q < min(RING)):
                    act.wait_ge(mul_done, s.n("unit", q - min(RING) + 1))
                act.activation(silu[0:rows(q), k % RING[s.layer], :], hps[0:rows(q), k % 2, :], ACT.Silu,
                               scale=1.0 / WS).then_inc(silu_done, 1)

            def follow(b, q):
                for name in steps_at(ACT_AT, q):
                    if name == "g":
                        act.wait_ge(dn_done, b.n("unit", NQ[b.layer]))
                        if not b.first():
                            act.wait_ge(prod_done, b.n("once", 0))
                        act.activation(gT[:], yps[:], ACT.Silu, scale=1.0 / YS).then_inc(g_done, 1)
                        continue
                    if b.layer:
                        continue
                    if name == "share":
                        act.wait_ge(top, b.n("top", TOPS))
                        if not b.first():
                            act.wait_ge(shared_out, b.n("shares", 0))
                        act.activation(tgap[:], gap[:], ACT.Tanh, scale=0.5).then_inc(tgap_done, 1)
                        continue
                    act.wait_ge(m_full, b.n("m_full", USES[0].index(name) + 1))
                    src = bank(b, name)
                    if name == "xnT":
                        if not b.first():
                            act.wait_ge(split, b.n("two", 0))
                        act.activation(xnT[:], src, ACT.Copy).then_inc(act_rel, 1)
                    elif name == "logits":
                        if not b.first():
                            act.wait_ge(top, b.n("top", 0))
                        act.activation(lg[:].rearrange("p t e -> p (t e)"), src[:, 0:TILES * E1], ACT.Copy
                                       ).then_inc(act_rel, 1)
                    elif name in "fizo":
                        w = "fioz".index(name)
                        if not b.first():
                            if name == "z":
                                act.wait_ge(iz_done, b.n("prep", 0))
                            else:
                                act.wait_ge(gate_lin, b.n("three", 0))
                        act.activation(tg[name][:], src, ACT.Tanh, scale=1.0 if name == "z" else 0.5,
                                       bias=bgh[:, w:w + 1]).then_inc(act_rel, 1)
                    elif name == "cwT":
                        if not b.first():
                            act.wait_ge(cw_out, b.n("dma", 0))
                        act.activation(cwT[:], src.bitcast(F16)[0:2 * E1, 0:TOK], ACT.Copy).then_inc(act_rel, 1)
                    elif name == "nT":
                        if not b.first():
                            act.wait_ge(s_done, b.n("prep", 0))
                        act.activation(hT[:], src, ACT.Tanh, scale=lnw[:], bias=lnb[:]).then_inc(act_rel, 1)

            act.wait_ge(w_in, 16 * W_LOADS)
            act.activation(bgh[:, 0:3], bg[:, 0:3], ACT.Copy, scale=0.5).then_inc(bias_done, 1)
            act.activation(bgh[:, 3:4], bg[:, 3:4], ACT.Copy).then_inc(bias_done, 1)
            act.wait_ge(bias_done, 2)
            run_stages(act, unit, follow)
            follow(Turn(1, PASSES - 1, 1), ACT_AT["g"])

        @block.tensor
        def _(pe):
            def down(s, q):
                n, r, r0 = s.layer, s.place(q) % RING[s.layer], rows(q)
                pe.wait_ge(lo_done, s.n("unit", q + 1))
                if s.first() and q < UNITS and q % CHUNK == 0:
                    pe.wait_ge(wsplit, 4 * (q // CHUNK) + 4)
                if s.first() and q == UNITS:
                    pe.wait_ge(wsplit, 2 * JOBS + 4)
                if q == 0 and not s.first():
                    pe.wait_ge(g_done, s.n("once", 0))
                if q == 0 and n:
                    pe.matmul(yps[:], liftid[:], xh[s.p][:], start=True, stop=False)
                    pe.matmul(yps[:], liftid[:], xl[s.p][:], start=False, stop=False)
                pe.matmul(yps[:], wdh[n][0:r0, q, :], hidh[0:r0, r, :], start=(q == 0 and not n), stop=False)
                pe.matmul(yps[:], wdl[n][0:r0, q, :], hidh[0:r0, r, :], start=False, stop=False)
                pe.matmul(yps[:], wdh[n][0:r0, q, :], hidl[0:r0, r, :], start=False, stop=(q == NQ[n] - 1)
                          ).then_inc(dn_done, 1)

            def unit(s, q):
                n, k = s.layer, s.place(q) % 2
                if q == 0:
                    pe.wait_ge(st_in[s.p], s.half("st_in", 48))
                    if n and isinstance(s.i, int) and s.i == 0 and s.p == 0:
                        pe.wait_ge(wsplit, 2 * (2 * JOBS + 1) + 2)
                if s.first() and q < UNITS and q % CHUNK == 0:
                    pe.wait_ge(wsplit, 4 * (q // CHUNK) + 2)
                if s.first() and q == UNITS:
                    pe.wait_ge(wsplit, 2 * JOBS + 4)
                if not (s.first() and q < 2):
                    pe.wait_ge(silu_done, s.n("unit", q - 1))
                dst, high, low = hps[0:rows(q), k, :], wuh[n][:, q, 0:rows(q)], wul[n][:, q, 0:rows(q)]
                pe.matmul(dst, high, xh[s.p][:], start=True, stop=False)
                pe.matmul(dst, high, xl[s.p][:], start=False, stop=False)
                pe.matmul(dst, low, xh[s.p][:], start=False, stop=True).then_inc(up_done, 1)
                if q < UNITS and q % UPC[n] == 0:
                    c = q // UPC[n]
                    if not (s.first() and c < 2):
                        ago = (c - 1) * UPC[n] - (NQ[n] - UNITS if c < 2 else 0)
                        if n and c < 2 and isinstance(s.i, int) and s.i == 0 and s.p == 0:
                            ago = -1
                        pe.wait_ge(mul_done, s.n("unit", ago))
                    r = slice(0, 2 * (E0, E1)[n])
                    pe.matmul(cps[:, c % 2, :], sel[n][:, c, :], cw[s.p][r], start=True, stop=True
                              ).then_inc(c_done, 1)
                if q >= LAG:
                    down(s, q - LAG)
                elif not s.first():
                    b = s.back()
                    down(b, NQ[b.layer] - LAG + q)

            def bank_free(b, name):
                if b.layer:
                    if isinstance(b.i, int) and b.i == 0 and b.p == 0:
                        pe.wait_ge(act_rel, BATCH * len(ACT_USES))
                    pe.wait_ge(dve_rel, b.n("dve_rel", 0))
                    return
                order = USES[0]
                k = order.index(name)
                same = [j for j in range(len(order)) if j % NBANKS == k % NBANKS]
                prev = k < NBANKS
                old = order[same[-1] if prev else k - NBANKS]
                if prev and b.first():
                    return
                if old in ACT_USES:
                    pe.wait_ge(act_rel, b.n("act_rel", ACT_USES.index(old) + 1 - prev * len(ACT_USES)))
                else:
                    pe.wait_ge(dve_rel, b.n("dve_rel", DVE_USES.index(old) + 1 - prev * len(DVE_USES)))

            def follow(b, q):
                for name in [u for u in USES[b.layer] if PE_AT[u] == q]:
                    dst = bank(b, name)
                    bank_free(b, name)
                    if name == "prodT":
                        pe.wait_ge(prod_done, b.n("once", 1))
                        for t in range(TILES):
                            op = pe.transpose(dst[:, t * P:t * P + P], prod[:, t * P:t * P + P], ident[:])
                    elif name == "xnT":
                        pe.wait_ge(xn_ready, b.n("tiles", TILES))
                        for t in range(TILES):
                            op = pe.transpose(dst[:, t * P:t * P + P], xn[:, t, :], ident[:])
                    elif name == "logits":
                        pe.wait_ge(act_rel, b.n("act_rel", ACT_USES.index("xnT") + 1))
                        for t in range(TILES):
                            op = pe.matmul(dst[:, t * E1:t * E1 + E1], xnT[:, t * P:t * P + P], rw[:],
                                           start=True, stop=True)
                    elif name in "fizo":
                        op = pe.matmul(dst, wg[:, "fioz".index(name), :], xnT[:], start=True, stop=True)
                    elif name == "rank":
                        pe.wait_ge(counting, b.n("counting", COUNTS))
                        pe.matmul(dst[:, 0:TILES * E1], earlier[:], selh[:].rearrange("p t e -> p (t e)"),
                                  start=True, stop=False)
                        op = pe.matmul(dst[:, 0:TILES * E1], ones[:],
                                       taken[:, 0:TILES, :].rearrange("p t e -> p (t e)"), start=False, stop=True)
                    elif name == "cT":
                        pe.wait_ge(scan_done, b.n("prep", 1))
                        for t in range(TILES):
                            op = pe.transpose(dst[:, t * P:t * P + P], cell[:, t * P:t * P + P], ident[:])
                    elif name == "cwT":
                        pe.wait_ge(cut, b.n("two", 2))
                        half = dst.bitcast(F16)[0:2 * E1]
                        for t in range(TILES):
                            op = pe.transpose(half[:, t * P:t * P + P],
                                              cwhl[:, t].rearrange("p a e -> p (a e)"), identh[:])
                    elif name == "nT":
                        pe.wait_ge(dve_rel, b.n("dve_rel", DVE_USES.index("cT") + 1))
                        for t in range(TILES):
                            op = pe.transpose(dst[:, t * P:t * P + P], cn[:, t, :], ident[:])
                    op.then_inc(m_full, 1)

            pe.wait_ge(cst, 5)
            pe.wait_ge(w_in, 16 * W_LOADS)
            run_stages(pe, unit, follow)
            last = Turn(1, PASSES - 1, 1)
            for k in range(LAG):
                down(last, NQ[1] - LAG + k)
            follow(last, PE_AT["prodT"])

        @block.vector
        def _(dve):
            def lift(j, side, layer, src, part):
                high, low = ((wuh, wul), (wdh, wdl))[side]
                dve.tensor_scalar(high[layer][part], src[:], WS, None, ALU.mult).then_inc(wsplit, 1)
                dve.wait_ge(wsplit, 2 * j + 1)
                dve.scalar_tensor_tensor(low[layer][part], src[:], WS, high[layer][part], ALU.mult, ALU.subtract
                                         ).then_inc(wsplit, 1)

            def do_job(j):
                if j == JOBS:
                    dve.wait_ge(shared_in, 32)
                    lift(j, 0, 0, raw_up, (slice(None), UNITS, slice(0, SHARED)))
                    lift(j + 1, 1, 0, raw_down, (slice(0, SHARED), UNITS, slice(None)))
                    return
                layer, side, units, k = chunk(j)
                order = (j - layer) // 2 + 1
                dve.wait_ge(raw_in[k], 16 * order)
                lift(j + layer, side, layer, raw[k], (slice(None), units, slice(None)))

            def unit(s, q):
                k, r, r0 = s.place(q), RING[s.layer], rows(q)
                dve.wait_ge(silu_done, s.n("unit", q + 1))
                if q < UNITS and q % UPC[s.layer] == 0:
                    dve.wait_ge(c_done, s.n("c", q // UPC[s.layer] + 1))
                if not (s.first() and q < min(RING)):
                    dve.wait_ge(lo_done, s.n("unit", q - min(RING) + 1))
                if q < UNITS:
                    dve.tensor_tensor(hid[:, k % r, :], silu[:, k % r, :], cps[:, (q // UPC[s.layer]) % 2, :],
                                      ALU.mult).then_inc(mul_done, 1)
                else:
                    dve.tensor_scalar(hid[0:r0, k % r, :], silu[0:r0, k % r, :], WS, None, ALU.mult
                                      ).then_inc(mul_done, 1)
                dve.wait_ge(mul_done, s.n("unit", q + 1))
                if not (s.first() and q < min(RING)):
                    dve.wait_ge(dn_done, s.n("unit", q - min(RING) + 1))
                dve.tensor_scalar(hidh[0:r0, k % r, :], hid[0:r0, k % r, :], 1.0, None, ALU.mult
                                  ).then_inc(hi_done, 1)
                j = job_at(s, q)
                if j is not None:
                    do_job(j)

            def wide(t):
                return t[:].broadcast_to(grid)

            def follow(b, q):
                for name in steps_at(DVE_AT, q):
                    if name == "prod":
                        dve.wait_ge(g_done, b.n("once", 1))
                        dve.wait_ge(ep_in[b.p], b.half("ep_in", 32))
                        if not b.first():
                            dve.wait_ge(m_full, b.n("m_full", 1 - PER["m_full"][b.layer]))
                        dve.tensor_tensor(prod[:], gT[:], sT[b.p][:], ALU.mult).then_inc(prod_done, 1)
                    elif name == "xadd":
                        dve.wait_ge(m_full, b.n("m_full", 1))
                        if not b.first():
                            dve.wait_ge(x_out, b.n("x_out", 0))
                        dve.tensor_tensor(xnew[:].rearrange("p t d -> p (t d)"),
                                          xres[b.p][:].rearrange("p t d -> p (t d)"), bank(b, "prodT"), ALU.add
                                          ).then_inc(dve_rel, 1)
                    elif b.layer:
                        continue
                    elif name == "stats":
                        dve.wait_ge(dve_rel, b.n("dve_rel", 1))
                        if not b.first():
                            dve.wait_ge(ln_rstd, b.n("prep", 0))
                        apart(dve)
                        for t in range(TILES):
                            dve.bn_stats(stats[:, t, :], xnew[:, t, :]).then_inc(ln_stats, 1)
                        dve.wait_ge(ln_stats, b.n("tiles", TILES))
                        apart(dve)
                        for t in range(TILES):
                            dve.bn_aggr(mv[:, t, :], stats[:, t, :]).then_inc(ln_aggr, 1)
                        dve.wait_ge(ln_aggr, b.n("tiles", TILES))
                        dve.tensor_scalar(vareps[:], mv[:, :, 1:2], LN_EPS, None, ALU.add).then_inc(ln_eps, 1)
                    elif name == "norm":
                        dve.wait_ge(ln_rstd, b.n("prep", 1))
                        if not b.first():
                            dve.wait_ge(m_full, b.n("m_full", 2 - len(USES[0])))
                        for t in range(TILES):
                            dve.tensor_scalar(xn[:, t, :], xnew[:, t, :], mv[:, t, 0:1], rstd[:, t, :],
                                              ALU.subtract, ALU.mult).then_inc(xn_ready, 1)
                    elif name in ("lin_f", "lin_i", "lin_o"):
                        g = name[-1]
                        dve.wait_ge(act_rel, b.n("act_rel", ACT_USES.index(g) + 1))
                        if g == "o" and not b.first():
                            dve.wait_ge(s_done, b.n("prep", 0))
                        if g == "i" and not b.first():
                            dve.wait_ge(iz_done, b.n("prep", 0))
                        dve.tensor_scalar(gl[g][:], tg[g][:], 0.5, 0.5, ALU.mult, ALU.add).then_inc(gate_lin, 1)
                    elif name == "scan":
                        dve.wait_ge(iz_done, b.n("prep", 1))
                        if not b.first():
                            dve.wait_ge(m_full, b.n("m_full", USES[0].index("cT") + 1 - len(USES[0])))
                        dve.tensor_tensor_scan(cell[:], gl["f"][:], iz[:], 0.0, ALU.mult, ALU.add
                                               ).then_inc(scan_done, 1)
                    elif name == "cstats":
                        dve.wait_ge(m_full, b.n("m_full", USES[0].index("cT") + 1))
                        if not b.first():
                            dve.wait_ge(c_rstd, b.n("prep", 0))
                        apart(dve)
                        for t in range(TILES):
                            dve.bn_stats(cstats[:, t, :], bank(b, "cT")[:, t * P:t * P + P]).then_inc(c_stats, 1)
                    elif name == "caggr":
                        dve.wait_ge(c_stats, b.n("tiles", TILES))
                        apart(dve)
                        for t in range(TILES):
                            dve.bn_aggr(cmv[:, t, :], cstats[:, t, :]).then_inc(c_aggr, 1)
                        dve.wait_ge(c_aggr, b.n("tiles", TILES))
                        dve.tensor_scalar(cvareps[:], cmv[:, :, 1:2], LN_EPS, None, ALU.add).then_inc(c_eps, 1)
                    elif name == "cnorm":
                        dve.wait_ge(c_rstd, b.n("prep", 1))
                        if not b.first():
                            dve.wait_ge(m_full, b.n("m_full", 0))
                        for t in range(TILES):
                            op = dve.tensor_scalar(cn[:, t, :], bank(b, "cT")[:, t * P:t * P + P], cmv[:, t, 0:1],
                                                   crstd[:, t, :], ALU.subtract, ALU.mult)
                        op.then_inc(dve_rel, 1)
                    elif name in ("top0", "top1"):
                        k = int(name[-1])
                        n = 6 * k
                        src = others if k else lg
                        if k:
                            dve.wait_ge(top, b.n("top", 6))
                        else:
                            dve.wait_ge(act_rel, b.n("act_rel", ACT_USES.index("logits") + 1))
                        dve.tensor_reduce(best[k][:], src[:], AX.X, ALU.max).then_inc(top, 1)
                        dve.wait_ge(top, b.n("top", n + 1))
                        dve.tensor_tensor(equal[k][:], src[:], wide(best[k]), ALU.is_equal).then_inc(top, 1)
                        dve.wait_ge(top, b.n("top", n + 2))
                        dve.tensor_tensor(rated[k][:], equal[k][:], priority[:].broadcast_to(grid), ALU.mult
                                          ).then_inc(top, 1)
                        dve.wait_ge(top, b.n("top", n + 3))
                        dve.tensor_reduce(prior[k][:], rated[k][:], AX.X, ALU.max).then_inc(top, 1)
                        dve.wait_ge(top, b.n("top", n + 4))
                        dve.tensor_tensor(chosen[k][:], rated[k][:], wide(prior[k]), ALU.is_equal
                                          ).then_inc(top, 1)
                        if k:
                            if not b.first():
                                dve.wait_ge(tgap_done, b.n("prep", 0))
                            dve.tensor_tensor(gap[:], best[0][:], best[1][:], ALU.subtract).then_inc(top, 1)
                        else:
                            dve.wait_ge(top, b.n("top", 5))
                            dve.scalar_tensor_tensor(others[:], chosen[0][:], -3.0e38, lg[:], ALU.mult, ALU.add
                                                     ).then_inc(top, 1)
                    elif name == "share":
                        dve.wait_ge(tgap_done, b.n("prep", 1))
                        for k, sign in enumerate((0.5, -0.5)):
                            dve.tensor_scalar(share[k][:], tgap[:], sign, 0.5, ALU.mult, ALU.add
                                              ).then_inc(shared_out, 1)
                        for k in range(K1):
                            dve.wait_ge(shared_out, b.n("shares", 1 + 2 * k))
                            dve.tensor_tensor(weighed[k][:], chosen[k][:], wide(share[k]), ALU.mult
                                              ).then_inc(shared_out, 1)
                        dve.wait_ge(shared_out, b.n("shares", 4))
                        dve.tensor_tensor(cwall[:], weighed[0][:], weighed[1][:], ALU.add).then_inc(shared_out, 1)
                        if not b.first():
                            dve.wait_ge(m_full, b.n("m_full", USES[0].index("rank") + 1 - len(USES[0])))
                        dve.tensor_tensor(selh[:], chosen[0][:], chosen[1][:], ALU.add).then_inc(shared_out, 1)
                    elif name == "count":
                        dve.wait_ge(shared_out, b.n("shares", 6))
                        dve.tensor_scalar(taken[:, 0, :], taken[:, TILES, :], 1.0, None, ALU.mult
                                          ).then_inc(counting, 1)
                        for t in range(TILES):
                            dve.wait_ge(counting, b.n("counting", t + 1))
                            dve.tensor_tensor(taken[:, t + 1, :], taken[:, t, :], selh[:, t, :], ALU.add
                                              ).then_inc(counting, 1)
                    elif name == "cut":
                        dve.wait_ge(m_full, b.n("m_full", USES[0].index("rank") + 1))
                        dve.scalar_tensor_tensor(cwcut[:], bank(b, "rank")[:, 0:TILES * E1].rearrange(
                            "p (t e) -> p t e", e=E1), float(CAPACITY), cwall[:], ALU.is_lt, ALU.mult
                            ).then_inc(dve_rel, 1)
                        dve.wait_ge(dve_rel, b.n("dve_rel", DVE_USES.index("rank") + 1))
                        if not b.first():
                            dve.wait_ge(m_full, b.n("m_full", USES[0].index("cwT") + 1 - len(USES[0])))
                        dve.tensor_scalar(cwhl[:, :, 0, :], cwcut[:], 1.0, None, ALU.mult).then_inc(cut, 1)
                        dve.wait_ge(cut, b.n("two", 1))
                        dve.tensor_tensor(cwhl[:, :, 1, :], cwcut[:], cwhl[:, :, 0, :], ALU.subtract
                                          ).then_inc(cut, 1)

            do_job(0)
            do_job(1)
            dve.memset(zeros[:], 0.0).then_inc(dcst, 1)
            dve.memset(neghalf[:], -0.5).then_inc(dcst, 1)
            dve.memset(taken[:], 0.0).then_inc(dcst, 1)
            for e in range(E1):
                dve.memset(priority[:, :, e:e + 1], float(E1 - e)).then_inc(dcst, 1)
            dve.wait_ge(dcst, 3 + E1)
            run_stages(dve, unit, follow)
            last = Turn(1, PASSES - 1, 1)
            follow(last, DVE_AT["prod"])
            follow(last, DVE_AT["xadd"])



def build_program(nc, io):
    def dram(name, shape, dt=F32):
        return nc.dram_tensor("t_" + name, shape, dt, kind="Internal").ap()

    scratch = {
        "parts": dram("parts", [2, TILES, 3, P, TOK // TILES], BF16),
        "x1": dram("x1", [NTOK, D]),
        "cw0": dram("cw0", [2 * E0, NTOK], F16), "cw1": dram("cw1", [2 * E1, NTOK], F16)}
    for layer in range(2):
        for part in ("xh", "xl"):
            scratch[f"{part}{layer}"] = dram(f"{part}{layer}", [P, NTOK], F16)
        scratch[f"s{layer}"] = dram(f"s{layer}", [P, NTOK])

    with ExitStack() as ctx:
        ident = ctx.enter_context(nc.sbuf_tensor("ident", [P, P], F32))
        identh = ctx.enter_context(nc.sbuf_tensor("identh", [P, P], F16))
        sel = [ctx.enter_context(nc.sbuf_tensor(f"sel{k}", [2 * (E0, E1)[k], UNITS // UPC[k], P], F16))
               for k in range(2)]
        sel_built = ctx.enter_context(nc.semaphore("sel_built"))
        consts_ready = ctx.enter_context(nc.semaphore("consts_ready"))

        with nc.Block() as block:
            @block.gpsimd
            def _(pool):
                pool.memset(ident[:], 0.0).then_inc(consts_ready, 1)
                pool.memset(identh[:], 0.0).then_inc(consts_ready, 1)
                pool.wait_ge(consts_ready, 2)
                for m in (ident, identh):
                    pool.affine_select(out=m[:], in_=m[:], compare_op=ALU.not_equal, fill=1.0, base=0,
                                       pattern=[[-1, P]], channel_multiplier=1).then_inc(consts_ready, 1)

        attention_phase(nc, io, scratch, ident, identh, consts_ready, sel, sel_built)
        mixture_phase(nc, io, scratch, ident, identh, sel)


def kernel(**inputs):
    import concourse.bacc as bacc
    from concourse.bass_utils import run_bass_kernel_spmd

    def permuted(w):
        return w.reshape(-1, CH, DH).transpose(0, 2, 1).reshape(-1, D)

    a = {k: np.asarray(v) for k, v in inputs.items()}
    arrays = {
        "x": a["L0_attn_x"].reshape(NTOK, D),
        "wq": permuted(a["L0_attn_Wq"]), "wk": permuted(a["L0_attn_Wk"]),
        "wv": a["L0_attn_Wv"].reshape(D, KT, CH // KT, DH).transpose(0, 2, 1, 3).reshape(D, D),
        "wf": a["L0_attn_Wf"],
        "bq": permuted(a["L0_attn_bq"]).reshape(D, 1), "bk": permuted(a["L0_attn_bk"]).reshape(D, 1),
        "bf": a["L0_attn_bf"].reshape(D, 1), "bv": a["L0_attn_bv"].reshape(1, D),
        "cent": a["L0_ffn_centroids"].T, "ebias": a["L0_ffn_expert_biases"].reshape(1, E0),
        "ups": a["L0_ffn_Ws_up"], "downs": a["L0_ffn_Ws_down"],
        "up0": a["L0_ffn_W_up"].transpose(1, 0, 2).reshape(D, UNITS, P),
        "down0": a["L0_ffn_W_down"].reshape(UNITS, P, D).transpose(1, 0, 2),
        "wg": a["L1_attn_W"].T.reshape(D, 4, D), "bg": a["L1_attn_b"].reshape(4, D).T,
        "lnw": a["L1_attn_ln_w"].reshape(D, 1), "lnb": a["L1_attn_ln_b"].reshape(D, 1),
        "rw": a["L1_ffn_router_w"].T,
        "up1": a["L1_ffn_w1"].transpose(1, 0, 2).reshape(D, UNITS, P),
        "down1": a["L1_ffn_w2"].reshape(UNITS, P, D).transpose(1, 0, 2)}
    arrays = {k: np.ascontiguousarray(v) for k, v in arrays.items()}

    nc = bacc.Bacc("TRN2", target_bir_lowering=False, num_devices=1)
    io = {k: nc.dram_tensor(k, v.shape, mybir.dt.from_np(v.dtype), kind="ExternalInput").ap()
          for k, v in arrays.items()}
    io["out"] = nc.dram_tensor("out", [NTOK, D], F32, kind="ExternalOutput").ap()
    build_program(nc, io)
    r = run_bass_kernel_spmd(nc, [arrays], core_ids=[0])
    return r.results[0]["out"].reshape(BATCH, SEQ, D)
```
